# Optimizing a Trainium2 kernel written in Bass

```python
import numpy as np
import jax
import jax.numpy as jnp

def _softmax(x, axis=-1):
    return jax.nn.softmax(x, axis=axis)

def _gelu(x):
    return jax.nn.gelu(x, approximate=True)

def _silu(x):
    return jax.nn.silu(x)

def _sigmoid(x):
    return jax.nn.sigmoid(x)

def _layernorm(x, axis=-1, eps=1e-05):
    m = jnp.mean(x, axis=axis, keepdims=True)
    v = jnp.var(x, axis=axis, keepdims=True)
    return (x - m) / jnp.sqrt(v + eps)

def _scatter_add(tgt, idx, src, axis=0):
    return tgt.at[idx].add(src)

def _segment_sum(src, seg, n):
    return jax.ops.segment_sum(src, seg, n)
kernel_name = 'mk_decoder_postln_d2_seqx_r8_919e2e'

def setup_inputs(seed: int=0):
    np.random.seed(seed)
    _w = jnp.asarray

    def _rec_inputs():
        import jax
        import jax.numpy as jnp
        _rk = jax.random.key(seed)
        x = 0.0002417 + 0.9998 * jax.random.normal(jax.random.fold_in(_rk, 1), (64, 128, 128), jnp.float32)
        _lenS = 128 - jax.random.randint(jax.random.fold_in(_rk, 7), (64,), 0, max(1, 128 // 4) + 1, jnp.int32)
        _lenS2 = 77 - jax.random.randint(jax.random.fold_in(_rk, 8), (64,), 0, max(1, 77 // 4) + 1, jnp.int32)
        _ctx_1024P = jax.random.normal(jax.random.fold_in(_rk, 11), (64, 16, 128), jnp.float32)
        _ctx_1024c = jax.random.dirichlet(jax.random.fold_in(_rk, 511), 0.3 * jnp.ones((16,), jnp.float32), (64, 77))
        _ctx_1024t = jnp.einsum('bsk,bkd->bsd', _ctx_1024c, _ctx_1024P)
        _ctx_1024t = _ctx_1024t * jax.lax.rsqrt(jnp.mean(jnp.square(_ctx_1024t)) + 1e-12) * 0.953939
        ctx_1024 = 7.22013e-05 + 1.00017 * (_ctx_1024t + 0.3 * jax.random.normal(jax.random.fold_in(_rk, 611), (64, 77, 128), jnp.float32))
        _validS = jnp.arange(128)[None, :] < _lenS[:, None]
        _validS2 = jnp.arange(77)[None, :] < _lenS2[:, None]
        _causal = jnp.tril(jnp.ones((128, 128), dtype=bool))
        mask_BxS_ff1 = jnp.where(jnp.ones((64, 128), dtype=bool), 1.0, 0.0).astype(jnp.float32)
        mask_BxS2_ik0 = jnp.where(jnp.broadcast_to(_validS2[:, :], (64, 77)), 0, 1).astype(jnp.int32)
        return (x, ctx_1024, mask_BxS_ff1, mask_BxS2_ik0)
    x, ctx_1024, mask_BxS_ff1, mask_BxS2_ik0 = _rec_inputs()

    def _L0_attn_setup():
        import jax, jax.numpy as jnp
        import numpy as np
        NUM_HEADS = 16

        def _sinusoid_rel_pos(seq_len, dim):
            pos = jnp.arange(seq_len - 1, -1, -1, dtype=jnp.float32)
            inv_freq = 1.0 / 10000.0 ** (jnp.arange(0, dim, 2, dtype=jnp.float32) / dim)
            ang = pos[:, None] * inv_freq[None, :]
            return jnp.concatenate([jnp.sin(ang), jnp.cos(ang)], axis=-1)

        def _rel_shift(x):
            B, H, S, L = x.shape
            x = jnp.pad(x, ((0, 0), (0, 0), (0, 0), (1, 0)))
            x = x.reshape(B, H, L + 1, S)
            return x[:, :, 1:S + 1, :]
        key = jax.random.key(seed)
        ks = jax.random.split(key, 8)
        B, S, C = (2, 256, 128)
        Dk, Dv, H = (128, 128, NUM_HEADS)
        dk = Dk // H
        scale = 0.02
        return {'x': jax.random.normal(ks[0], (B, S, C), dtype=jnp.float32), 'Wq': jax.random.normal(ks[1], (C, Dk), dtype=jnp.float32) * scale, 'Wk': jax.random.normal(ks[2], (C, Dk), dtype=jnp.float32) * scale, 'Wv': jax.random.normal(ks[3], (C, Dv), dtype=jnp.float32) * scale, 'u': jax.random.normal(ks[4], (H, dk), dtype=jnp.float32) * scale, 'v': jax.random.normal(ks[5], (H, dk), dtype=jnp.float32) * scale, 'Wo': jax.random.normal(ks[6], (Dv, C), dtype=jnp.float32) * scale, 'bo': jnp.zeros((C,), dtype=jnp.float32)}
    _L0_attn_all = _L0_attn_setup()
    _L0_attn_in = {k: v for k, v in _L0_attn_all.items() if k in ('Wq', 'Wk', 'Wv', 'u', 'v', 'Wo', 'bo')}
    del _L0_attn_all

    def _L0_xattn_setup():
        import jax, jax.numpy as jnp
        import numpy as np
        D_MODEL = 128
        B, S = (4, 256)
        key = jax.random.key(seed)
        ks = jax.random.split(key, 10)
        s = 1.0 / np.sqrt(D_MODEL)
        return {'k': jax.random.normal(ks[0], (B, S, D_MODEL), jnp.float32), 'v': jax.random.normal(ks[1], (B, S, D_MODEL), jnp.float32), 'q': jax.random.normal(ks[2], (B, S, D_MODEL), jnp.float32), 'Wk': jax.random.normal(ks[3], (D_MODEL, D_MODEL), jnp.float32) * s, 'Wv': jax.random.normal(ks[4], (D_MODEL, D_MODEL), jnp.float32) * s, 'bv': jnp.zeros((D_MODEL,), jnp.float32), 'Wq': jax.random.normal(ks[5], (D_MODEL, D_MODEL), jnp.float32) * s, 'bq': jnp.zeros((D_MODEL,), jnp.float32), 'Wo': jax.random.normal(ks[6], (D_MODEL, D_MODEL), jnp.float32) * s, 'bo': jnp.zeros((D_MODEL,), jnp.float32)}
    _L0_xattn_all = _L0_xattn_setup()
    _L0_xattn_in = {k: v for k, v in _L0_xattn_all.items() if k in ('Wk', 'Wv', 'bv', 'Wq', 'bq', 'Wo', 'bo')}
    del _L0_xattn_all

    def _L0_ffn_setup():
        import jax, jax.numpy as jnp
        import numpy as np
        D_MODEL = 128
        EXPANSION = 4
        D_HIDDEN = D_MODEL * EXPANSION
        NUM_STAGES = int(np.log2(D_HIDDEN))

        def butterfly(y, weights, dim):
            lead = y.shape[:-1]
            for stage in range(weights.shape[0]):
                s = 2 ** stage
                nb = dim // (2 * s)
                yr = y.reshape(*lead, nb, 2, s)
                a = yr[..., 0, :]
                b = yr[..., 1, :]
                w = weights[stage].reshape(nb, s, 2, 2)
                na = w[..., 0, 0] * a + w[..., 0, 1] * b
                nb2 = w[..., 1, 0] * a + w[..., 1, 1] * b
                y = jnp.stack([na, nb2], axis=-2).reshape(*lead, dim)
            return y
        key = jax.random.key(seed)
        ks = jax.random.split(key, 6)
        B, S = (4, 256)
        x = jax.random.normal(ks[0], (B, S, D_MODEL), jnp.float32)
        W_exp = jax.random.normal(ks[1], (D_MODEL, D_HIDDEN), jnp.float32) * 0.02
        b_exp = jnp.zeros((D_HIDDEN,), jnp.float32)
        up_weights = jax.random.normal(ks[2], (NUM_STAGES, D_HIDDEN // 2, 2, 2), jnp.float32) * 0.02
        up_bias = jnp.zeros((D_HIDDEN,), jnp.float32)
        down_weights = jax.random.normal(ks[3], (NUM_STAGES, D_HIDDEN // 2, 2, 2), jnp.float32) * 0.02
        W_con = jax.random.normal(ks[4], (D_HIDDEN, D_MODEL), jnp.float32) * 0.02
        b_con = jnp.zeros((D_MODEL,), jnp.float32)
        down_bias = jnp.zeros((D_MODEL,), jnp.float32)
        return dict(x=x, W_exp=W_exp, b_exp=b_exp, up_weights=up_weights, up_bias=up_bias, down_weights=down_weights, W_con=W_con, b_con=b_con, down_bias=down_bias)
    _L0_ffn_all = _L0_ffn_setup()
    _L0_ffn_in = {k: v for k, v in _L0_ffn_all.items() if k in ('W_exp', 'b_exp', 'up_weights', 'up_bias', 'down_weights', 'W_con', 'b_con', 'down_bias')}
    del _L0_ffn_all

    def _L1_attn_setup():
        import math
        import jax, jax.numpy as jnp
        import numpy as np
        B, T, C, H, DQK, DV = (2, 256, 128, 16, 64, 64)
        key = jax.random.key(seed)
        ks = jax.random.split(key, 5)
        x = jax.random.normal(ks[0], (B, T, C), dtype=jnp.float32)
        w_q = jax.random.normal(ks[1], (H, DQK, C), dtype=jnp.float32) / math.sqrt(C)
        w_k = jax.random.normal(ks[2], (H, DQK, C), dtype=jnp.float32) / math.sqrt(C)
        w_v = jax.random.normal(ks[3], (H, DV, C), dtype=jnp.float32) / math.sqrt(C)
        w_o = jax.random.normal(ks[4], (DV * H, C), dtype=jnp.float32) / math.sqrt(C)
        return {'x': x, 'w_q': w_q, 'w_k': w_k, 'w_v': w_v, 'w_o': w_o}
    _L1_attn_all = _L1_attn_setup()
    _L1_attn_in = {k: v for k, v in _L1_attn_all.items() if k in ('w_q', 'w_k', 'w_v', 'w_o')}
    del _L1_attn_all

    def _L1_xattn_setup():
        import jax, jax.numpy as jnp
        import numpy as np
        B, F, T, D = (8, 32, 32, 128)
        NEG = -1e+30
        key = jax.random.key(seed)
        ks = jax.random.split(key, 10)
        s = 1.0 / np.sqrt(D)
        return {'features': jax.random.normal(ks[0], (B, F, D), jnp.float32), 'masks': jnp.ones((B, F), jnp.float32), 'textual_features': jax.random.normal(ks[1], (B, T, D), jnp.float32), 'q_masks': jax.random.randint(ks[2], (B, T), 0, 2, jnp.int32), 'Ws': jax.random.normal(ks[3], (D, D), jnp.float32) * s, 'W': jax.random.normal(ks[4], (D, D), jnp.float32) * s, 'w': jax.random.normal(ks[5], (D, 1), jnp.float32) * s, 'b': jax.random.normal(ks[6], (1, D), jnp.float32) * s, 'Wcw': jax.random.normal(ks[7], (1, D), jnp.float32) * s, 'bcw': jnp.zeros((1,), jnp.float32), 'Wcb': jax.random.normal(ks[8], (1, D), jnp.float32) * s, 'bcb': jnp.zeros((1,), jnp.float32)}
    _L1_xattn_all = _L1_xattn_setup()
    _L1_xattn_in = {k: v for k, v in _L1_xattn_all.items() if k in ('Ws', 'W', 'w', 'b', 'Wcw', 'bcw', 'Wcb', 'bcb')}
    del _L1_xattn_all

    def _L1_ffn_setup():
        import jax, jax.numpy as jnp
        import numpy as np
        D, F, E, K = (128, 344, 8, 2)
        key = jax.random.key(seed)
        k0, k1, k2, k3, k4 = jax.random.split(key, 5)
        s = 0.02
        x = jax.random.normal(k0, (2, 64, D), jnp.float32)
        Ws = jax.random.normal(k1, (D, E), jnp.float32) * s
        bs = jnp.zeros((E,), jnp.float32)
        Wg = jax.random.normal(k2, (E, D, F), jnp.float32) * s
        Wu = jax.random.normal(k3, (E, D, F), jnp.float32) * s
        Wd = jax.random.normal(k4, (E, F, D), jnp.float32) * s
        return {'x': x, 'Ws': Ws, 'bs': bs, 'Wg': Wg, 'Wu': Wu, 'Wd': Wd}
    _L1_ffn_all = _L1_ffn_setup()
    _L1_ffn_in = {k: v for k, v in _L1_ffn_all.items() if k in ('Ws', 'bs', 'Wg', 'Wu', 'Wd')}
    del _L1_ffn_all
    return {'x': x, 'ctx_1024': ctx_1024, 'mask_BxS_ff1': mask_BxS_ff1, 'mask_BxS2_ik0': mask_BxS2_ik0, 'L0_attn_Wq': _L0_attn_in['Wq'], 'L0_attn_Wk': _L0_attn_in['Wk'], 'L0_attn_Wv': _L0_attn_in['Wv'], 'L0_attn_u': _L0_attn_in['u'], 'L0_attn_v': _L0_attn_in['v'], 'L0_attn_Wo': _L0_attn_in['Wo'], 'L0_attn_bo': _L0_attn_in['bo'], 'L0_xattn_Wk': _L0_xattn_in['Wk'], 'L0_xattn_Wv': _L0_xattn_in['Wv'], 'L0_xattn_bv': _L0_xattn_in['bv'], 'L0_xattn_Wq': _L0_xattn_in['Wq'], 'L0_xattn_bq': _L0_xattn_in['bq'], 'L0_xattn_Wo': _L0_xattn_in['Wo'], 'L0_xattn_bo': _L0_xattn_in['bo'], 'L0_ffn_W_exp': _L0_ffn_in['W_exp'], 'L0_ffn_b_exp': _L0_ffn_in['b_exp'], 'L0_ffn_up_weights': _L0_ffn_in['up_weights'], 'L0_ffn_up_bias': _L0_ffn_in['up_bias'], 'L0_ffn_down_weights': _L0_ffn_in['down_weights'], 'L0_ffn_W_con': _L0_ffn_in['W_con'], 'L0_ffn_b_con': _L0_ffn_in['b_con'], 'L0_ffn_down_bias': _L0_ffn_in['down_bias'], 'L1_attn_w_q': _L1_attn_in['w_q'], 'L1_attn_w_k': _L1_attn_in['w_k'], 'L1_attn_w_v': _L1_attn_in['w_v'], 'L1_attn_w_o': _L1_attn_in['w_o'], 'L1_xattn_Ws': _L1_xattn_in['Ws'], 'L1_xattn_W': _L1_xattn_in['W'], 'L1_xattn_w': _L1_xattn_in['w'], 'L1_xattn_b': _L1_xattn_in['b'], 'L1_xattn_Wcw': _L1_xattn_in['Wcw'], 'L1_xattn_bcw': _L1_xattn_in['bcw'], 'L1_xattn_Wcb': _L1_xattn_in['Wcb'], 'L1_xattn_bcb': _L1_xattn_in['bcb'], 'L1_ffn_Ws': _L1_ffn_in['Ws'], 'L1_ffn_bs': _L1_ffn_in['bs'], 'L1_ffn_Wg': _L1_ffn_in['Wg'], 'L1_ffn_Wu': _L1_ffn_in['Wu'], 'L1_ffn_Wd': _L1_ffn_in['Wd']}

def reference(x, ctx_1024, mask_BxS_ff1, mask_BxS2_ik0, L0_attn_Wq, L0_attn_Wk, L0_attn_Wv, L0_attn_u, L0_attn_v, L0_attn_Wo, L0_attn_bo, L0_xattn_Wk, L0_xattn_Wv, L0_xattn_bv, L0_xattn_Wq, L0_xattn_bq, L0_xattn_Wo, L0_xattn_bo, L0_ffn_W_exp, L0_ffn_b_exp, L0_ffn_up_weights, L0_ffn_up_bias, L0_ffn_down_weights, L0_ffn_W_con, L0_ffn_b_con, L0_ffn_down_bias, L1_attn_w_q, L1_attn_w_k, L1_attn_w_v, L1_attn_w_o, L1_xattn_Ws, L1_xattn_W, L1_xattn_w, L1_xattn_b, L1_xattn_Wcw, L1_xattn_bcw, L1_xattn_Wcb, L1_xattn_bcb, L1_ffn_Ws, L1_ffn_bs, L1_ffn_Wg, L1_ffn_Wu, L1_ffn_Wd):
    import jax
    import jax.numpy as jnp

    def _L0_attn_ref(x, Wq, Wk, Wv, u, v, Wo, bo):
        import jax, jax.numpy as jnp
        import numpy as np
        NUM_HEADS = 16

        def _sinusoid_rel_pos(seq_len, dim):
            pos = jnp.arange(seq_len - 1, -1, -1, dtype=jnp.float32)
            inv_freq = 1.0 / 10000.0 ** (jnp.arange(0, dim, 2, dtype=jnp.float32) / dim)
            ang = pos[:, None] * inv_freq[None, :]
            return jnp.concatenate([jnp.sin(ang), jnp.cos(ang)], axis=-1)

        def _rel_shift(x):
            B, H, S, L = x.shape
            x = jnp.pad(x, ((0, 0), (0, 0), (0, 0), (1, 0)))
            x = x.reshape(B, H, L + 1, S)
            return x[:, :, 1:S + 1, :]
        B, S, C = x.shape
        H = NUM_HEADS
        dk = Wq.shape[1] // H
        dv = Wv.shape[1] // H
        Q = (x @ Wq).reshape(B, S, H, dk).transpose(0, 2, 1, 3)
        K = (x @ Wk).reshape(B, S, H, dk).transpose(0, 2, 1, 3)
        V = (x @ Wv).reshape(B, S, H, dv).transpose(0, 2, 1, 3)
        r = _sinusoid_rel_pos(S, dk)
        term1 = jnp.einsum('bhqd,bhkd->bhqk', Q, K)
        term2 = jnp.einsum('bhqd,kd->bhqk', Q, r)
        term3 = jnp.einsum('hd,bhkd->bhk', u, K)[:, :, None, :]
        term4 = jnp.einsum('hd,kd->hk', v, r)[None, :, None, :]
        scores = (term1 + term3 + _rel_shift(term2 + term4)) / jnp.sqrt(jnp.asarray(dk, dtype=x.dtype))
        attn = jax.nn.softmax(scores, axis=-1)
        out = jnp.einsum('bhqk,bhkd->bqhd', attn, V).reshape(B, S, H * dv)
        return out @ Wo + bo

    def _L0_xattn_ref(k, v, q, Wk, Wv, bv, Wq, bq, Wo, bo):
        import jax, jax.numpy as jnp
        import numpy as np
        D_MODEL = 128
        B, S = (4, 256)
        kp = jnp.einsum('bsd,ed->bse', k, Wk)
        vp = jnp.einsum('bsd,ed->bse', v, Wv) + bv
        qp = jnp.einsum('bsd,ed->bse', q, Wq) + bq
        scale = 1.0 / jnp.sqrt(jnp.float32(kp.shape[-1]))
        scores = jnp.einsum('bqd,bkd->bqk', qp, kp) * scale
        probs = jax.nn.softmax(scores, axis=-1)
        ctx = jnp.einsum('bqk,bkd->bqd', probs, vp)
        return jnp.einsum('bqd,ed->bqe', ctx, Wo) + bo

    def _L0_ffn_ref(x, W_exp, b_exp, up_weights, up_bias, down_weights, W_con, b_con, down_bias):
        import jax, jax.numpy as jnp
        import numpy as np
        D_MODEL = 128
        EXPANSION = 4
        D_HIDDEN = D_MODEL * EXPANSION
        NUM_STAGES = int(np.log2(D_HIDDEN))

        def butterfly(y, weights, dim):
            lead = y.shape[:-1]
            for stage in range(weights.shape[0]):
                s = 2 ** stage
                nb = dim // (2 * s)
                yr = y.reshape(*lead, nb, 2, s)
                a = yr[..., 0, :]
                b = yr[..., 1, :]
                w = weights[stage].reshape(nb, s, 2, 2)
                na = w[..., 0, 0] * a + w[..., 0, 1] * b
                nb2 = w[..., 1, 0] * a + w[..., 1, 1] * b
                y = jnp.stack([na, nb2], axis=-2).reshape(*lead, dim)
            return y
        h = jnp.einsum('bsd,dh->bsh', x, W_exp) + b_exp
        h = butterfly(h, up_weights, D_HIDDEN)
        h = jax.nn.gelu(h + up_bias, approximate=False)
        h = butterfly(h, down_weights, D_HIDDEN)
        y = jnp.einsum('bsh,hd->bsd', h, W_con) + b_con
        return y + down_bias

    def _L1_attn_ref(x, w_q, w_k, w_v, w_o):
        import math
        import jax, jax.numpy as jnp
        import numpy as np
        B, T, C, H, DQK, DV = (2, 256, 128, 16, 64, 64)
        n, t, c = x.shape
        q = jnp.einsum('ntc,hdc->nhtd', x, w_q)
        k = jnp.einsum('ntc,hdc->nhtd', x, w_k)
        v = jnp.einsum('ntc,hdc->nhtd', x, w_v)
        scale = 1.0 / math.sqrt(w_q.shape[1])
        a = jnp.einsum('nhtd,nhsd->nhts', q, k) * scale
        causal = jnp.arange(t)[:, None] < jnp.arange(t)[None, :]
        a = jnp.where(causal[None, None, :, :], -jnp.inf, a)
        a = jax.nn.softmax(a, axis=3)
        y = jnp.einsum('nhts,nhsd->nthd', a, v).reshape(n, t, -1)
        return y @ w_o

    def _L1_xattn_ref(features, masks, textual_features, q_masks, Ws, W, w, b, Wcw, bcw, Wcb, bcb):
        import jax, jax.numpy as jnp
        import numpy as np
        B, F, T, D = (8, 32, 32, 128)
        NEG = -1e+30
        txt_proj = jnp.einsum('btd,de->bte', textual_features, Ws)
        feat_proj = jnp.einsum('bfd,de->bfe', features, W)
        h = jnp.tanh(txt_proj[:, None, :, :] + feat_proj[:, :, None, :] + b[None, None, :, :][..., 0, :])
        rho = jnp.einsum('bftd,d->bft', h, w[:, 0])
        qm = q_masks.astype(jnp.float32)
        rho = rho + (1.0 - qm)[:, None, :] * NEG
        att = jax.nn.softmax(rho, axis=-1)
        txt_h = jnp.einsum('bft,btd->bfd', att, textual_features)
        w_s = jnp.tanh(jnp.einsum('bfd,od->bfo', txt_h, Wcw) + bcw)
        b_s = jnp.tanh(jnp.einsum('bfd,od->bfo', txt_h, Wcb) + bcb)
        return w_s * features + b_s

    def _L1_ffn_ref(x, Ws, bs, Wg, Wu, Wd):
        import jax, jax.numpy as jnp
        import numpy as np
        D, F, E, K = (128, 344, 8, 2)
        b, n, d = x.shape
        xt = x.reshape(-1, d)
        logits = xt @ Ws + bs
        topk_w, topk_idx = jax.lax.top_k(logits, K)
        topk_w = jax.nn.softmax(topk_w, axis=-1)
        combine = jnp.sum(jax.nn.one_hot(topk_idx, E, dtype=xt.dtype) * topk_w[..., None], axis=1)
        g = jnp.einsum('td,edf->tef', xt, Wg)
        u = jnp.einsum('td,edf->tef', xt, Wu)
        h = jax.nn.silu(g) * u
        y = jnp.einsum('tef,efd->ted', h, Wd)
        out = jnp.einsum('ted,te->td', y, combine)
        return out.reshape(b, n, d)
    x = _layernorm(x + _L0_attn_ref(x, L0_attn_Wq, L0_attn_Wk, L0_attn_Wv, L0_attn_u, L0_attn_v, L0_attn_Wo, L0_attn_bo), axis=-1)
    x = _layernorm(x + _L0_xattn_ref(ctx_1024, ctx_1024, x, L0_xattn_Wk, L0_xattn_Wv, L0_xattn_bv, L0_xattn_Wq, L0_xattn_bq, L0_xattn_Wo, L0_xattn_bo), axis=-1)
    x = _layernorm(x + _L0_ffn_ref(x, L0_ffn_W_exp, L0_ffn_b_exp, L0_ffn_up_weights, L0_ffn_up_bias, L0_ffn_down_weights, L0_ffn_W_con, L0_ffn_b_con, L0_ffn_down_bias), axis=-1)
    x = _layernorm(x + _L1_attn_ref(x, L1_attn_w_q, L1_attn_w_k, L1_attn_w_v, L1_attn_w_o), axis=-1)
    x = _layernorm(x + _L1_xattn_ref(x, mask_BxS_ff1, ctx_1024, mask_BxS2_ik0, L1_xattn_Ws, L1_xattn_W, L1_xattn_w, L1_xattn_b, L1_xattn_Wcw, L1_xattn_bcw, L1_xattn_Wcb, L1_xattn_bcb), axis=-1)
    x = _layernorm(x + _L1_ffn_ref(x, L1_ffn_Ws, L1_ffn_bs, L1_ffn_Wg, L1_ffn_Wu, L1_ffn_Wd), axis=-1)
    return x

_drawn_inputs = setup_inputs


def setup_inputs(seed=0):
    import zlib

    import numpy as np

    out = dict(_drawn_inputs(seed))
    spreads = {'L0_attn_bo': (0.0, 0.1),
     'L0_xattn_bv': (0.0, 0.1),
     'L0_xattn_bq': (0.0, 0.1),
     'L0_xattn_bo': (0.0, 0.1),
     'L0_ffn_b_exp': (0.0, 0.1),
     'L0_ffn_up_bias': (0.0, 0.1),
     'L0_ffn_b_con': (0.0, 0.1),
     'L0_ffn_down_bias': (0.0, 0.1),
     'L1_ffn_bs': (0.0, 0.8)}
    factors = {'L0_attn_Wq': 8.0,
     'L0_attn_Wk': 8.0,
     'L0_attn_Wv': 8.0,
     'L0_attn_u': 8.0,
     'L0_attn_v': 8.0,
     'L0_attn_Wo': 8.0,
     'L1_xattn_Ws': 8.0,
     'L1_xattn_W': 8.0,
     'L1_xattn_w': 8.0,
     'L1_xattn_b': 8.0,
     'L1_xattn_Wcw': 8.0,
     'L1_xattn_Wcb': 8.0,
     'L1_ffn_Ws': 8.0,
     'L1_ffn_Wg': 8.0,
     'L1_ffn_Wu': 8.0,
     'L1_ffn_Wd': 8.0}
    for name, (base, spread) in spreads.items():
        noise = np.random.default_rng([zlib.crc32(name.encode()), seed]).standard_normal(out[name].shape)
        drawn = base * np.exp(spread * noise) if base else spread * noise
        out[name] = jnp.asarray(drawn.astype(out[name].dtype))
    for name, factor in factors.items():
        out[name] = (out[name] * factor).astype(out[name].dtype)
    return out
```

```python
from contextlib import ExitStack

import concourse.bass as bass
from concourse import mybir
from concourse.alu_op_type import AluOpType as ALU

F32 = mybir.dt.float32
BF16 = mybir.dt.bfloat16
I32 = mybir.dt.int32
U32 = mybir.dt.uint32
ACT = mybir.ActivationFunctionType
AX = mybir.AxisListType.X

S = 128
D = 128
T2 = 77
T2P = 80
H = 16
DK = D // H
DQ = 64
HID = 512
NSTAGE = 9
FE = 344
E = 8
EPS = 1e-5
HIDDEN = -1e30
PEEL = 4
UNROLL = 4


def need(eng, sem, value):
    if not isinstance(value, int) or value > 0:
        eng.wait_ge(sem, value)


def apart(eng, passed, count, waits):
    for _, v in waits:
        if not isinstance(v, int):
            eng.to_reg(v)
    eng.wait_ge(passed, count)
    for sem, v in waits:
        need(eng, sem, v)


def rounds(eng, n, lag, body, peel=PEEL):
    def peeled(i):
        body(i, i % UNROLL, lambda k: 0 <= i - k < n)
    for i in range(peel):
        peeled(i)
    with eng.Fori(peel // UNROLL, n // UNROLL) as r:
        for u in range(UNROLL):
            body(r * UNROLL + u, u, lambda k: True)
    for i in range(n, n + lag):
        peeled(i)


def landed(i, par):
    return i * 8 + (16 - 8 * par)


def heads(ap, n):
    return ap.rearrange("p (h k) -> p h k", h=n)


def spread(ap, n, where):
    ap = ap.unsqueeze(where)
    shape = list(ap.shape)
    shape[where] = n
    return ap.broadcast_to(shape)


def norm_parts(sb, sem, p, g=1):
    return {
        "g": g,
        "stats": [sb(f"{p}_stats{k}", [S, g, 6], F32) for k in range(2)],
        "mv": [sb(f"{p}_mv{k}", [S, g, 2], F32) for k in range(2)],
        "vare": [sb(f"{p}_vare{k}", [S, g], F32) for k in range(2)],
        "rstd": [sb(f"{p}_rstd{k}", [S, g], F32) for k in range(2)],
        "power": sb(f"{p}_power", [S, g], F32),
        "power_set": sem(f"{p}_power_set"),
        "stat_done": sem(f"{p}_stat_done"),
        "mv_done": sem(f"{p}_mv_done"),
        "vare_done": sem(f"{p}_vare_done"),
        "rstd_done": sem(f"{p}_rstd_done"),
        "normed": sem(f"{p}_normed"),
    }


def norm_measure(nc, dve, norm, i, par, y):
    g = norm["g"]
    need(dve, norm["mv_done"], g * (i - 1))
    for k in range(g):
        nc.vector.bn_stats(norm["stats"][par][:, k, :], y[:, k, :]).then_inc(norm["stat_done"], 1)
    apart(dve, norm["power_set"], 1, (
        (norm["stat_done"], g * (i + 1)),
        (norm["normed"], g * (i - 1)),
        (norm["vare_done"], i - 1)))
    for k in range(g):
        nc.vector.bn_aggr(norm["mv"][par][:, k, :], norm["stats"][par][:, k, :]).then_inc(norm["mv_done"], 1)


def norm_start(nc, pool, norm):
    nc.gpsimd.memset(norm["power"][:], -0.5).then_inc(norm["power_set"], 1)
    pool.wait_ge(norm["power_set"], 1)


def norm_root(nc, pool, norm, i, par, also=()):
    apart(pool, norm["power_set"], 1, (
        (norm["mv_done"], norm["g"] * (i + 1)),
        (norm["rstd_done"], i - 1),
        *also))
    nc.gpsimd.tensor_scalar(norm["vare"][par][:], norm["mv"][par][:, :, 1], EPS, None, ALU.add).then_inc(norm["vare_done"], 1)
    need(pool, norm["vare_done"], i + 1)
    need(pool, norm["normed"], norm["g"] * (i - 1))
    nc.gpsimd.tensor_tensor(norm["rstd"][par][:], norm["vare"][par][:], norm["power"][:], ALU.pow).then_inc(norm["rstd_done"], 1)


def norm_apply(nc, dve, norm, i, par, out, y):
    need(dve, norm["rstd_done"], i + 1)
    for k in range(norm["g"]):
        nc.vector.tensor_scalar(out[:, k, :], y[:, k, :], norm["mv"][par][:, k, 0:1], norm["rstd"][par][:, k:k + 1],
                                ALU.subtract, ALU.mult).then_inc(norm["normed"], 1)


def self_attention_0(nc, sem, n, x_all, ident, A):
    NQ = 4
    HQ = H // NQ
    with ExitStack() as ctx:
        def sb(name, shape, dt):
            return ctx.enter_context(nc.sbuf_tensor(name, shape, dt))

        def psum(name, shape):
            return ctx.enter_context(nc.psum_tensor(name, shape, F32))

        wq = sb("a_wq", [D, 5, 128], F32)
        wv = sb("a_wv", [D, D], F32)
        wo = sb("a_wo", [D, D], F32)
        bo = sb("a_bo", [S, D], F32)
        ub = sb("a_ub", [128, 4], F32)
        turn = sb("a_turn", [128, 8, S], F32)
        hmask = sb("a_hmask", [128, 8], F32)
        hsum = sb("a_hsum", [128, H], F32)
        above = sb("a_above", [S, S], U32)
        beside = sb("a_beside", [S, S], U32)
        xs = [sb(f"a_xs{k}", [S, D], F32) for k in range(2)]
        xT = [sb(f"a_xT{k}", [D, S], F32) for k in range(2)]
        kT = [sb(f"a_kT{k}", [D, S], F32) for k in range(2)]
        kr = [sb(f"a_kr{k}", [128, H * S], F32) for k in range(2)]
        vp = [sb(f"a_vp{k}", [S, H, 32], F32) for k in range(4)]
        ql = [sb(f"a_ql{k}", [128, 2, S], F32) for k in range(2)]
        qu = [sb(f"a_qu{k}", [128, 2, S], F32) for k in range(2)]
        t1 = sb("a_t1", [128, 4, S], F32)
        qb = sb("a_qb", [128, 4, S], F32)
        t2 = sb("a_t2", [128, 4, S], F32)
        pr = [sb(f"a_pr{k}", [128, S], F32) for k in range(2)]
        nmx = [sb(f"a_nmx{k}", [S, HQ], F32) for k in range(NQ)]
        pe_ = [sb(f"a_pe{k}", [S, HQ * S], F32) for k in range(NQ)]
        bs = [sb(f"a_bs{k}", [S, H], F32) for k in range(2)]
        pT = [sb(f"a_pT{k}", [S, HQ * S], F32) for k in range(2)]
        avs = sb("a_avs", [128, 4, S], F32)
        rden = sb("a_rden", [S, H], F32)
        att = sb("a_att", [S, D], F32)
        attT = sb("a_attT", [D, S], F32)
        y = [sb(f"a_y{k}", [S, D], F32) for k in range(2)]
        y2 = [sb(f"a_y2{k}", [S, D], F32) for k in range(2)]
        norm = norm_parts(sb, sem, "a")

        pS = [psum(f"a_pS{k}", [128, 512]) for k in range(2)]
        pU = psum("a_pU", [128, 512])
        pT_ = psum("a_pT_", [128, 512])
        pA = psum("a_pA", [128, 512])
        pO = psum("a_pO", [128, 512])
        pQ = psum("a_pQ", [128, 512])
        pW = psum("a_pW", [128, 512])
        pxT, pkT, pv, pB = pW[:, 0:128], pW[:, 128:256], pW[:, 256:384], pW[:, 384:384 + H]

        s_w = sem("a_weights")
        s_set = sem("a_set")
        s_x = [sem(f"a_x_loaded{k}") for k in range(2)]
        s_xTp = sem("a_xT_in_psum")
        s_xT = sem("a_xT_ready")
        s_kvp = sem("a_kv_in_psum")
        s_kT = sem("a_kT_ready")
        s_v = sem("a_v_ready")
        s_qp = sem("a_q_in_psum")
        s_t = sem("a_turned_parts")
        s_ql = sem("a_ql_ready")
        s_ub = sem("a_biased_queries")
        s_tm = sem("a_turned_parts_above")
        s_qu = sem("a_qu_turned")
        s_kr = sem("a_kr_ready")
        s_pr = sem("a_products")
        s_B = sem("a_beside_scores")
        s_su = sem("a_scores")
        s_pu = sem("a_above_put")
        s_pe = sem("a_beside_put")
        s_mx = sem("a_max")
        s_Bc = sem("a_beside_copied")
        s_ex = sem("a_probs")
        s_tp = sem("a_probsT_in_psum")
        s_pT = sem("a_probsT")
        s_av = sem("a_values_mixed")
        s_avs = sem("a_mixed_copied")
        s_ot = sem("a_mixed_turned")
        s_rd = sem("a_den_inverse")
        s_at = sem("a_att_normed")
        s_atp = sem("a_attT_in_psum")
        s_atT = sem("a_attT")
        s_wo = sem("a_projected")
        s_y = sem("a_y")
        s_y2 = sem("a_y2")
        s_qb = sem("a_qu_base")
        s_ini = sem("a_rows_loaded")
        s_zero = sem("a_zeroed")
        NW = 12

        block = ctx.enter_context(nc.Block())

        @block.sync
        def _(sp):
            for dst, src in ((ident[:], A["ident"]), (wq[:], A["a_wq"]), (wv[:], A["L0_attn_Wv"]),
                             (wo[:], A["L0_attn_Wo"]), (ub[:], A["a_ub"]), (turn[:], A["a_turn"]),
                             (hmask[:], A["a_hmask"]), (hsum[:], A["a_hsum"]), (above[:], A["above"]),
                             (beside[:], A["beside"]), (bo[:], A["L0_attn_bo"].unsqueeze(0).broadcast_to([S, D]))):
                sp.dma_start(dst, src).then_inc(s_w, 16)
            sp.dma_start(x_all[:, 0:n, :], A["x"].rearrange("b s d -> s b d")[:, 0:n, :]).then_inc(s_w, 16)
            sp.wait_ge(s_w, 16 * NW)

            def body(i, u, on):
                par = u % 2
                need(sp, s_xTp, i - 1)
                sp.dma_start(xs[par][:], x_all[:, bass.ds(i, 1), :].rearrange("s b d -> s (b d)")).then_inc(s_x[par], 16)
            rounds(sp, n, 0, body)

        @block.tensor
        def _(pe):
            pe.wait_ge(s_w, 16 * NW)
            pe.wait_ge(s_set, 4)

            def scores(a, par, c):
                g, half = c // 2, c % 2
                if c == 0:
                    need(pe, s_ql, a + 1)
                    need(pe, s_qb, 2 * a + 2)
                if half == 0:
                    need(pe, s_qu, 2 * a + g + 1)
                    need(pe, s_kr, 2 * a + g + 1)
                need(pe, s_ex, 4 * a + c - 1)
                nc.tensor.matmul(pS[c % 2][:], ql[par][:, g, :], kr[par][:, c * 512:(c + 1) * 512],
                                 start=True, stop=True)
                need(pe, s_pu, 4 * a + c)
                nc.tensor.matmul(pU[:], qu[par][:, g, :], kr[par][:, c * 512:(c + 1) * 512],
                                 start=True, stop=True).then_inc(s_su, 1)

            def turn_probs(a, c):
                need(pe, s_ex, 4 * a + c + 1)
                need(pe, s_pT, 4 * a + c)
                for j in range(HQ):
                    last = nc.tensor.transpose(pT_[:, j * S:(j + 1) * S], pe_[c][:, j * S:(j + 1) * S], ident[:])
                last.then_inc(s_tp, 1)

            def mix(a, v, c):
                need(pe, s_pT, 4 * a + c + 1)
                if c == 0:
                    need(pe, s_v, a + 1)
                    need(pe, s_avs, a)
                for j in range(HQ):
                    last = nc.tensor.matmul(pA[32 * j:32 * j + 32, c * S:(c + 1) * S], v[:, 4 * c + j, :],
                                            pT[c % 2][:, j * S:(j + 1) * S], start=True, stop=True)
                last.then_inc(s_av, 1)

            def body(i, u, on):
                par = u % 2
                a, t, z, q = i - 1, i - 2, i - 3, 1 - par
                v1, v2 = vp[(u + 3) % 4], vp[(u + 2) % 4]
                if on(1):
                    scores(a, q, 0)
                if on(0):
                    need(pe, s_x[par], landed(i, par))
                    need(pe, s_Bc, i)
                    nc.tensor.transpose(pxT, xs[par][:], ident[:]).then_inc(s_xTp, 1)
                if on(2):
                    turn_probs(t, 2)
                    mix(t, v2, 1)
                if on(1):
                    scores(a, q, 1)
                if on(0):
                    need(pe, s_xT, i + 1)
                    nc.tensor.matmul(pkT, wq[:, 4, :], xT[par][:], start=True, stop=True)
                    nc.tensor.matmul(pv, xT[par][:], wv[:], start=True, stop=True).then_inc(s_kvp, 1)
                if on(2):
                    turn_probs(t, 3)
                    mix(t, v2, 2)
                if on(0):
                    need(pe, s_t, 4 * i)
                    need(pe, s_ub, i)
                    for m in range(4):
                        last = nc.tensor.matmul(pQ[:, m * S:(m + 1) * S], wq[:, m, :], xT[par][:],
                                                start=True, stop=True)
                    last.then_inc(s_qp, 1)
                if on(3):
                    need(pe, s_at, z + 1)
                    nc.tensor.transpose(pO[:, 0:128], att[:], ident[:]).then_inc(s_atp, 1)
                if on(1):
                    scores(a, q, 2)
                    turn_probs(a, 0)
                if on(2):
                    mix(t, v2, 3)
                if on(3):
                    need(pe, s_atT, z + 1)
                    nc.tensor.matmul(pO[:, 128:256], attT[:], wo[:], start=True, stop=True).then_inc(s_wo, 1)
                if on(1):
                    scores(a, q, 3)
                    turn_probs(a, 1)
                    mix(a, v1, 0)
                if on(0):
                    need(pe, s_pr, 2 * i + 2)
                    need(pe, s_kT, i + 1)
                    need(pe, s_v, i + 1)
                    nc.tensor.matmul(pB, pr[par][:], hsum[:], start=True, stop=True).then_inc(s_B, 1)
                if on(2):
                    need(pe, s_avs, t + 1)
                    need(pe, s_y, t)
                    for c in range(4):
                        last = nc.tensor.transpose(pO[:, c * S:(c + 1) * S], avs[:, c, :], ident[:])
                    last.then_inc(s_ot, 1)
            rounds(pe, n, 3, body)

        @block.vector
        def _(dve):
            dve.wait_ge(s_w, 16 * NW)
            dve.wait_ge(s_set, 4)

            def soften(a, par, c):
                s3 = heads(pS[c % 2][:], HQ)
                apart(dve, s_set, 4, ((s_su, 4 * a + c + 1),))
                nc.vector.copy_predicated(s3, spread(above[:], HQ, 1), heads(pU[:], HQ)).then_inc(s_pu, 1)
                apart(dve, s_set, 4, ((s_pu, 4 * a + c + 1), (s_Bc, a + 1)))
                nc.vector.copy_predicated(s3, spread(beside[:], HQ, 1),
                                          spread(bs[par][:, 4 * c:4 * c + 4], S, 2)).then_inc(s_pe, 1)
                need(dve, s_pe, 4 * a + c + 1)
                need(dve, s_ex, 4 * a + c - 3)
                nc.vector.tensor_reduce(nmx[c][:], s3, AX, ALU.max, negate=True).then_inc(s_mx, 1)

            def body(i, u, on):
                par = u % 2
                a, z, w, q = i - 1, i - 3, i - 4, 1 - par
                if on(1):
                    soften(a, q, 0)
                if on(3):
                    need(dve, s_ot, z + 1)
                    o4 = pO[:].rearrange("p (h e) -> p h e", h=H)
                    nc.vector.reciprocal(rden[:], o4[:, :, DK]).then_inc(s_rd, 1)
                    need(dve, s_rd, z + 1)
                    need(dve, s_atp, z)
                    nc.vector.tensor_tensor(heads(att[:], H), o4[:, :, 0:DK], spread(rden[:], DK, 2),
                                            ALU.mult).then_inc(s_at, 1)
                if on(1):
                    soften(a, q, 1)
                if on(4):
                    norm_apply(nc, dve, norm, w, par, x_all[:, bass.ds(w, 1), :], y2[par][:].unsqueeze(1))
                if on(0):
                    need(dve, s_qp, i + 1)
                    need(dve, s_ql, i)
                    for k in range(4):
                        nc.vector.scalar_tensor_tensor(t1[:, k, :], pQ[:, k * S:(k + 1) * S], ub[:, k:k + 1], turn[:, k, :],
                                                       ALU.add, ALU.mult).then_inc(s_t, 1)
                    need(dve, s_t, 4 * i + 4)
                    need(dve, s_su, 4 * (i - 1))
                    need(dve, s_pr, 2 * (i - 1))
                    t4 = t1[:].rearrange("p (g m) q -> p g m q", g=2)
                    nc.vector.tensor_tensor(ql[par][:], t4[:, :, 0, :], t4[:, :, 1, :], ALU.add).then_inc(s_ql, 1)
                if on(1):
                    soften(a, q, 2)
                if on(3):
                    need(dve, s_wo, z + 1)
                    need(dve, s_y2, z - 1)
                    nc.vector.tensor_tensor(y[q][:], pO[:, 128:256], x_all[:, bass.ds(z, 1), :].rearrange("s b d -> s (b d)"),
                                            ALU.add).then_inc(s_y, 1)
                    need(dve, s_y, z + 1)
                    need(dve, norm["normed"], z - 1)
                    nc.vector.tensor_tensor(y2[q][:], y[q][:], bo[:], ALU.add).then_inc(s_y2, 1)
                    need(dve, s_y2, z + 1)
                    norm_measure(nc, dve, norm, z, q, y2[q][:].unsqueeze(1))
                if on(1):
                    soften(a, q, 3)
            rounds(dve, n, 4, body)

        @block.scalar
        def _(act):
            act.wait_ge(s_set, 4)

            def probs(a, c):
                need(act, s_mx, 4 * a + c + 1)
                need(act, s_tp, 4 * a + c - 3)
                for j in range(HQ):
                    last = nc.scalar.activation(pe_[c][:, j * S:(j + 1) * S], pS[c % 2][:, j * S:(j + 1) * S], ACT.Exp,
                                                bias=nmx[c][:, j:j + 1])
                last.then_inc(s_ex, 1)

            def probsT(a, c):
                need(act, s_tp, 4 * a + c + 1)
                need(act, s_av, 4 * a + c - 1)
                nc.scalar.copy(pT[c % 2][:], pT_[:]).then_inc(s_pT, 1)

            def body(i, u, on):
                par = u % 2
                a, t, z = i - 1, i - 2, i - 3
                if on(0):
                    need(act, s_xTp, i + 1)
                    need(act, s_qp, i - 1)
                    nc.scalar.copy(xT[par][:], pxT).then_inc(s_xT, 1)
                if on(2):
                    probsT(t, 2)
                if on(1):
                    probs(a, 0)
                if on(0):
                    need(act, s_kvp, i + 1)
                    need(act, s_kr, 2 * (i - 1))
                    need(act, s_pr, 2 * (i - 1))
                    nc.scalar.copy(kT[par][:], pkT).then_inc(s_kT, 1)
                    need(act, s_av, 4 * (i - 3))
                    nc.scalar.copy(vp[u][:, :, 0:DK], heads(pv, H)).then_inc(s_v, 1)
                if on(2):
                    probsT(t, 3)
                if on(1):
                    probs(a, 1)
                if on(3):
                    need(act, s_atp, z + 1)
                    need(act, s_wo, z)
                    nc.scalar.copy(attT[:], pO[:, 0:128]).then_inc(s_atT, 1)
                if on(1):
                    probsT(a, 0)
                if on(0):
                    need(act, s_t, 4 * i + 4)
                    need(act, s_tm, 2 * i)
                    for k in range(4):
                        rel = slice(64, 128) if k < 2 else slice(0, 64)
                        last = nc.scalar.activation(qb[rel, k, :], pQ[rel, k * S:(k + 1) * S], ACT.Identity, bias=ub[rel, k:k + 1])
                    last.then_inc(s_ub, 1)
                if on(2):
                    need(act, s_av, 4 * t + 4)
                    need(act, s_ot, t)
                    nc.scalar.copy(avs[:], heads(pA[:], 4)).then_inc(s_avs, 1)
                if on(1):
                    probs(a, 2)
                    probsT(a, 1)
                if on(0):
                    need(act, s_B, i + 1)
                    need(act, s_pe, 4 * (i - 1))
                    nc.scalar.copy(bs[par][:], pB).then_inc(s_Bc, 1)
                if on(1):
                    probs(a, 3)
            rounds(act, n, 3, body)

        @block.gpsimd
        def _(pool):
            norm_start(nc, pool, norm)
            for k in range(2):
                pool.dma_start(kr[k][:], A["a_rpos"]).then_inc(s_ini, 16)
                nc.gpsimd.memset(pr[k][:], 0.0).then_inc(s_zero, 1)
                nc.gpsimd.memset(qu[k][:], 0.0).then_inc(s_zero, 1)
            for k in range(4):
                nc.gpsimd.memset(vp[k][:], 0.0).then_inc(s_zero, 1)
            pool.wait_ge(s_zero, 8)
            pool.wait_ge(s_ini, 32)
            pool.wait_ge(s_w, 16 * NW)
            for k in range(4):
                nc.gpsimd.memset(vp[k][:, :, DK:DK + 1], 1.0).then_inc(s_set, 1)

            def keys(i, par, g):
                r = slice(64 * g, 64 * g + 64)
                nc.gpsimd.tensor_tensor(heads(kr[par][r, g * 1024:(g + 1) * 1024], 8), spread(kT[par][r, :], 8, 1),
                                        spread(hmask[r, :], S, 2), ALU.mult).then_inc(s_kr, 1)

            def above_rows(i, par, g):
                rel = slice(64, 128) if g == 0 else slice(0, 64)
                nc.gpsimd.tensor_tensor(t2[rel, 2 * g:2 * g + 2, 0:S - 1], qb[rel, 2 * g:2 * g + 2, 1:S],
                                        turn[rel, 4 + 2 * g:6 + 2 * g, 0:S - 1], ALU.mult).then_inc(s_tm, 1)
                need(pool, s_tm, 2 * i + g + 1)
                nc.gpsimd.tensor_tensor(qu[par][rel, g, 0:S - 1], t2[rel, 2 * g, 0:S - 1], t2[rel, 2 * g + 1, 0:S - 1],
                                        ALU.add).then_inc(s_qu, 1)

            def body(i, u, on):
                par = u % 2
                z, q = i - 3, 1 - par
                if on(0):
                    need(pool, s_kT, i + 1)
                    need(pool, s_su, 4 * (i - 1))
                    need(pool, norm["rstd_done"], i - 3)
                    need(pool, s_kr, 2 * i)
                    keys(i, par, 0)
                    need(pool, s_ql, i + 1)
                    need(pool, s_B, i - 1)
                    need(pool, s_kr, 2 * i + 1)
                    for g in range(2):
                        r = slice(64 * g, 64 * g + 64)
                        need(pool, s_qb, 2 * i + g)
                        nc.gpsimd.tensor_tensor(pr[par][r, 0:S - 1], ql[par][r, g, 0:S - 1], kT[par][r, 1:S],
                                                ALU.mult).then_inc(s_pr, 1)
                        apart(pool, s_zero, 8, ((s_pr, 2 * i + g + 1),))
                        nc.gpsimd.tensor_copy(qu[par][r, g, :], ql[par][r, g, :]).then_inc(s_qb, 1)
                    need(pool, s_qb, 2 * i + 2)
                    need(pool, s_ub, i + 1)
                    need(pool, s_qu, 2 * i)
                    above_rows(i, par, 0)
                    need(pool, s_qu, 2 * i + 1)
                    keys(i, par, 1)
                    need(pool, s_kr, 2 * i + 2)
                    above_rows(i, par, 1)
                if on(3):
                    norm_root(nc, pool, norm, z, q, ((s_qu, 2 * i + 2),) if on(0) else ())
            rounds(pool, n, 3, body)


def cross_attention_0(nc, sem, n, x_all, ident, A):
    SCALE = float(D) ** -0.5
    with ExitStack() as ctx:
        def sb(name, shape, dt=F32):
            return ctx.enter_context(nc.sbuf_tensor(name, shape, dt))

        def pair(name, shape):
            return [sb(f"{name}{k}", shape) for k in range(2)]

        def bank(name):
            return ctx.enter_context(nc.psum_tensor(name, [128, 512], F32))

        w = sb("c_w", [D, 4, D])
        bq, bv, bo = sb("c_bq", [D, 1]), sb("c_bv", [D, 1]), sb("c_bo", [S, D])
        xs, cs = pair("c_xs", [S, D]), pair("c_cs", [T2, D])
        xT, cT = pair("c_xT", [D, S]), pair("c_cT", [D, 128])
        qT, kT = pair("c_qT", [D, S]), pair("c_kT", [D, 128])
        v = [sb(f"c_v{k}", [T2, D]) for k in range(4)]
        mx, nm, den, rden = pair("c_mx", [S, 1]), pair("c_nm", [S, 1]), pair("c_den", [S, 1]), pair("c_rden", [S, 1])
        ex, pn = pair("c_ex", [S, T2]), pair("c_pn", [S, T2])
        pT, oT = pair("c_pT", [T2, S]), pair("c_oT", [D, S])
        y, y2 = pair("c_y", [S, 1, D]), pair("c_y2", [S, 1, D])
        norm = norm_parts(sb, sem, "c")
        pX, pQ, pS, pP, pM, pO = (bank(f"c_p{k}") for k in "XQSPMO")

        s_w, s_set = sem("c_weights"), sem("c_set")
        s_x = [sem(f"c_loaded{k}") for k in range(2)]
        s_xp, s_xT, s_cT = sem("c_xcT_in_psum"), sem("c_xT"), sem("c_cT")
        s_qp, s_q, s_k, s_v = sem("c_qkv_in_psum"), sem("c_q"), sem("c_k"), sem("c_v_ready")
        s_s, s_mx, s_nm, s_ex, s_rd, s_pn = (sem(f"c_{k}") for k in ("scores", "max", "negmax", "exp", "rden", "probs"))
        s_pp, s_pT, s_mp, s_oT, s_op, s_y, s_y2 = (sem(f"c_{k}") for k in (
            "pT_in_psum", "pT_ready", "mixed_in_psum", "mixed", "out_in_psum", "y_ready", "y2_ready"))

        block = ctx.enter_context(nc.Block())

        @block.sync
        def _(sp):
            for k, name in enumerate(("c_wqT", "c_wkT", "c_wvT", "c_woT")):
                sp.dma_start(w[:, k, :], A[name]).then_inc(s_w, 16)
            sp.dma_start(bq[:], A["L0_xattn_bq"].unsqueeze(1)).then_inc(s_w, 16)
            sp.dma_start(bv[:], A["L0_xattn_bv"].unsqueeze(1)).then_inc(s_w, 16)
            sp.dma_start(bo[:], A["L0_xattn_bo"].unsqueeze(0).broadcast_to([S, D])).then_inc(s_w, 16)

            def body(i, u, on):
                par = u % 2
                need(sp, s_xp, i - 1)
                sp.dma_start(xs[par][:], x_all[:, bass.ds(i, 1), :].rearrange("s b d -> s (b d)")).then_inc(s_x[par], 16)
                sp.dma_start(cs[par][:], A["ctx_1024"][bass.ds(i, 1), :, :].rearrange("b t d -> (b t) d")).then_inc(s_x[par], 16)
            rounds(sp, n, 0, body, 8)

        @block.tensor
        def _(pe):
            pe.wait_ge(s_w, 16 * 7)
            pe.wait_ge(s_set, 2)

            def body(i, u, on):
                par = u % 2
                q = 1 - par
                if on(5):
                    t = i - 5
                    need(pe, s_oT, t + 1)
                    need(pe, s_y, t)
                    nc.tensor.matmul(pO[:, 0:D], oT[q][:], w[:, 3, :], start=True, stop=True).then_inc(s_op, 1)
                if on(4):
                    t = i - 4
                    need(pe, s_pT, t + 1)
                    need(pe, s_oT, t)
                    nc.tensor.matmul(pM[:, 0:S], v[u][:], pT[par][:], start=True, stop=True).then_inc(s_mp, 1)
                if on(3):
                    t = i - 3
                    need(pe, s_pn, t + 1)
                    need(pe, s_pT, t)
                    nc.tensor.transpose(pP[0:T2, 0:S], pn[q][:], ident[:]).then_inc(s_pp, 1)
                if on(2):
                    t = i - 2
                    need(pe, s_q, t + 1)
                    need(pe, s_k, t + 1)
                    need(pe, s_ex, t)
                    nc.tensor.matmul(pS[:, 0:128], qT[par][:], kT[par][:], start=True, stop=True).then_inc(s_s, 1)
                if on(1):
                    t = i - 1
                    need(pe, s_xT, t + 1)
                    need(pe, s_cT, t + 1)
                    need(pe, s_v, t)
                    nc.tensor.matmul(pQ[:, 0:128], w[:, 0, :], xT[q][:], start=True, stop=True)
                    nc.tensor.matmul(pQ[:, 128:256], w[:, 1, :], cT[q][:], start=True, stop=True)
                    nc.tensor.matmul(pQ[0:T2, 256:384], cT[q][:, 0:T2], w[:, 2, :], start=True, stop=True).then_inc(s_qp, 1)
                if on(0):
                    need(pe, s_x[par], landed(i, par) * 2)
                    need(pe, s_cT, i)
                    nc.tensor.transpose(pX[:, 0:S], xs[par][:], ident[:])
                    nc.tensor.transpose(pX[:, S:S + T2], cs[par][:], ident[0:T2, 0:T2]).then_inc(s_xp, 1)
            rounds(pe, n, 5, body, 8)

        @block.scalar
        def _(act):
            act.wait_ge(s_w, 16 * 7)
            act.wait_ge(s_set, 2)

            def body(i, u, on):
                par = u % 2
                q = 1 - par
                if on(4):
                    t = i - 4
                    need(act, s_mp, t + 1)
                    need(act, s_op, t - 1)
                    nc.scalar.activation(oT[par][:], pM[:, 0:S], ACT.Identity, bias=bv[:]).then_inc(s_oT, 1)
                if on(3):
                    t = i - 3
                    need(act, s_pp, t + 1)
                    need(act, s_mp, t - 1)
                    nc.scalar.copy(pT[q][:], pP[0:T2, 0:S]).then_inc(s_pT, 1)
                if on(2):
                    t = i - 2
                    need(act, s_nm, t + 1)
                    need(act, s_pn, t - 1)
                    need(act, s_rd, t - 1)
                    nc.scalar.activation(ex[par][:], pS[:, 0:T2], ACT.Exp, bias=nm[par][:], scale=SCALE,
                                         accum_out=den[par][:]).then_inc(s_ex, 1)
                if on(1):
                    t = i - 1
                    need(act, s_qp, t + 1)
                    need(act, s_s, t - 1)
                    nc.scalar.activation(qT[q][:], pQ[:, 0:128], ACT.Identity, bias=bq[:]).then_inc(s_q, 1)
                    nc.scalar.copy(kT[q][:], pQ[:, 128:256]).then_inc(s_k, 1)
                    need(act, s_mp, t - 3)
                    nc.scalar.copy(v[(u - 1) % 4][:], pQ[0:T2, 256:384]).then_inc(s_v, 1)
                if on(0):
                    need(act, s_xp, i + 1)
                    need(act, s_qp, i - 1)
                    nc.scalar.copy(xT[par][:], pX[:, 0:S]).then_inc(s_xT, 1)
                    nc.scalar.copy(cT[par][:, 0:T2], pX[:, S:S + T2]).then_inc(s_cT, 1)
            rounds(act, n, 5, body, 8)

        @block.vector
        def _(dve):
            dve.wait_ge(s_w, 16 * 7)

            def body(i, u, on):
                par = u % 2
                q = 1 - par
                if on(6):
                    t = i - 6
                    norm_apply(nc, dve, norm, t, par, x_all[:, bass.ds(t, 1), :], y2[par][:])
                if on(5):
                    t = i - 5
                    need(dve, s_op, t + 1)
                    need(dve, s_y2, t - 1)
                    nc.vector.tensor_tensor(y[q][:, 0, :], pO[:, 0:D], x_all[:, bass.ds(t, 1), :].rearrange("s b d -> s (b d)"),
                                            ALU.add).then_inc(s_y, 1)
                    need(dve, s_y, t + 1)
                    need(dve, norm["normed"], t - 1)
                    nc.vector.tensor_tensor(y2[q][:, 0, :], y[q][:, 0, :], bo[:], ALU.add).then_inc(s_y2, 1)
                    need(dve, s_y2, t + 1)
                    norm_measure(nc, dve, norm, t, q, y2[q][:])
                if on(2):
                    t = i - 2
                    need(dve, s_s, t + 1)
                    nc.vector.tensor_reduce(mx[par][:], pS[:, 0:T2], AX, ALU.max).then_inc(s_mx, 1)
                    need(dve, s_mx, t + 1)
                    need(dve, s_ex, t - 1)
                    nc.vector.tensor_scalar(nm[par][:], mx[par][:], -SCALE, None, ALU.mult).then_inc(s_nm, 1)
                    need(dve, s_ex, t + 1)
                    need(dve, s_pn, t - 1)
                    nc.vector.reciprocal(rden[par][:], den[par][:]).then_inc(s_rd, 1)
                    need(dve, s_rd, t + 1)
                    need(dve, s_pp, t - 1)
                    nc.vector.tensor_scalar(pn[par][:], ex[par][:], rden[par][:], None, ALU.mult).then_inc(s_pn, 1)
            rounds(dve, n, 6, body, 8)

        @block.gpsimd
        def _(pool):
            norm_start(nc, pool, norm)
            for k in range(2):
                nc.gpsimd.memset(cT[k][:], 0.0).then_inc(s_set, 1)

            def body(i, u, on):
                par = u % 2
                if on(5):
                    norm_root(nc, pool, norm, i - 5, 1 - par)
            rounds(pool, n, 6, body, 8)

def butterfly_weights(nc, sem, ident, A, w1, b1, w2, b2):
    with ExitStack() as ctx:
        def sb(name, shape, dt=F32):
            return ctx.enter_context(nc.sbuf_tensor(name, shape, dt))

        RING = 3
        wr = {k: [sb(f"b_w{k}{j}", [128, 2 * HID]) for j in range(RING)] for k in "ud"}
        row = {"u": [sb(f"b_u{j}", [128, 2, HID]) for j in range(2)], "d": [sb(f"b_d{j}", [128, 1, HID]) for j in range(2)]}
        tmp = {k: sb(f"b_t{k}", [128, 2, 2, HID]) for k in "ud"}
        bias = sb("b_bias", [128, 2, D])
        upb = sb("b_upb", [128, HID // 128])
        ones = sb("b_ones", [1, 1])
        p1 = ctx.enter_context(nc.psum_tensor("b_p1", [128, 512], F32))
        p2 = ctx.enter_context(nc.psum_tensor("b_p2", [128, 512], F32))
        s_in = sem("b_inputs")
        s_w = {k: [sem(f"b_w_{k}{j}") for j in range(RING)] for k in "ud"}
        s_mul = {k: sem(f"b_products_{k}") for k in "ud"}
        s_add = {k: sem(f"b_stage_{k}") for k in "ud"}
        s_cp, s_one, s_t, s_up, s_b2 = sem("b_w1_copied"), sem("b_one"), sem("b_turned"), sem("b_up_bias"), sem("b_out")
        nrow = {"u": 2, "d": 1}
        block = ctx.enter_context(nc.Block())

        def stage(k, n):
            return n if k == "u" else NSTAGE - 1 - n

        @block.sync
        def _(sp):
            sp.dma_start(row["u"][0][:, 0, :], A["L0_ffn_W_exp"]).then_inc(s_in, 16)
            sp.dma_start(row["u"][0][:, 1, :], A["L0_ffn_b_exp"].unsqueeze(0).broadcast_to([128, HID])).then_inc(s_in, 16)
            sp.dma_start(row["d"][0][:, 0, :], A["f_wconT"]).then_inc(s_in, 16)
            sp.dma_start(bias[:, 0, :], A["L0_ffn_b_con"].unsqueeze(0).broadcast_to([128, D])).then_inc(s_in, 16)
            sp.dma_start(bias[:, 1, :], A["L0_ffn_down_bias"].unsqueeze(0).broadcast_to([128, D])).then_inc(s_in, 16)
            sp.dma_start(upb[:], A["f_upb"]).then_inc(s_in, 16)
            for n in range(NSTAGE):
                for k, name in (("u", "L0_ffn_up_weights"), ("d", "L0_ffn_down_weights")):
                    if n >= RING:
                        sp.wait_ge(s_mul[k], 2 * nrow[k] * (n - RING + 1))
                    src = A[name][stage(k, n)].rearrange("p i j -> (p i j)").unsqueeze(0).broadcast_to([128, 2 * HID])
                    sp.dma_start(wr[k][n % RING][:], src).then_inc(s_w[k][n % RING], 16)

        def stages(eng, ops, k):
            R = nrow[k]
            eng.wait_ge(s_in, 16 * 6)
            for n in range(NSTAGE):
                st = 2 ** stage(k, n)
                nb = HID // (2 * st)
                w = wr[k][n % RING][:].rearrange("p (b s i j) -> p b s i j", b=nb, s=st, i=2)
                eng.wait_ge(s_w[k][n % RING], 16 * (n // RING + 1))
                if n >= 1:
                    eng.wait_ge(s_add[k], R * n)
                for r in range(R):
                    pairs = row[k][n % 2][:, r, :].rearrange("p (b w s) -> p b w s", b=nb, w=2)
                    for j in range(2):
                        wj = (w[:, :, :, :, j] if k == "u" else w[:, :, :, j, :]).rearrange("p b s i -> p b i s")
                        out = tmp[k][:, r, j, :].rearrange("p (b i s) -> p b i s", b=nb, i=2)
                        ops.tensor_tensor(out, pairs[:, :, j:j + 1, :].broadcast_to([128, nb, 2, st]), wj,
                                          ALU.mult).then_inc(s_mul[k], 1)
                eng.wait_ge(s_mul[k], 2 * R * (n + 1))
                for r in range(R):
                    ops.tensor_tensor(row[k][(n + 1) % 2][:, r, :], tmp[k][:, r, 0, :], tmp[k][:, r, 1, :],
                                      ALU.add).then_inc(s_add[k], 1)

        @block.vector
        def _(dve):
            nc.vector.memset(ones[:], 1.0).then_inc(s_one, 1)
            stages(dve, nc.vector, "u")
            dve.wait_ge(s_add["u"], 2 * NSTAGE)
            nc.vector.tensor_copy(w1[:], row["u"][NSTAGE % 2][:, 0, :]).then_inc(s_cp, 1)
            dve.wait_ge(s_t, 1)
            nc.vector.tensor_tensor(b1[:], p1[:, 0:4], upb[:], ALU.add).then_inc(s_up, 1)

        @block.gpsimd
        def _(pool):
            stages(pool, nc.gpsimd, "d")
            nc.gpsimd.tensor_tensor(b2[:], bias[:, 0, :], bias[:, 1, :], ALU.add).then_inc(s_b2, 1)

        @block.tensor
        def _(pe):
            pe.wait_ge(s_one, 1)
            pe.wait_ge(s_add["u"], 2 * NSTAGE)
            for c in range(4):
                last = nc.tensor.matmul(p1[:, c:c + 1], row["u"][NSTAGE % 2][0:1, 1, c * 128:(c + 1) * 128], ones[:],
                                        start=True, stop=True)
            last.then_inc(s_t, 1)
            pe.wait_ge(s_add["d"], NSTAGE)
            for c in range(4):
                last = nc.tensor.transpose(p2[:, c * 128:(c + 1) * 128], row["d"][NSTAGE % 2][:, 0, c * 128:(c + 1) * 128], ident[:])
            last.then_inc(s_t, 1)

        @block.scalar
        def _(act):
            act.wait_ge(s_t, 2)
            nc.scalar.copy(w2[:], p2[:].rearrange("p (c d) -> p c d", c=4)).then_inc(s_b2, 1)


def butterfly_ffn(nc, sem, n, x_all, ident, A):
    G = 4
    C = HID // 128
    with ExitStack() as ctx:
        def sb(name, shape, dt=F32):
            return ctx.enter_context(nc.sbuf_tensor(name, shape, dt))

        def bank(name):
            return ctx.enter_context(nc.psum_tensor(name, [128, 512], F32))

        w1, b1 = sb("f_w1", [D, HID]), sb("f_b1", [128, C])
        w2, b2 = sb("f_w2", [128, C, D]), sb("f_b2", [128, D])
        butterfly_weights(nc, sem, ident, A, w1, b1, w2, b2)

        xs = [sb(f"f_xs{k}", [S, G, D]) for k in range(2)]
        xT = [sb(f"f_xT{k}", [D, G * S]) for k in range(2)]
        g = [sb(f"f_g{k}", [128, C, G * S]) for k in range(2)]
        y, y2 = ([sb(f"f_{m}{k}", [S, G, D]) for k in range(2)] for m in ("y", "z"))
        norm = norm_parts(sb, sem, "f", G)
        pX, pY = bank("f_pX"), bank("f_pY")
        pH = [bank(f"f_pH{k}") for k in range(2)]
        s_x = [sem(f"f_loaded{k}") for k in range(2)]
        s_xp, s_xT, s_h, s_g, s_yp, s_y, s_y2 = (sem(f"f_{k}") for k in (
            "xT_in_psum", "xT_ready", "hidden", "gelu", "out_in_psum", "y_ready", "y2_ready"))
        block = ctx.enter_context(nc.Block())
        m = n // G

        @block.sync
        def _(sp):
            def body(i, u, on):
                par = u % 2
                need(sp, s_xp, i - 1)
                sp.dma_start(xs[par][:], x_all[:, bass.ds(i * G, G), :]).then_inc(s_x[par], 16)
            rounds(sp, m, 0, body)

        @block.tensor
        def _(pe):
            def body(i, u, on):
                par = u % 2
                q = 1 - par
                if on(0):
                    need(pe, s_x[par], landed(i, par))
                    need(pe, s_xT, i)
                    for k in range(G):
                        last = nc.tensor.transpose(pX[:, k * S:(k + 1) * S], xs[par][:, k, :], ident[:])
                    last.then_inc(s_xp, 1)
                if on(1):
                    t = i - 1
                    need(pe, s_xT, t + 1)
                    for c in range(C):
                        need(pe, s_g, C * t + c - 1)
                        nc.tensor.matmul(pH[c % 2][:], w1[:, c * 128:(c + 1) * 128], xT[q][:], start=True, stop=True).then_inc(s_h, 1)
                if on(2):
                    t = i - 2
                    need(pe, s_g, C * (t + 1))
                    need(pe, s_y, t)
                    for k in range(G):
                        for c in range(C):
                            last = nc.tensor.matmul(pY[:, k * D:(k + 1) * D], g[par][:, c, k * S:(k + 1) * S], w2[:, c, :],
                                                    start=(c == 0), stop=(c == C - 1))
                    last.then_inc(s_yp, 1)
            rounds(pe, m, 2, body)

        @block.scalar
        def _(act):
            def body(i, u, on):
                par = u % 2
                q = 1 - par
                if on(0):
                    need(act, s_xp, i + 1)
                    need(act, s_h, C * (i - 1))
                    nc.scalar.copy(xT[par][:], pX[:]).then_inc(s_xT, 1)
                if on(1):
                    t = i - 1
                    need(act, s_yp, t - 1)
                    for c in range(C):
                        need(act, s_h, C * t + c + 1)
                        nc.scalar.activation(g[q][:, c, :], pH[c % 2][:], ACT.Gelu, bias=b1[:, c:c + 1]).then_inc(s_g, 1)
            rounds(act, m, 1, body)

        @block.vector
        def _(dve):
            def body(i, u, on):
                par = u % 2
                q = 1 - par
                if on(3):
                    t = i - 3
                    norm_apply(nc, dve, norm, t, q, x_all[:, bass.ds(t * G, G), :], y2[q][:])
                if on(2):
                    t = i - 2
                    need(dve, s_yp, t + 1)
                    need(dve, s_y2, t - 1)
                    nc.vector.tensor_tensor(y[par][:], pY[:].rearrange("p (g d) -> p g d", g=G), x_all[:, bass.ds(t * G, G), :],
                                            ALU.add).then_inc(s_y, 1)
                    need(dve, s_y, t + 1)
                    need(dve, norm["normed"], G * (t - 1))
                    nc.vector.tensor_tensor(y2[par][:], y[par][:], spread(b2[:], G, 1), ALU.add).then_inc(s_y2, 1)
                    need(dve, s_y2, t + 1)
                    norm_measure(nc, dve, norm, t, par, y2[par][:])
            rounds(dve, m, 3, body)

        @block.gpsimd
        def _(pool):
            norm_start(nc, pool, norm)

            def body(i, u, on):
                if on(2):
                    norm_root(nc, pool, norm, i - 2, u % 2)
            rounds(pool, m, 2, body)


def self_attention_1(nc, sem, n, x_all, ident, A):
    HQ = 4
    SCALE = float(DQ) ** -0.5
    with ExitStack() as ctx:
        def sb(name, shape, dt=F32):
            return ctx.enter_context(nc.sbuf_tensor(name, shape, dt))

        def bank(name):
            return ctx.enter_context(nc.psum_tensor(name, [128, 512], F32))

        wqk = sb("s_wqk", [DQ, 2, H, D])
        wa = sb("s_wa", [D, H, D])
        wv = sb("s_wv", [D, H * DQ])
        wo = sb("s_wo", [128, 8, D])
        hide = sb("s_hide", [S, S])
        hide_b, ident_b = sb("s_hide_b", [S, S], BF16), sb("s_ident_b", [128, 128], BF16)
        xs = [sb(f"s_xs{k}", [S, D]) for k in range(2)]
        xT = [sb(f"s_xT{k}", [D, S]) for k in range(2)]
        tT = [sb(f"s_tT{k}", [D, HQ * S]) for k in range(2)]
        v = [sb(f"s_v{k}", [S, H * DQ]) for k in range(2)]
        mx, nm = ([sb(f"s_{m}{k}", [S, HQ]) for k in range(2)] for m in ("mx", "nm"))
        den, rden = ([sb(f"s_{m}{k}", [S, HQ]) for k in range(4)] for m in ("den", "rden"))
        p = [sb(f"s_p{k}", [S, HQ * S]) for k in range(4)]
        pn = [sb(f"s_pn{k}", [S, HQ * S]) for k in range(2)]
        pT = [sb(f"s_pT{k}", [S, HQ * S]) for k in range(2)]
        yT = [sb(f"s_yT{k}", [128, 8, S]) for k in range(2)]
        y = [sb(f"s_y{k}", [S, 1, D]) for k in range(2)]
        norm = norm_parts(sb, sem, "s")
        pX, pT_, pY, pO = (bank(f"s_p{k}_") for k in "XTYO")
        pP = [bank(f"s_pP{k}") for k in range(2)]
        pS = [bank(f"s_pS{k}") for k in range(2)]

        s_w, s_b, s_ab, s_wa = sem("s_weights"), sem("s_casts"), sem("s_wa_in_psum"), sem("s_wa_ready")
        s_x = [sem(f"s_loaded{k}") for k in range(2)]
        s_xp, s_xT = sem("s_xT_in_psum"), sem("s_xT_ready")
        s_tq, s_tT = sem("s_t_in_psum"), sem("s_t_ready")
        s_vp, s_v = sem("s_v_in_psum"), sem("s_v_ready")
        s_s, s_mx, s_nm, s_ex, s_rd, s_pn, s_tp, s_mix = (sem(f"s_{k}") for k in (
            "scores", "max", "negmax", "exp", "rden", "probs", "probsT_in_psum", "mixed"))
        s_pT = [sem(f"s_probsT{k}") for k in range(2)]
        s_yT, s_op, s_y = sem("s_yT_ready"), sem("s_out_in_psum"), sem("s_y_ready")

        def back(c, k):
            return (1, c - k) if c >= k else (2, c - k + 4)

        block = ctx.enter_context(nc.Block())

        @block.sync
        def _(sp):
            sp.dma_start(wqk[:, 0, :, :], A["L1_attn_w_q"].rearrange("h d c -> d h c")).then_inc(s_w, 16)
            sp.dma_start(wqk[:, 1, :, :], A["L1_attn_w_k"].rearrange("h d c -> d h c")).then_inc(s_w, 16)
            sp.dma_start(wv[:], A["s_wvT"]).then_inc(s_w, 16)
            sp.dma_start(wo[:], A["L1_attn_w_o"].rearrange("(m p) d -> p m d", p=128)).then_inc(s_w, 16)
            sp.dma_start(hide[:], A["hide"]).then_inc(s_w, 16)

            def body(i, u, on):
                par = u % 2
                need(sp, s_xp, i - 1)
                sp.dma_start(xs[par][:], x_all[:, bass.ds(i, 1), :].rearrange("s b d -> s (b d)")).then_inc(s_x[par], 16)
            rounds(sp, n, 0, body)

        @block.tensor
        def _(pe):
            pe.wait_ge(s_w, 16 * 5)
            for h in range(H):
                if h % 4 == 0 and h >= 8:
                    pe.wait_ge(s_wa, h // 4 - 1)
                last = nc.tensor.matmul(pS[h // 4 % 2][:, h % 4 * D:(h % 4 + 1) * D], wqk[:, 0, h, :], wqk[:, 1, h, :],
                                        start=True, stop=True)
                if h % 4 == 3:
                    last.then_inc(s_ab, 1)
            pe.wait_ge(s_wa, 4)
            pe.wait_ge(s_b, 2)

            def turn_queries(a, q, c):
                if c == 0:
                    need(pe, s_xT, a + 1)
                if c < 3:
                    need(pe, s_tT, 4 * a + c - (1 if c == 0 else 0))
                else:
                    need(pe, s_v, 2 * a + 2)
                for j in range(HQ):
                    last = nc.tensor.matmul(pP[c // 3][:, j * S:(j + 1) * S], wa[:, HQ * c + j, :], xT[q][:],
                                            start=True, stop=True)
                last.then_inc(s_tq, 1)

            def values(a, q, k):
                if k == 0:
                    need(pe, s_tT, 4 * a)
                else:
                    need(pe, s_v, 2 * a + 1)
                nc.tensor.matmul(pP[1][:], xT[q][:], wv[:, k * 512:(k + 1) * 512], start=True, stop=True).then_inc(s_vp, 1)

            def scores(x, par, c):
                need(pe, s_tT, 4 * x + c + 1)
                need(pe, s_ex, 4 * x + c - 1)
                nc.tensor.matmul(pS[c % 2][:], ident_b[:], spread(hide_b[:], HQ, 1), start=True, stop=True)
                for j in range(HQ):
                    last = nc.tensor.matmul(pS[c % 2][:, j * S:(j + 1) * S], tT[c % 2][:, j * S:(j + 1) * S], xT[par][:],
                                            start=False, stop=True, skip_group_check=True)
                last.then_inc(s_s, 1)

            def turn_probs(x, c):
                need(pe, s_pn, 4 * x + c + 1)
                need(pe, s_pT[1 - c % 2], 2 * x + (c + 1) // 2)
                for j in range(HQ):
                    last = nc.tensor.transpose(pT_[:, j * S:(j + 1) * S], pn[c % 2][:, j * S:(j + 1) * S], ident[:])
                last.then_inc(s_tp, 1)

            def mix(x, par, c):
                need(pe, s_pT[c % 2], 2 * x + c // 2 + 1)
                if c == 0:
                    need(pe, s_v, 2 * x + 2)
                if c % 2 == 0:
                    need(pe, s_yT, 2 * x + c // 2)
                for j in range(HQ):
                    r, m = 64 * (j % 2), (2 * c + j // 2) % 4
                    last = nc.tensor.matmul(pY[r:r + 64, m * S:(m + 1) * S], v[par][:, (HQ * c + j) * DQ:(HQ * c + j + 1) * DQ],
                                            pT[c % 2][:, j * S:(j + 1) * S], start=True, stop=True)
                last.then_inc(s_mix, 1)

            def body(i, u, on):
                par = u % 2
                q = 1 - par
                for c in range(4):
                    if on(1):
                        turn_queries(i - 1, q, c)
                    lag, cc = back(c, 1)
                    if on(lag):
                        scores(i - lag, (par + lag) % 2, cc)
                    if on(1) and c < 2:
                        values(i - 1, q, c)
                    lag, cc = back(c, 3)
                    if on(lag):
                        turn_probs(i - lag, cc)
                    if c == 0 and on(0):
                        need(pe, s_x[par], landed(i, par))
                        need(pe, s_xT, i)
                        nc.tensor.transpose(pX[:, 0:S], xs[par][:], ident[:]).then_inc(s_xp, 1)
                    if c == 1 and on(3):
                        t = i - 3
                        need(pe, s_yT, 2 * t + 2)
                        need(pe, s_y, t)
                        for m in range(8):
                            last = nc.tensor.matmul(pO[:, 0:D], yT[q][:, m, :], wo[:, m, :], start=(m == 0), stop=(m == 7))
                        last.then_inc(s_op, 1)
                    if on(2):
                        mix(i - 2, par, c)
            rounds(pe, n, 3, body)

        @block.scalar
        def _(act):
            for k in range(4):
                act.wait_ge(s_ab, k + 1)
                nc.scalar.copy(wa[:, 4 * k:4 * k + 4, :], heads(pS[k % 2][:], 4)).then_inc(s_wa, 1)

            def exps(x, c):
                need(act, s_nm, 4 * x + c + 1)
                need(act, s_pn, 4 * x + c - 3)
                need(act, s_rd, 4 * x + c - 3)
                for j in range(HQ):
                    last = nc.scalar.activation(p[c][:, j * S:(j + 1) * S], pS[c % 2][:, j * S:(j + 1) * S], ACT.Exp,
                                                bias=nm[c % 2][:, j:j + 1], scale=SCALE, accum_out=den[c][:, j:j + 1])
                last.then_inc(s_ex, 1)

            def body(i, u, on):
                par = u % 2
                q = 1 - par
                for c in range(4):
                    if c in (0, 2):
                        lag, half = (3, 1) if c == 0 else (2, 0)
                        if on(lag):
                            t = i - lag
                            need(act, s_mix, 4 * t + 2 * half + 2)
                            need(act, s_op, t - 1)
                            nc.scalar.copy(yT[(u + lag) % 2][:, 4 * half:4 * half + 4, :], heads(pY[:], 4)).then_inc(s_yT, 1)
                    lag, cc = back(c, 1)
                    if on(lag):
                        exps(i - lag, cc)
                    if on(1) and c < 2:
                        a = i - 1
                        need(act, s_vp, 2 * a + c + 1)
                        need(act, s_mix, 4 * (a - 1))
                        nc.scalar.copy(v[q][:, c * 512:(c + 1) * 512], pP[1][:]).then_inc(s_v, 1)
                    lag, cc = back(c, 3)
                    if on(lag) and cc % 2 == 1:
                        x = i - lag
                        need(act, s_tp, 4 * x + cc + 1)
                        need(act, s_mix, 4 * x + cc - 1)
                        nc.scalar.copy(pT[1][:], pT_[:]).then_inc(s_pT[1], 1)
                    if c == 1 and on(0):
                        need(act, s_xp, i + 1)
                        need(act, s_s, 4 * (i - 1))
                        nc.scalar.copy(xT[par][:], pX[:, 0:S]).then_inc(s_xT, 1)
            rounds(act, n, 3, body)

        @block.vector
        def _(dve):
            dve.wait_ge(s_w, 16 * 5)
            nc.vector.tensor_copy(hide_b[:], hide[:]).then_inc(s_b, 1)
            nc.vector.tensor_copy(ident_b[:], ident[:]).then_inc(s_b, 1)

            def body(i, u, on):
                par = u % 2
                for c in range(4):
                    lag, cc = back(c, 2)
                    if on(lag):
                        x = i - lag
                        need(dve, s_ex, 4 * x + cc + 1)
                        need(dve, s_pn, 4 * x + cc - 3)
                        nc.vector.reciprocal(rden[cc][:], den[cc][:]).then_inc(s_rd, 1)
                    if c == 0 and on(4):
                        norm_apply(nc, dve, norm, i - 4, par, x_all[:, bass.ds(i - 4, 1), :], y[par][:])
                    lag, cc = back(c, 1)
                    if on(lag):
                        x = i - lag
                        need(dve, s_s, 4 * x + cc + 1)
                        need(dve, s_nm, 4 * x + cc - 1)
                        nc.vector.tensor_reduce(mx[cc % 2][:], heads(pS[cc % 2][:], HQ), AX, ALU.max).then_inc(s_mx, 1)
                        need(dve, s_mx, 4 * x + cc + 1)
                        need(dve, s_ex, 4 * x + cc - 1)
                        nc.vector.tensor_scalar(nm[cc % 2][:], mx[cc % 2][:], -SCALE, None, ALU.mult).then_inc(s_nm, 1)
                    if on(1):
                        a = i - 1
                        need(dve, s_tq, 4 * a + c + 1)
                        need(dve, s_s, 4 * a + c - 1)
                        nc.vector.tensor_copy(tT[c % 2][:], pP[c // 3][:]).then_inc(s_tT, 1)
                    lag, cc = back(c, 3)
                    if on(lag) and cc % 2 == 0:
                        x = i - lag
                        need(dve, s_tp, 4 * x + cc + 1)
                        need(dve, s_mix, 4 * x + cc - 1)
                        nc.vector.tensor_copy(pT[0][:], pT_[:]).then_inc(s_pT[0], 1)
                    if c == 2 and on(3):
                        t = i - 3
                        need(dve, s_op, t + 1)
                        need(dve, norm["normed"], t - 1)
                        nc.vector.tensor_tensor(y[(u + 1) % 2][:, 0, :], pO[:, 0:D], x_all[:, bass.ds(t, 1), :].rearrange("s b d -> s (b d)"),
                                                ALU.add).then_inc(s_y, 1)
                        need(dve, s_y, t + 1)
                        norm_measure(nc, dve, norm, t, (u + 1) % 2, y[(u + 1) % 2][:])
            rounds(dve, n, 4, body)

        @block.gpsimd
        def _(pool):
            norm_start(nc, pool, norm)

            def body(i, u, on):
                for c in range(4):
                    lag, cc = back(c, 2)
                    if on(lag):
                        x = i - lag
                        need(pool, s_rd, 4 * x + cc + 1)
                        need(pool, s_tp, 4 * x + cc - 1)
                        nc.gpsimd.tensor_tensor(heads(pn[cc % 2][:], HQ), heads(p[cc][:], HQ), spread(rden[cc][:], S, 2),
                                                ALU.mult).then_inc(s_pn, 1)
                    if c == 2 and on(3):
                        norm_root(nc, pool, norm, i - 3, (u + 1) % 2)
            rounds(pool, n, 3, body)


def additive_attention_1(nc, sem, n, x_all, ident, A):
    TC = 16
    CH = [(t, min(TC, T2 - t)) for t in range(0, T2, TC)]
    NCH = len(CH)
    ON_POOL = (1, 3)
    NB = T2P // 4
    R = NB // 4
    with ExitStack() as ctx:
        def sb(name, shape, dt=F32):
            return ctx.enter_context(nc.sbuf_tensor(name, shape, dt))

        def pair(name, shape, dt=F32):
            return [sb(f"{name}{k}", shape, dt) for k in range(2)]

        def bank(name):
            return ctx.enter_context(nc.psum_tensor(name, [128, 512], F32))

        wt, wf = sb("t_ws", [D, D]), sb("t_w", [D, D])
        wc = sb("t_wc", [D, 2, D])
        wcol = sb("t_wcol", [D, 2, 1])
        wz = sb("t_wz", [D, 63])
        wv = sb("t_wv", [D, 1])
        b = sb("t_b", [D, 1])
        bc = sb("t_bc", [S, 2])
        xs, cs, qm = pair("t_xs", [S, D]), pair("t_cs", [T2, D]), pair("t_qm", [S, T2P], I32)
        xT, cT = pair("t_xT", [D, S]), pair("t_cT", [D, 128])
        feat, txt = pair("t_feat", [D, S]), pair("t_txt", [D, T2P])
        cw = [sb(f"t_cw{k}", [S, 2, 128]) for k in range(4)]
        args = [sb(f"t_args{k}", [D, TC, S]) for k in range(4)]
        th = [sb(f"t_th{k}", [D, TC, S]) for k in range(2)]
        rho_s = sb("t_rho_s", [128, 4, S])
        mk = [sb(f"t_mk{k}", [S, T2P]) for k in range(4)]
        rho = pair("t_rho", [S, T2P])
        nmx, den, rden, acc, g = (pair(f"t_{k}", [S, w]) for k, w in (("nmx", 1), ("den", 1), ("rden", 1), ("acc", 2), ("g", 2)))
        ex, scr = pair("t_ex", [S, T2]), pair("t_scr", [S, 2, T2])
        y, y2 = pair("t_y", [S, 1, D]), pair("t_z", [S, 1, D])
        norm = norm_parts(sb, sem, "t")
        pX, pG, pR2 = (bank(f"t_p{k}") for k in "XGT")
        pF = [bank(f"t_pF{k}") for k in range(2)]
        pR = [bank(f"t_pR{k}") for k in range(2)]

        s_w, s_set, s_zero = sem("t_weights"), sem("t_set"), sem("t_zeroed")
        s_x = [sem(f"t_loaded{k}") for k in range(2)]
        s_xp, s_xT, s_cT, s_fg = (sem(f"t_{k}") for k in ("xcT_in_psum", "xT", "cT", "proj_in_psum"))
        s_feat, s_txt, s_cw = (sem(f"t_{k}_ready") for k in ("feat", "txt", "cw"))
        s_sumd, s_sump = sem("t_sums_vector"), sem("t_sums_gpsimd")
        s_th, s_red = sem("t_tanh"), sem("t_reduced")
        s_rs, s_rt, s_m1, s_mk, s_rho, s_mx, s_ex = (sem(f"t_{k}") for k in (
            "rho_copied", "rho_turned", "unmasked", "mask_ready", "rho_ready", "negmax", "exp"))
        s_rd, s_acc, s_g, s_y, s_y2 = (sem(f"t_{k}") for k in ("rden", "averaged", "gates", "y_ready", "y2_ready"))
        m1 = pair("t_m1", [S, T2P])

        def chunk_buffer(k, par):
            return 2 + k // 2 if k in ON_POOL else (k // 2 + par) % 2

        def sums_ready(eng, i, k):
            if k in ON_POOL:
                need(eng, s_sump, 2 * i + ON_POOL.index(k) + 1)
            else:
                need(eng, s_sumd, 3 * i + k // 2 + 1)

        block = ctx.enter_context(nc.Block())

        @block.sync
        def _(sp):
            for dst, src in ((wt[:], A["L1_xattn_Ws"]), (wf[:], A["L1_xattn_W"]), (wv[:], A["L1_xattn_w"]),
                             (b[:], A["L1_xattn_b"].rearrange("o d -> d o")),
                             (wcol[:, 0, :], A["L1_xattn_Wcw"].rearrange("o d -> d o")),
                             (wcol[:, 1, :], A["L1_xattn_Wcb"].rearrange("o d -> d o")),
                             (bc[:, 0:1], A["L1_xattn_bcw"].unsqueeze(0).broadcast_to([S, 1])),
                             (bc[:, 1:2], A["L1_xattn_bcb"].unsqueeze(0).broadcast_to([S, 1]))):
                sp.dma_start(dst, src).then_inc(s_w, 16)

            def body(i, u, on):
                par = u % 2
                need(sp, s_xp, i - 1)
                need(sp, s_m1, i - 1)
                sp.dma_start(xs[par][:], x_all[:, bass.ds(i, 1), :].rearrange("s b d -> s (b d)")).then_inc(s_x[par], 16)
                sp.dma_start(cs[par][:], A["ctx_1024"][bass.ds(i, 1), :, :].rearrange("b t d -> (b t) d")).then_inc(s_x[par], 16)
                sp.dma_start(qm[par][:, 0:T2], A["mask_BxS2_ik0"][bass.ds(i, 1), :].broadcast_to([S, T2])).then_inc(s_x[par], 16)
            rounds(sp, n, 0, body, 8)

        @block.tensor
        def _(pe):
            pe.wait_ge(s_w, 16 * 8)
            pe.wait_ge(s_set, 5)

            def reduce(a, q, k):
                need(pe, s_th, NCH * a + k + 1)
                if k == 0:
                    need(pe, s_rs, a - 1)
                t0, nt = CH[k]
                for b0 in range(0, nt, 4):
                    blk = (t0 + b0) // 4
                    j, r = blk % 4, blk // 4
                    w = min(4, nt - b0)
                    last = nc.tensor.matmul(pR[q][32 * j:32 * j + 32, 0:w * S], wz[:, 31 - r:63 - r],
                                            th[(k + q) % 2][:, b0:b0 + w, :].rearrange("p t f -> p (t f)"),
                                            start=(r == 0), stop=(r == R - 1), skip_group_check=True)
                last.then_inc(s_red, 1)

            def body(i, u, on):
                par = u % 2
                q = 1 - par
                if on(0):
                    need(pe, s_x[par], landed(i, par) * 3)
                    need(pe, s_cT, i)
                    nc.tensor.transpose(pX[:, 0:S], xs[par][:], ident[:])
                    nc.tensor.transpose(pX[:, S:S + T2], cs[par][:], ident[0:T2, 0:T2]).then_inc(s_xp, 1)
                if on(2):
                    reduce(i - 2, par, 0)
                if on(3):
                    t = i - 3
                    need(pe, s_rs, t + 1)
                    need(pe, s_rho, t)
                    for k in range(4):
                        last = nc.tensor.transpose(pR2[:, k * S:(k + 1) * S], rho_s[:, k, :], ident[:])
                    last.then_inc(s_rt, 1)
                if on(2):
                    reduce(i - 2, par, 1)
                if on(1):
                    t = i - 1
                    need(pe, s_cT, t + 1)
                    need(pe, s_sumd, 3 * (t - 1))
                    need(pe, s_cw, t)
                    nc.tensor.matmul(pF[q][:, 0:S], wf[:], xT[q][:], start=True, stop=True)
                    nc.tensor.matmul(pG[:, 0:128], wt[:], cT[q][:], start=True, stop=True)
                    for k in range(2):
                        last = nc.tensor.matmul(pG[:, 128 * (k + 1):128 * (k + 2)], wc[:, k, :], cT[q][:], start=True, stop=True)
                    last.then_inc(s_fg, 1)
                if on(2):
                    for k in range(2, NCH):
                        reduce(i - 2, par, k)
            rounds(pe, n, 3, body, 8)

        @block.scalar
        def _(act):
            act.wait_ge(s_w, 16 * 8)
            act.wait_ge(s_set, 5)

            def tanh(a, q, k):
                sums_ready(act, a, k)
                need(act, s_red, NCH * a + k - 1)
                nt = CH[k][1]
                nc.scalar.activation(th[(k + q) % 2][:, 0:nt, :], args[chunk_buffer(k, q)][:, 0:nt, :], ACT.Tanh).then_inc(s_th, 1)

            def body(i, u, on):
                par = u % 2
                q = 1 - par
                if on(2):
                    tanh(i - 2, par, 0)
                if on(0):
                    need(act, s_xp, i + 1)
                    need(act, s_fg, i - 1)
                    nc.scalar.copy(xT[par][:], pX[:, 0:S]).then_inc(s_xT, 1)
                    nc.scalar.copy(cT[par][:, 0:T2], pX[:, S:S + T2]).then_inc(s_cT, 1)
                if on(2):
                    tanh(i - 2, par, 1)
                if on(4):
                    t = i - 4
                    need(act, s_acc, 2 * t + 2)
                    need(act, s_rd, t + 1)
                    need(act, s_y, t - 1)
                    for k in range(2):
                        last = nc.scalar.activation(g[par][:, k:k + 1], acc[par][:, k:k + 1], ACT.Tanh, bias=bc[:, k:k + 1],
                                                    scale=rden[par][:])
                    last.then_inc(s_g, 1)
                if on(2):
                    tanh(i - 2, par, 2)
                if on(1):
                    t = i - 1
                    need(act, s_fg, t + 1)
                    need(act, s_sump, 2 * (t - 1))
                    nc.scalar.copy(feat[q][:], pF[q][:, 0:S]).then_inc(s_feat, 1)
                    need(act, s_sumd, 3 * (t - 1))
                    nc.scalar.activation(txt[q][:], pG[:, 0:T2P], ACT.Identity, bias=b[:]).then_inc(s_txt, 1)
                    need(act, s_acc, 2 * (t - 3))
                    nc.scalar.copy(cw[(u + 3) % 4][:], pG[:, 128:384].rearrange("p (k t) -> p k t", k=2)).then_inc(s_cw, 1)
                if on(2):
                    tanh(i - 2, par, 3)
                if on(3):
                    t = i - 3
                    need(act, s_mx, t + 1)
                    need(act, s_acc, 2 * (t - 1))
                    need(act, s_rd, t - 1)
                    nc.scalar.activation(ex[q][:], rho[q][:, 0:T2], ACT.Exp, bias=nmx[q][:], accum_out=den[q][:]).then_inc(s_ex, 1)
                if on(2):
                    tanh(i - 2, par, 4)
            rounds(act, n, 4, body, 8)

        @block.vector
        def _(dve):
            dve.wait_ge(s_w, 16 * 8)
            for k in range(2):
                nc.vector.tensor_copy(wc[:, k, :], wcol[:, k, :].broadcast_to([D, D])).then_inc(s_set, 1)
            dve.wait_ge(s_set, 5)

            def sums(a, q, k):
                t0, nt = CH[k]
                need(dve, s_feat, a + 1)
                need(dve, s_txt, a + 1)
                need(dve, s_th, NCH * a + {0: -2, 2: 0, 4: 1}[k])
                nc.vector.tensor_tensor(args[chunk_buffer(k, q)][:, 0:nt, :], spread(pF[q][:, 0:S], nt, 1),
                                        spread(txt[q][:, t0:t0 + nt], S, 2), ALU.add).then_inc(s_sumd, 1)

            def body(i, u, on):
                par = u % 2
                q = 1 - par
                if on(5):
                    norm_apply(nc, dve, norm, i - 5, q, x_all[:, bass.ds(i - 5, 1), :], y2[q][:])
                if on(2):
                    sums(i - 2, par, 0)
                if on(3):
                    t = i - 3
                    need(dve, s_red, NCH * (t + 1))
                    need(dve, s_rt, t)
                    nc.vector.tensor_copy(rho_s[:], heads(pR[q][:], 4)).then_inc(s_rs, 1)
                if on(4):
                    t = i - 4
                    need(dve, s_ex, t + 1)
                    need(dve, s_g, t - 1)
                    nc.vector.reciprocal(rden[par][:], den[par][:]).then_inc(s_rd, 1)
                    for k in range(2):
                        nc.vector.tensor_tensor_reduce(scr[par][:, k, :], ex[par][:], cw[u][:, k, 0:T2], 1.0, 0.0, ALU.mult,
                                                       ALU.add, acc[par][:, k:k + 1]).then_inc(s_acc, 1)
                if on(2):
                    sums(i - 2, par, 2)
                if on(1):
                    t = i - 1
                    need(dve, s_x[q], landed(t, q) * 3)
                    need(dve, s_mk, t - 1)
                    nc.vector.tensor_scalar(m1[q][:, 0:T2], qm[q][:, 0:T2], -1.0, 1.0, ALU.mult, ALU.add).then_inc(s_m1, 1)
                    need(dve, s_m1, t + 1)
                    need(dve, s_rho, t - 3)
                    nc.vector.tensor_scalar(mk[(u + 3) % 4][:, 0:T2], m1[q][:, 0:T2], HIDDEN, None, ALU.mult).then_inc(s_mk, 1)
                if on(3):
                    t = i - 3
                    need(dve, s_rt, t + 1)
                    need(dve, s_mk, t + 1)
                    need(dve, s_ex, t - 1)
                    shape = "p (r j t) -> p r j t"
                    turned = pR2[:].rearrange("p (t j r) -> p r j t", t=4, j=4)[:, 0:R]
                    nc.vector.tensor_tensor(rho[q][:].rearrange(shape, r=R, j=4), turned,
                                            mk[(u + 1) % 4][:].rearrange(shape, r=R, j=4), ALU.add).then_inc(s_rho, 1)
                    need(dve, s_rho, t + 1)
                    nc.vector.tensor_reduce(nmx[q][:], rho[q][:, 0:T2], AX, ALU.max, negate=True).then_inc(s_mx, 1)
                if on(2):
                    sums(i - 2, par, 4)
                if on(4):
                    t = i - 4
                    rows = x_all[:, bass.ds(t, 1), :]
                    need(dve, s_g, t + 1)
                    need(dve, s_y2, t - 1)
                    nc.vector.tensor_scalar(y[par][:], rows, g[par][:, 0:1], g[par][:, 1:2], ALU.mult, ALU.add).then_inc(s_y, 1)
                    need(dve, s_y, t + 1)
                    need(dve, norm["normed"], t - 1)
                    nc.vector.tensor_tensor(y2[par][:], y[par][:], rows, ALU.add).then_inc(s_y2, 1)
                    need(dve, s_y2, t + 1)
                    norm_measure(nc, dve, norm, t, par, y2[par][:])
            rounds(dve, n, 5, body, 8)

        @block.gpsimd
        def _(pool):
            norm_start(nc, pool, norm)
            nc.gpsimd.memset(wz[:], 0.0).then_inc(s_zero, 1)
            nc.gpsimd.memset(cT[0][:], 0.0).then_inc(s_set, 1)
            nc.gpsimd.memset(cT[1][:], 0.0).then_inc(s_set, 1)
            for k in range(4):
                nc.gpsimd.memset(mk[k][:], 0.0).then_inc(s_zero, 1)
            pool.wait_ge(s_zero, 5)
            pool.wait_ge(s_w, 16 * 8)
            nc.gpsimd.tensor_copy(wz[:, 31:32], wv[:]).then_inc(s_set, 1)

            def body(i, u, on):
                par = u % 2
                if on(2):
                    a = i - 2
                    for k in ON_POOL:
                        t0, nt = CH[k]
                        need(pool, s_feat, a + 1)
                        need(pool, s_txt, a + 1)
                        need(pool, s_th, NCH * (a - 1) + k + 1)
                        nc.gpsimd.tensor_tensor(args[chunk_buffer(k, par)][:, 0:nt, :], spread(feat[par][:], nt, 1),
                                                spread(txt[par][:, t0:t0 + nt], S, 2), ALU.add).then_inc(s_sump, 1)
                if on(4):
                    norm_root(nc, pool, norm, i - 4, par)
            rounds(pool, n, 4, body, 8)


def experts_ffn_1(nc, sem, n, x_all, ident, A, out):
    G = 4
    CH = [(c, min(128, FE - c)) for c in range(0, FE, 128)]
    NC = len(CH)
    with ExitStack() as ctx:
        def sb(name, shape, dt=F32):
            return ctx.enter_context(nc.sbuf_tensor(name, shape, dt))

        def pair(name, shape, dt=F32):
            return [sb(f"{name}{k}", shape, dt) for k in range(2)]

        def bank(name):
            return ctx.enter_context(nc.psum_tensor(name, [128, 512], F32))

        wg, wu = sb("e_wg", [D, E, FE]), sb("e_wu", [D, E, FE])
        wd = sb("e_wd", [128, E, NC, D])
        wr, br = sb("e_wr", [D, E]), sb("e_br", [S, E])
        number = sb("e_number", [S, E])
        xs, xT = pair("e_xs", [S, G, D]), pair("e_xT", [D, G * S])
        logit, top, topi, topf = (pair(f"e_{k}", [S, G, 8], dt) for k, dt in (("logit", F32), ("top", F32), ("topi", U32), ("topf", F32)))
        gap, tg = pair("e_gap", [S, G]), pair("e_tg", [S, G])
        pw = pair("e_pw", [S, 2, G])
        c1, c2, w1, w2, cb = (pair(f"e_{k}", [S, G, E]) for k in ("c1", "c2", "w1", "w2", "cb"))
        sg, h = [sb(f"e_sg{k}", [128, G * S]) for k in range(2)], [sb(f"e_h{k}", [128, G * S]) for k in range(6)]
        acc = pair("e_acc", [S, G, D])
        res = pair("e_res", [S, G, D])
        norm = norm_parts(sb, sem, "e", G)
        pX = bank("e_pX")
        pY = bank("e_pY")
        pG = [bank(f"e_pG{k}") for k in range(3)]
        pU = [bank(f"e_pU{k}") for k in range(3)]

        s_w = sem("e_weights")
        s_x = [sem(f"e_loaded{k}") for k in range(2)]
        s_xp, s_xT, s_lp, s_lg, s_top, s_topi, s_topf, s_gap, s_tg, s_pw, s_c1, s_c2, s_cb = (sem(f"e_{k}") for k in (
            "xT_in_psum", "xT_ready", "logits_in_psum", "logits", "top", "top_number", "top_number_f", "gap", "tanh_gap",
            "pair_weights", "first", "second", "combine"))
        s_eq = sem("e_chosen")
        s_gp, s_up, s_sg, s_h = (sem(f"e_{k}") for k in ("gate_in_psum", "up_in_psum", "silu", "hidden"))
        s_yp, s_acc = sem("e_expert_in_psum"), sem("e_added")
        s_st = [sem(f"e_stored{k}") for k in range(2)]
        block = ctx.enter_context(nc.Block())
        m = n // G
        NCE = NC * E

        @block.sync
        def _(sp):
            sp.dma_start(wr[:], A["L1_ffn_Ws"]).then_inc(s_w, 16)
            sp.dma_start(br[:], A["L1_ffn_bs"].unsqueeze(0).broadcast_to([S, E])).then_inc(s_w, 16)
            sp.dma_start(number[:], A["number"].unsqueeze(0).broadcast_to([S, E])).then_inc(s_w, 16)
            for e in range(0, E, 4):
                sp.dma_start(wg[:, e:e + 4, :], A["L1_ffn_Wg"][e:e + 4].rearrange("e d f -> d e f")).then_inc(s_w, 16)
                sp.dma_start(wu[:, e:e + 4, :], A["L1_ffn_Wu"][e:e + 4].rearrange("e d f -> d e f")).then_inc(s_w, 16)
            for c, (f0, nf) in enumerate(CH):
                sp.dma_start(wd[0:nf, :, c, :], A["L1_ffn_Wd"][:, f0:f0 + nf, :].rearrange("e f d -> f e d")).then_inc(s_w, 16)

            def body(i, u, on):
                par = u % 2
                if on(0):
                    need(sp, s_xp, i - 1)
                    sp.dma_start(xs[par][:], x_all[:, bass.ds(i * G, G), :]).then_inc(s_x[par], 16)
                if on(2):
                    t = i - 2
                    need(sp, norm["normed"], G * (t + 1))
                    sp.dma_start(out[bass.ds(t * G, G), :, :].rearrange("b s d -> s b d"), res[par][:]).then_inc(s_st[par], 16)
            rounds(sp, m, 2, body)
            for k in range(2):
                sp.wait_ge(s_st[k], 16 * (m // 2))

        @block.tensor
        def _(pe):
            pe.wait_ge(s_w, 16 * 10)

            def body(i, u, on):
                par = u % 2
                q = 1 - par

                def down(t, e):
                    need(pe, s_h, NCE * t + NC * (e + 1))
                    need(pe, s_acc, G * (E * t + e))
                    for k in range(G):
                        for c, (f0, nf) in enumerate(CH):
                            last = nc.tensor.matmul(pY[:, k * D:(k + 1) * D], h[(NC * e + c) % 6][0:nf, k * S:(k + 1) * S],
                                                    wd[0:nf, e, c, :], start=(c == 0), stop=(c == NC - 1))
                    last.then_inc(s_yp, 1)

                def front(k):
                    if k == 0:
                        need(pe, s_x[par], landed(i, par))
                        need(pe, s_lg, i)
                        for j in range(G):
                            last = nc.tensor.transpose(pX[:, j * S:(j + 1) * S], xs[par][:, j, :], ident[:])
                        last.then_inc(s_xp, 1)
                    else:
                        need(pe, s_xT, i + 1)
                        for j in range(G):
                            last = nc.tensor.matmul(pX[:, j * E:(j + 1) * E], xT[par][:, j * S:(j + 1) * S], wr[:], start=True, stop=True)
                        last.then_inc(s_lp, 1)

                for e in range(E):
                    if on(1):
                        t = i - 1
                        if e == 0:
                            need(pe, s_xT, t + 1)
                        for c, (f0, nf) in enumerate(CH):
                            k = NC * e + c
                            need(pe, s_sg, NCE * t + k - 2)
                            nc.tensor.matmul(pG[c][0:nf, :], wg[:, e, f0:f0 + nf], xT[q][:], start=True, stop=True).then_inc(s_gp, 1)
                            need(pe, s_h, NCE * t + k - 2)
                            nc.tensor.matmul(pU[c][0:nf, :], wu[:, e, f0:f0 + nf], xT[q][:], start=True, stop=True).then_inc(s_up, 1)
                        if e >= 1:
                            down(t, e - 1)
                    if on(0) and e in (2, 4):
                        front(e // 2 - 1)
                if on(1):
                    down(i - 1, E - 1)
            rounds(pe, m, 1, body)

        @block.scalar
        def _(act):
            def body(i, u, on):
                par = u % 2
                for e in range(E):
                    if on(1):
                        t = i - 1
                        for c, (f0, nf) in enumerate(CH):
                            k = NC * e + c
                            need(act, s_gp, NCE * t + k + 1)
                            need(act, s_h, NCE * t + k - 1)
                            nc.scalar.activation(sg[k % 2][0:nf, :], pG[c][0:nf, :], ACT.Silu).then_inc(s_sg, 1)
                    if on(0) and e == 2:
                        need(act, s_xp, i + 1)
                        need(act, s_up, NCE * (i - 1))
                        need(act, s_lp, i - 1)
                        nc.scalar.copy(xT[par][:], pX[:]).then_inc(s_xT, 1)
                    if on(0) and e == 6:
                        need(act, s_gap, i + 1)
                        need(act, s_pw, 2 * (i - 1))
                        nc.scalar.activation(tg[par][:], gap[par][:], ACT.Tanh, scale=0.5).then_inc(s_tg, 1)
            rounds(act, m, 1, body)

        @block.vector
        def _(dve):
            dve.wait_ge(s_w, 16 * 10)

            def combine(i, par, k):
                if k == 0:
                    need(dve, s_lp, i + 1)
                    need(dve, s_topi, G * (i - 1))
                    nc.vector.tensor_tensor(logit[par][:], pX[:, 0:G * E].rearrange("p (g e) -> p g e", g=G), spread(br[:], G, 1),
                                            ALU.add).then_inc(s_lg, 1)
                    apart(dve, s_w, 16 * 10, ((s_lg, i + 1), (s_gap, i - 1)))
                    for j in range(G):
                        nc.vector.max(top[par][:, j, :], logit[par][:, j, :]).then_inc(s_top, 1)
                    apart(dve, s_w, 16 * 10, ((s_top, G * (i + 1)), (s_topf, i - 1)))
                    for j in range(G):
                        nc.vector.max_index(topi[par][:, j, :], top[par][:, j, :], logit[par][:, j, :]).then_inc(s_topi, 1)
                    need(dve, s_tg, i - 1)
                    nc.vector.tensor_tensor(gap[par][:], top[par][:, :, 0], top[par][:, :, 1], ALU.subtract).then_inc(s_gap, 1)
                    need(dve, s_topi, G * (i + 1))
                    need(dve, s_c2, i - 1)
                    nc.vector.tensor_copy(topf[par][:], topi[par][:]).then_inc(s_topf, 1)
                else:
                    need(dve, s_tg, i + 1)
                    need(dve, s_c2, i - 1)
                    nc.vector.tensor_scalar(pw[par][:, 0, :], tg[par][:], 0.5, 0.5, ALU.mult, ALU.add).then_inc(s_pw, 1)
                    nc.vector.tensor_scalar(pw[par][:, 1, :], tg[par][:], -0.5, 0.5, ALU.mult, ALU.add).then_inc(s_pw, 1)
                    need(dve, s_topf, i + 1)
                    need(dve, s_cb, i - 1)
                    nc.vector.tensor_tensor(c1[par][:], spread(number[:], G, 1), topf[par][:, :, 0:1].broadcast_to([S, G, E]),
                                            ALU.is_equal).then_inc(s_eq, 1)
                    nc.vector.tensor_tensor(c2[par][:], spread(number[:], G, 1), topf[par][:, :, 1:2].broadcast_to([S, G, E]),
                                            ALU.is_equal).then_inc(s_eq, 1)
                    need(dve, s_eq, 2 * (i + 1))
                    need(dve, s_pw, 2 * (i + 1))
                    nc.vector.tensor_tensor(w1[par][:], c1[par][:], spread(pw[par][:, 0, :], E, 2), ALU.mult).then_inc(s_c1, 1)
                    nc.vector.tensor_tensor(w2[par][:], c2[par][:], spread(pw[par][:, 1, :], E, 2), ALU.mult).then_inc(s_c2, 1)
                    need(dve, s_c1, i + 1)
                    need(dve, s_c2, i + 1)
                    need(dve, s_acc, G * E * (i - 1))
                    nc.vector.tensor_tensor(cb[par][:], w1[par][:], w2[par][:], ALU.add).then_inc(s_cb, 1)

            def body(i, u, on):
                par = u % 2
                q = 1 - par

                def add(t, e):
                    need(dve, s_yp, E * t + e + 1)
                    if e == 0:
                        need(dve, s_cb, t + 1)
                        need(dve, norm["normed"], G * (t - 1))
                    else:
                        need(dve, s_acc, G * (E * t + e))
                    for k in range(G):
                        before = x_all[:, bass.ds(t * G + k, 1), :].rearrange("s b d -> s (b d)") if e == 0 else acc[q][:, k, :]
                        nc.vector.scalar_tensor_tensor(acc[q][:, k, :], pY[:, k * D:(k + 1) * D], cb[q][:, k, e:e + 1], before,
                                                       ALU.mult, ALU.add).then_inc(s_acc, 1)

                for e in range(E):
                    if on(1):
                        t = i - 1
                        for c, (f0, nf) in enumerate(CH):
                            k = NC * e + c
                            need(dve, s_sg, NCE * t + k + 1)
                            need(dve, s_up, NCE * t + k + 1)
                            need(dve, s_yp, E * t + e - 1)
                            nc.vector.tensor_tensor(h[k % 6][0:nf, :], sg[k % 2][0:nf, :], pU[c][0:nf, :], ALU.mult).then_inc(s_h, 1)
                        if e >= 1:
                            add(t, e - 1)
                    if on(2) and e == 0:
                        t = i - 2
                        need(dve, s_st[par], 8 * t - 8 * par)
                        norm_apply(nc, dve, norm, t, par, res[par][:], acc[par][:])
                    if on(0) and e == 5:
                        combine(i, par, 0)
                    if on(0) and e == 7:
                        combine(i, par, 1)
                if on(1):
                    add(i - 1, E - 1)
                    need(dve, s_acc, G * E * i)
                    norm_measure(nc, dve, norm, i - 1, q, acc[q][:])
            rounds(dve, m, 2, body)

        @block.gpsimd
        def _(pool):
            norm_start(nc, pool, norm)

            def body(i, u, on):
                if on(1):
                    norm_root(nc, pool, norm, i - 1, 1 - u % 2)
            rounds(pool, m, 1, body)


def decoder_kernel(nc, A, out):
    n = A["x"].shape[0]
    with ExitStack() as ctx:
        x_all = ctx.enter_context(nc.sbuf_tensor("x_all", [S, n, D], F32))
        ident = ctx.enter_context(nc.sbuf_tensor("ident", [128, 128], F32))
        for sublayer, more in ((self_attention_0, ()), (cross_attention_0, ()), (butterfly_ffn, ()), (self_attention_1, ()),
                               (additive_attention_1, ()), (experts_ffn_1, (out,))):
            with nc.cleanup_on_exit():
                sublayer(nc, nc.alloc_semaphore, n, x_all, ident, A, *more)


def shape_tables():
    import numpy as np

    c = {"ident": np.eye(128, dtype=np.float32), "number": np.arange(E, dtype=np.float32)}
    q, r = np.arange(S), np.arange(128)
    c["above"] = (q[None, :] > q[:, None] + 1).astype(np.uint32)
    c["beside"] = (q[None, :] == q[:, None] + 1).astype(np.uint32)
    c["hide"] = np.where(q[None, :] > q[:, None], np.float32(HIDDEN), np.float32(0))
    c["a_hmask"] = (((r // DK) % 8)[:, None] == np.arange(8)[None]).astype(np.float32)
    c["a_hsum"] = ((r // DK)[:, None] == np.arange(H)[None]).astype(np.float32)
    freq = 1.0 / 10000.0 ** (np.arange(0, DK, 2) / DK)
    turn, rpos = np.zeros((128, 8, S)), np.zeros((128, H, S))
    for g in range(2):
        base, rel = (slice(0, 64), 64) if g == 0 else (slice(64, 128), 0)
        turn[base, 2 * g] = 1.0
        for h in range(8):
            for d in range(DK):
                row, w = rel + h * DK + d, freq[d % 4]
                for at, angle in ((0, q * w), (4, (S + 1 + q) * w)):
                    turn[row, at + 2 * g] = -np.cos(angle) if d < 4 else np.cos(angle)
                    turn[row, at + 2 * g + 1] = np.sin(angle)
                rpos[row, 8 * g + h] = np.sin(q * w) if d < 4 else np.cos(q * w)
    c["a_turn"] = (turn * DK ** -0.5).astype(np.float32)
    c["a_rpos"] = rpos.reshape(128, H * S).astype(np.float32)
    return c


def laid_out(inputs):
    import numpy as np

    A = {k: np.asarray(v) for k, v in inputs.items() if k != "mask_BxS_ff1"}
    swap = np.arange(D).reshape(H, 2, DK // 2)[:, ::-1].reshape(-1)
    lo, hi = slice(0, 64), slice(64, 128)
    Wq, Wk = A["L0_attn_Wq"], A["L0_attn_Wk"]
    Ws = Wq[:, swap]
    A["a_wq"] = np.stack([np.concatenate(p, 1) for p in (
        (Wq[:, lo], Wq[:, lo]), (Wq[:, lo], Ws[:, lo]), (Wq[:, hi], Wq[:, hi]), (Ws[:, hi], Wq[:, hi]))] + [Wk], 1)
    u, v = A["L0_attn_u"].reshape(-1), A["L0_attn_v"].reshape(-1)
    vs = v[swap]
    A["a_ub"] = np.stack([np.concatenate(p) for p in ((u[lo], v[lo]), (v[lo], vs[lo]), (v[hi], u[hi]), (vs[hi], v[hi]))], 1)
    for new, old in (("q", "q"), ("k", "k"), ("v", "v"), ("o", "o")):
        A[f"c_w{new}T"] = A[f"L0_xattn_W{old}"].T
    A["f_wconT"] = A["L0_ffn_W_con"].T
    A["f_upb"] = A["L0_ffn_up_bias"].reshape(HID // 128, 128).T
    A["s_wvT"] = A["L1_attn_w_v"].reshape(H * DQ, D).T
    for k in ("L0_attn_Wq", "L0_attn_Wk", "L0_attn_u", "L0_attn_v", "L0_xattn_Wq", "L0_xattn_Wk", "L0_xattn_Wv", "L0_xattn_Wo",
              "L0_ffn_W_con", "L0_ffn_up_bias", "L1_attn_w_v"):
        del A[k]
    return A


def kernel(**inputs):
    import numpy as np
    import concourse.bacc as bacc
    from concourse.bass_utils import run_bass_kernel_spmd

    nc = bacc.Bacc("TRN2", target_bir_lowering=False, num_devices=1)
    arrays = {f"in_{k}": np.ascontiguousarray(v) for k, v in {**laid_out(inputs), **shape_tables()}.items()}
    A = {k[3:]: nc.dram_tensor(k, a.shape, mybir.dt.from_np(a.dtype), kind="ExternalInput").ap() for k, a in arrays.items()}
    shape = inputs["x"].shape
    out = nc.dram_tensor("out_x", shape, F32, kind="ExternalOutput").ap()
    decoder_kernel(nc, A, out)
    r = run_bass_kernel_spmd(nc, [arrays], core_ids=[0])
    return r.results[0]["out_x"]
```

```python
from contextlib import ExitStack

import concourse.bass as bass
from concourse import mybir
from concourse.alu_op_type import AluOpType as ALU

F32 = mybir.dt.float32
BF16 = mybir.dt.bfloat16
I32 = mybir.dt.int32
U32 = mybir.dt.uint32
ACT = mybir.ActivationFunctionType
AX = mybir.AxisListType.X

S = 128
D = 128
T2 = 77
T2P = 80
H = 16
DK = D // H
DQ = 64
HID = 512
NSTAGE = 9
FE = 344
E = 8
EPS = 1e-5
HIDDEN = -1e30
PEEL = 4
UNROLL = 4


def need(eng, sem, value):
    if not isinstance(value, int) or value > 0:
        eng.wait_ge(sem, value)


def apart(eng, passed, count, waits):
    for _, v in waits:
        if not isinstance(v, int):
            eng.to_reg(v)
    eng.wait_ge(passed, count)
    for sem, v in waits:
        need(eng, sem, v)


def rounds(eng, n, lag, body, peel=PEEL):
    def peeled(i):
        body(i, i % UNROLL, lambda k: 0 <= i - k < n)
    for i in range(peel):
        peeled(i)
    with eng.Fori(peel // UNROLL, n // UNROLL) as r:
        for u in range(UNROLL):
            body(r * UNROLL + u, u, lambda k: True)
    for i in range(n, n + lag):
        peeled(i)


def landed(i, par):
    return i * 8 + (16 - 8 * par)


def heads(ap, n):
    return ap.rearrange("p (h k) -> p h k", h=n)


def spread(ap, n, where):
    ap = ap.unsqueeze(where)
    shape = list(ap.shape)
    shape[where] = n
    return ap.broadcast_to(shape)


def norm_parts(sb, sem, p, g=1):
    return {
        "g": g,
        "stats": [sb(f"{p}_stats{k}", [S, g, 6], F32) for k in range(2)],
        "mv": [sb(f"{p}_mv{k}", [S, g, 2], F32) for k in range(2)],
        "vare": [sb(f"{p}_vare{k}", [S, g], F32) for k in range(2)],
        "rstd": [sb(f"{p}_rstd{k}", [S, g], F32) for k in range(2)],
        "power": sb(f"{p}_power", [S, g], F32),
        "power_set": sem(f"{p}_power_set"),
        "stat_done": sem(f"{p}_stat_done"),
        "mv_done": sem(f"{p}_mv_done"),
        "vare_done": sem(f"{p}_vare_done"),
        "rstd_done": sem(f"{p}_rstd_done"),
        "normed": sem(f"{p}_normed"),
    }


def norm_measure(nc, dve, norm, i, par, y):
    g = norm["g"]
    need(dve, norm["mv_done"], g * (i - 1))
    for k in range(g):
        nc.vector.bn_stats(norm["stats"][par][:, k, :], y[:, k, :]).then_inc(norm["stat_done"], 1)
    apart(dve, norm["power_set"], 1, (
        (norm["stat_done"], g * (i + 1)),
        (norm["normed"], g * (i - 1)),
        (norm["vare_done"], i - 1)))
    for k in range(g):
        nc.vector.bn_aggr(norm["mv"][par][:, k, :], norm["stats"][par][:, k, :]).then_inc(norm["mv_done"], 1)


def norm_start(nc, pool, norm):
    nc.gpsimd.memset(norm["power"][:], -0.5).then_inc(norm["power_set"], 1)
    pool.wait_ge(norm["power_set"], 1)


def norm_root(nc, pool, norm, i, par, also=()):
    apart(pool, norm["power_set"], 1, (
        (norm["mv_done"], norm["g"] * (i + 1)),
        (norm["rstd_done"], i - 1),
        *also))
    nc.gpsimd.tensor_scalar(norm["vare"][par][:], norm["mv"][par][:, :, 1], EPS, None, ALU.add).then_inc(norm["vare_done"], 1)
    need(pool, norm["vare_done"], i + 1)
    need(pool, norm["normed"], norm["g"] * (i - 1))
    nc.gpsimd.tensor_tensor(norm["rstd"][par][:], norm["vare"][par][:], norm["power"][:], ALU.pow).then_inc(norm["rstd_done"], 1)


def norm_apply(nc, dve, norm, i, par, out, y):
    need(dve, norm["rstd_done"], i + 1)
    for k in range(norm["g"]):
        nc.vector.tensor_scalar(out[:, k, :], y[:, k, :], norm["mv"][par][:, k, 0:1], norm["rstd"][par][:, k:k + 1],
                                ALU.subtract, ALU.mult).then_inc(norm["normed"], 1)


def self_attention_0(nc, sem, n, x_all, ident, A):
    NQ = 4
    HQ = H // NQ
    with ExitStack() as ctx:
        def sb(name, shape, dt):
            return ctx.enter_context(nc.sbuf_tensor(name, shape, dt))

        def psum(name, shape):
            return ctx.enter_context(nc.psum_tensor(name, shape, F32))

        wq = sb("a_wq", [D, 5, 128], F32)
        wv = sb("a_wv", [D, D], F32)
        wo = sb("a_wo", [D, D], F32)
        bo = sb("a_bo", [S, D], F32)
        ub = sb("a_ub", [128, 4], F32)
        turn = sb("a_turn", [128, 8, S], F32)
        hmask = sb("a_hmask", [128, 8], F32)
        hsum = sb("a_hsum", [128, H], F32)
        above = sb("a_above", [S, S], U32)
        beside = sb("a_beside", [S, S], U32)
        xs = [sb(f"a_xs{k}", [S, D], F32) for k in range(2)]
        xT = [sb(f"a_xT{k}", [D, S], F32) for k in range(2)]
        kT = [sb(f"a_kT{k}", [D, S], F32) for k in range(2)]
        kr = [sb(f"a_kr{k}", [128, H * S], F32) for k in range(2)]
        vp = [sb(f"a_vp{k}", [S, H, 32], F32) for k in range(4)]
        ql = [sb(f"a_ql{k}", [128, 2, S], F32) for k in range(2)]
        qu = [sb(f"a_qu{k}", [128, 2, S], F32) for k in range(2)]
        t1 = sb("a_t1", [128, 4, S], F32)
        qb = sb("a_qb", [128, 4, S], F32)
        t2 = sb("a_t2", [128, 4, S], F32)
        pr = [sb(f"a_pr{k}", [128, S], F32) for k in range(2)]
        nmx = [sb(f"a_nmx{k}", [S, HQ], F32) for k in range(NQ)]
        pe_ = [sb(f"a_pe{k}", [S, HQ * S], F32) for k in range(NQ)]
        bs = [sb(f"a_bs{k}", [S, H], F32) for k in range(2)]
        pT = [sb(f"a_pT{k}", [S, HQ * S], F32) for k in range(2)]
        avs = sb("a_avs", [128, 4, S], F32)
        rden = sb("a_rden", [S, H], F32)
        att = sb("a_att", [S, D], F32)
        attT = sb("a_attT", [D, S], F32)
        y = [sb(f"a_y{k}", [S, D], F32) for k in range(2)]
        y2 = [sb(f"a_y2{k}", [S, D], F32) for k in range(2)]
        norm = norm_parts(sb, sem, "a")

        pS = [psum(f"a_pS{k}", [128, 512]) for k in range(2)]
        pU = psum("a_pU", [128, 512])
        pT_ = psum("a_pT_", [128, 512])
        pA = psum("a_pA", [128, 512])
        pO = psum("a_pO", [128, 512])
        pQ = psum("a_pQ", [128, 512])
        pW = psum("a_pW", [128, 512])
        pxT, pkT, pv, pB = pW[:, 0:128], pW[:, 128:256], pW[:, 256:384], pW[:, 384:384 + H]

        s_w = sem("a_weights")
        s_set = sem("a_set")
        s_x = [sem(f"a_x_loaded{k}") for k in range(2)]
        s_xTp = sem("a_xT_in_psum")
        s_xT = sem("a_xT_ready")
        s_kvp = sem("a_kv_in_psum")
        s_kT = sem("a_kT_ready")
        s_v = sem("a_v_ready")
        s_qp = sem("a_q_in_psum")
        s_t = sem("a_turned_parts")
        s_ql = sem("a_ql_ready")
        s_ub = sem("a_biased_queries")
        s_tm = sem("a_turned_parts_above")
        s_qu = sem("a_qu_turned")
        s_kr = sem("a_kr_ready")
        s_pr = sem("a_products")
        s_B = sem("a_beside_scores")
        s_su = sem("a_scores")
        s_pu = sem("a_above_put")
        s_pe = sem("a_beside_put")
        s_mx = sem("a_max")
        s_Bc = sem("a_beside_copied")
        s_ex = sem("a_probs")
        s_tp = sem("a_probsT_in_psum")
        s_pT = sem("a_probsT")
        s_av = sem("a_values_mixed")
        s_avs = sem("a_mixed_copied")
        s_ot = sem("a_mixed_turned")
        s_rd = sem("a_den_inverse")
        s_at = sem("a_att_normed")
        s_atp = sem("a_attT_in_psum")
        s_atT = sem("a_attT")
        s_wo = sem("a_projected")
        s_y = sem("a_y")
        s_y2 = sem("a_y2")
        s_qb = sem("a_qu_base")
        s_ini = sem("a_rows_loaded")
        s_zero = sem("a_zeroed")
        NW = 12

        block = ctx.enter_context(nc.Block())

        @block.sync
        def _(sp):
            for dst, src in ((ident[:], A["ident"]), (wq[:], A["a_wq"]), (wv[:], A["L0_attn_Wv"]),
                             (wo[:], A["L0_attn_Wo"]), (ub[:], A["a_ub"]), (turn[:], A["a_turn"]),
                             (hmask[:], A["a_hmask"]), (hsum[:], A["a_hsum"]), (above[:], A["above"]),
                             (beside[:], A["beside"]), (bo[:], A["L0_attn_bo"].unsqueeze(0).broadcast_to([S, D]))):
                sp.dma_start(dst, src).then_inc(s_w, 16)
            sp.dma_start(x_all[:, 0:n, :], A["x"].rearrange("b s d -> s b d")[:, 0:n, :]).then_inc(s_w, 16)
            sp.wait_ge(s_w, 16 * NW)

            def body(i, u, on):
                par = u % 2
                need(sp, s_xTp, i - 1)
                sp.dma_start(xs[par][:], x_all[:, bass.ds(i, 1), :].rearrange("s b d -> s (b d)")).then_inc(s_x[par], 16)
            rounds(sp, n, 0, body)

        @block.tensor
        def _(pe):
            pe.wait_ge(s_w, 16 * NW)
            pe.wait_ge(s_set, 4)

            def scores(a, par, c):
                g, half = c // 2, c % 2
                if c == 0:
                    need(pe, s_ql, a + 1)
                    need(pe, s_qb, 2 * a + 2)
                if half == 0:
                    need(pe, s_qu, 2 * a + g + 1)
                    need(pe, s_kr, 2 * a + g + 1)
                need(pe, s_ex, 4 * a + c - 1)
                nc.tensor.matmul(pS[c % 2][:], ql[par][:, g, :], kr[par][:, c * 512:(c + 1) * 512],
                                 start=True, stop=True)
                need(pe, s_pu, 4 * a + c)
                nc.tensor.matmul(pU[:], qu[par][:, g, :], kr[par][:, c * 512:(c + 1) * 512],
                                 start=True, stop=True).then_inc(s_su, 1)

            def turn_probs(a, c):
                need(pe, s_ex, 4 * a + c + 1)
                need(pe, s_pT, 4 * a + c)
                for j in range(HQ):
                    last = nc.tensor.transpose(pT_[:, j * S:(j + 1) * S], pe_[c][:, j * S:(j + 1) * S], ident[:])
                last.then_inc(s_tp, 1)

            def mix(a, v, c):
                need(pe, s_pT, 4 * a + c + 1)
                if c == 0:
                    need(pe, s_v, a + 1)
                    need(pe, s_avs, a)
                for j in range(HQ):
                    last = nc.tensor.matmul(pA[32 * j:32 * j + 32, c * S:(c + 1) * S], v[:, 4 * c + j, :],
                                            pT[c % 2][:, j * S:(j + 1) * S], start=True, stop=True)
                last.then_inc(s_av, 1)

            def body(i, u, on):
                par = u % 2
                a, t, z, q = i - 1, i - 2, i - 3, 1 - par
                v1, v2 = vp[(u + 3) % 4], vp[(u + 2) % 4]
                if on(1):
                    scores(a, q, 0)
                if on(0):
                    need(pe, s_x[par], landed(i, par))
                    need(pe, s_Bc, i)
                    nc.tensor.transpose(pxT, xs[par][:], ident[:]).then_inc(s_xTp, 1)
                if on(2):
                    turn_probs(t, 2)
                    mix(t, v2, 1)
                if on(1):
                    scores(a, q, 1)
                if on(0):
                    need(pe, s_xT, i + 1)
                    nc.tensor.matmul(pkT, wq[:, 4, :], xT[par][:], start=True, stop=True)
                    nc.tensor.matmul(pv, xT[par][:], wv[:], start=True, stop=True).then_inc(s_kvp, 1)
                if on(2):
                    turn_probs(t, 3)
                    mix(t, v2, 2)
                if on(0):
                    need(pe, s_t, 4 * i)
                    need(pe, s_ub, i)
                    for m in range(4):
                        last = nc.tensor.matmul(pQ[:, m * S:(m + 1) * S], wq[:, m, :], xT[par][:],
                                                start=True, stop=True)
                    last.then_inc(s_qp, 1)
                if on(3):
                    need(pe, s_at, z + 1)
                    nc.tensor.transpose(pO[:, 0:128], att[:], ident[:]).then_inc(s_atp, 1)
                if on(1):
                    scores(a, q, 2)
                    turn_probs(a, 0)
                if on(2):
                    mix(t, v2, 3)
                if on(3):
                    need(pe, s_atT, z + 1)
                    nc.tensor.matmul(pO[:, 128:256], attT[:], wo[:], start=True, stop=True).then_inc(s_wo, 1)
                if on(1):
                    scores(a, q, 3)
                    turn_probs(a, 1)
                    mix(a, v1, 0)
                if on(0):
                    need(pe, s_pr, 2 * i + 2)
                    need(pe, s_kT, i + 1)
                    need(pe, s_v, i + 1)
                    nc.tensor.matmul(pB, pr[par][:], hsum[:], start=True, stop=True).then_inc(s_B, 1)
                if on(2):
                    need(pe, s_avs, t + 1)
                    need(pe, s_y, t)
                    for c in range(4):
                        last = nc.tensor.transpose(pO[:, c * S:(c + 1) * S], avs[:, c, :], ident[:])
                    last.then_inc(s_ot, 1)
            rounds(pe, n, 3, body)

        @block.vector
        def _(dve):
            dve.wait_ge(s_w, 16 * NW)
            dve.wait_ge(s_set, 4)

            def soften(a, par, c):
                s3 = heads(pS[c % 2][:], HQ)
                apart(dve, s_set, 4, ((s_su, 4 * a + c + 1),))
                nc.vector.copy_predicated(s3, spread(above[:], HQ, 1), heads(pU[:], HQ)).then_inc(s_pu, 1)
                apart(dve, s_set, 4, ((s_pu, 4 * a + c + 1), (s_Bc, a + 1)))
                nc.vector.copy_predicated(s3, spread(beside[:], HQ, 1),
                                          spread(bs[par][:, 4 * c:4 * c + 4], S, 2)).then_inc(s_pe, 1)
                need(dve, s_pe, 4 * a + c + 1)
                need(dve, s_ex, 4 * a + c - 3)
                nc.vector.tensor_reduce(nmx[c][:], s3, AX, ALU.max, negate=True).then_inc(s_mx, 1)

            def body(i, u, on):
                par = u % 2
                a, z, w, q = i - 1, i - 3, i - 4, 1 - par
                if on(1):
                    soften(a, q, 0)
                if on(3):
                    need(dve, s_ot, z + 1)
                    o4 = pO[:].rearrange("p (h e) -> p h e", h=H)
                    nc.vector.reciprocal(rden[:], o4[:, :, DK]).then_inc(s_rd, 1)
                    need(dve, s_rd, z + 1)
                    need(dve, s_atp, z)
                    nc.vector.tensor_tensor(heads(att[:], H), o4[:, :, 0:DK], spread(rden[:], DK, 2),
                                            ALU.mult).then_inc(s_at, 1)
                if on(1):
                    soften(a, q, 1)
                if on(4):
                    norm_apply(nc, dve, norm, w, par, x_all[:, bass.ds(w, 1), :], y2[par][:].unsqueeze(1))
                if on(0):
                    need(dve, s_qp, i + 1)
                    need(dve, s_ql, i)
                    for k in range(4):
                        nc.vector.scalar_tensor_tensor(t1[:, k, :], pQ[:, k * S:(k + 1) * S], ub[:, k:k + 1], turn[:, k, :],
                                                       ALU.add, ALU.mult).then_inc(s_t, 1)
                    need(dve, s_t, 4 * i + 4)
                    need(dve, s_su, 4 * (i - 1))
                    need(dve, s_pr, 2 * (i - 1))
                    t4 = t1[:].rearrange("p (g m) q -> p g m q", g=2)
                    nc.vector.tensor_tensor(ql[par][:], t4[:, :, 0, :], t4[:, :, 1, :], ALU.add).then_inc(s_ql, 1)
                if on(1):
                    soften(a, q, 2)
                if on(3):
                    need(dve, s_wo, z + 1)
                    need(dve, s_y2, z - 1)
                    nc.vector.tensor_tensor(y[q][:], pO[:, 128:256], x_all[:, bass.ds(z, 1), :].rearrange("s b d -> s (b d)"),
                                            ALU.add).then_inc(s_y, 1)
                    need(dve, s_y, z + 1)
                    need(dve, norm["normed"], z - 1)
                    nc.vector.tensor_tensor(y2[q][:], y[q][:], bo[:], ALU.add).then_inc(s_y2, 1)
                    need(dve, s_y2, z + 1)
                    norm_measure(nc, dve, norm, z, q, y2[q][:].unsqueeze(1))
                if on(1):
                    soften(a, q, 3)
            rounds(dve, n, 4, body)

        @block.scalar
        def _(act):
            act.wait_ge(s_set, 4)

            def probs(a, c):
                need(act, s_mx, 4 * a + c + 1)
                need(act, s_tp, 4 * a + c - 3)
                for j in range(HQ):
                    last = nc.scalar.activation(pe_[c][:, j * S:(j + 1) * S], pS[c % 2][:, j * S:(j + 1) * S], ACT.Exp,
                                                bias=nmx[c][:, j:j + 1])
                last.then_inc(s_ex, 1)

            def probsT(a, c):
                need(act, s_tp, 4 * a + c + 1)
                need(act, s_av, 4 * a + c - 1)
                nc.scalar.copy(pT[c % 2][:], pT_[:]).then_inc(s_pT, 1)

            def body(i, u, on):
                par = u % 2
                a, t, z = i - 1, i - 2, i - 3
                if on(0):
                    need(act, s_xTp, i + 1)
                    need(act, s_qp, i - 1)
                    nc.scalar.copy(xT[par][:], pxT).then_inc(s_xT, 1)
                if on(2):
                    probsT(t, 2)
                if on(1):
                    probs(a, 0)
                if on(0):
                    need(act, s_kvp, i + 1)
                    need(act, s_kr, 2 * (i - 1))
                    need(act, s_pr, 2 * (i - 1))
                    nc.scalar.copy(kT[par][:], pkT).then_inc(s_kT, 1)
                    need(act, s_av, 4 * (i - 3))
                    nc.scalar.copy(vp[u][:, :, 0:DK], heads(pv, H)).then_inc(s_v, 1)
                if on(2):
                    probsT(t, 3)
                if on(1):
                    probs(a, 1)
                if on(3):
                    need(act, s_atp, z + 1)
                    need(act, s_wo, z)
                    nc.scalar.copy(attT[:], pO[:, 0:128]).then_inc(s_atT, 1)
                if on(1):
                    probsT(a, 0)
                if on(2):
                    need(act, s_av, 4 * t + 4)
                    need(act, s_ot, t)
                    nc.scalar.copy(avs[:], heads(pA[:], 4)).then_inc(s_avs, 1)
                if on(0):
                    need(act, s_t, 4 * i + 4)
                    need(act, s_tm, 2 * i)
                    for k in range(4):
                        rel = slice(64, 128) if k < 2 else slice(0, 64)
                        last = nc.scalar.activation(qb[rel, k, :], pQ[rel, k * S:(k + 1) * S], ACT.Identity, bias=ub[rel, k:k + 1])
                    last.then_inc(s_ub, 1)
                if on(1):
                    probs(a, 2)
                    probsT(a, 1)
                if on(0):
                    need(act, s_B, i + 1)
                    need(act, s_pe, 4 * (i - 1))
                    nc.scalar.copy(bs[par][:], pB).then_inc(s_Bc, 1)
                if on(1):
                    probs(a, 3)
            rounds(act, n, 3, body)

        @block.gpsimd
        def _(pool):
            norm_start(nc, pool, norm)
            for k in range(2):
                pool.dma_start(kr[k][:], A["a_rpos"]).then_inc(s_ini, 16)
                nc.gpsimd.memset(pr[k][:], 0.0).then_inc(s_zero, 1)
                nc.gpsimd.memset(qu[k][:], 0.0).then_inc(s_zero, 1)
            for k in range(4):
                nc.gpsimd.memset(vp[k][:], 0.0).then_inc(s_zero, 1)
            pool.wait_ge(s_zero, 8)
            pool.wait_ge(s_ini, 32)
            pool.wait_ge(s_w, 16 * NW)
            for k in range(4):
                nc.gpsimd.memset(vp[k][:, :, DK:DK + 1], 1.0).then_inc(s_set, 1)

            def keys(i, par, g):
                r = slice(64 * g, 64 * g + 64)
                nc.gpsimd.tensor_tensor(heads(kr[par][r, g * 1024:(g + 1) * 1024], 8), spread(kT[par][r, :], 8, 1),
                                        spread(hmask[r, :], S, 2), ALU.mult).then_inc(s_kr, 1)

            def above_rows(i, par, g):
                rel = slice(64, 128) if g == 0 else slice(0, 64)
                nc.gpsimd.tensor_tensor(t2[rel, 2 * g:2 * g + 2, 0:S - 1], qb[rel, 2 * g:2 * g + 2, 1:S],
                                        turn[rel, 4 + 2 * g:6 + 2 * g, 0:S - 1], ALU.mult).then_inc(s_tm, 1)
                need(pool, s_tm, 2 * i + g + 1)
                nc.gpsimd.tensor_tensor(qu[par][rel, g, 0:S - 1], t2[rel, 2 * g, 0:S - 1], t2[rel, 2 * g + 1, 0:S - 1],
                                        ALU.add).then_inc(s_qu, 1)

            def body(i, u, on):
                par = u % 2
                z, q = i - 3, 1 - par
                if on(0):
                    need(pool, s_kT, i + 1)
                    need(pool, s_su, 4 * (i - 1))
                    need(pool, norm["rstd_done"], i - 3)
                    need(pool, s_kr, 2 * i)
                    keys(i, par, 0)
                    need(pool, s_ql, i + 1)
                    need(pool, s_B, i - 1)
                    need(pool, s_kr, 2 * i + 1)
                    for g in range(2):
                        r = slice(64 * g, 64 * g + 64)
                        need(pool, s_qb, 2 * i + g)
                        nc.gpsimd.tensor_tensor(pr[par][r, 0:S - 1], ql[par][r, g, 0:S - 1], kT[par][r, 1:S],
                                                ALU.mult).then_inc(s_pr, 1)
                        apart(pool, s_zero, 8, ((s_pr, 2 * i + g + 1),))
                        nc.gpsimd.tensor_copy(qu[par][r, g, :], ql[par][r, g, :]).then_inc(s_qb, 1)
                    need(pool, s_qb, 2 * i + 2)
                    need(pool, s_ub, i + 1)
                    need(pool, s_qu, 2 * i)
                    above_rows(i, par, 0)
                    need(pool, s_qu, 2 * i + 1)
                    keys(i, par, 1)
                    need(pool, s_kr, 2 * i + 2)
                    above_rows(i, par, 1)
                if on(3):
                    norm_root(nc, pool, norm, z, q, ((s_qu, 2 * i + 2),) if on(0) else ())
            rounds(pool, n, 3, body)


def cross_attention_0(nc, sem, n, x_all, ident, A):
    SCALE = float(D) ** -0.5
    with ExitStack() as ctx:
        def sb(name, shape, dt=F32):
            return ctx.enter_context(nc.sbuf_tensor(name, shape, dt))

        def pair(name, shape):
            return [sb(f"{name}{k}", shape) for k in range(2)]

        def bank(name):
            return ctx.enter_context(nc.psum_tensor(name, [128, 512], F32))

        w = sb("c_w", [D, 4, D])
        bq, bv, bo = sb("c_bq", [D, 1]), sb("c_bv", [D, 1]), sb("c_bo", [S, D])
        xs, cs = pair("c_xs", [S, D]), pair("c_cs", [T2, D])
        xT, cT = pair("c_xT", [D, S]), pair("c_cT", [D, 128])
        qT, kT = pair("c_qT", [D, S]), pair("c_kT", [D, 128])
        v = [sb(f"c_v{k}", [T2, D]) for k in range(4)]
        mx, nm, den, rden = pair("c_mx", [S, 1]), pair("c_nm", [S, 1]), pair("c_den", [S, 1]), pair("c_rden", [S, 1])
        ex, pn = pair("c_ex", [S, T2]), pair("c_pn", [S, T2])
        pT, oT = pair("c_pT", [T2, S]), pair("c_oT", [D, S])
        y, y2 = pair("c_y", [S, 1, D]), pair("c_y2", [S, 1, D])
        norm = norm_parts(sb, sem, "c")
        pX, pQ, pS, pP, pM, pO = (bank(f"c_p{k}") for k in "XQSPMO")

        s_w, s_set = sem("c_weights"), sem("c_set")
        s_x = [sem(f"c_loaded{k}") for k in range(2)]
        s_xp, s_xT, s_cT = sem("c_xcT_in_psum"), sem("c_xT"), sem("c_cT")
        s_qp, s_q, s_k, s_v = sem("c_qkv_in_psum"), sem("c_q"), sem("c_k"), sem("c_v_ready")
        s_s, s_mx, s_nm, s_ex, s_rd, s_pn = (sem(f"c_{k}") for k in ("scores", "max", "negmax", "exp", "rden", "probs"))
        s_pp, s_pT, s_mp, s_oT, s_op, s_y, s_y2 = (sem(f"c_{k}") for k in (
            "pT_in_psum", "pT_ready", "mixed_in_psum", "mixed", "out_in_psum", "y_ready", "y2_ready"))

        block = ctx.enter_context(nc.Block())

        @block.sync
        def _(sp):
            for k, name in enumerate(("c_wqT", "c_wkT", "c_wvT", "c_woT")):
                sp.dma_start(w[:, k, :], A[name]).then_inc(s_w, 16)
            sp.dma_start(bq[:], A["L0_xattn_bq"].unsqueeze(1)).then_inc(s_w, 16)
            sp.dma_start(bv[:], A["L0_xattn_bv"].unsqueeze(1)).then_inc(s_w, 16)
            sp.dma_start(bo[:], A["L0_xattn_bo"].unsqueeze(0).broadcast_to([S, D])).then_inc(s_w, 16)

            def body(i, u, on):
                par = u % 2
                need(sp, s_xp, i - 1)
                sp.dma_start(xs[par][:], x_all[:, bass.ds(i, 1), :].rearrange("s b d -> s (b d)")).then_inc(s_x[par], 16)
                sp.dma_start(cs[par][:], A["ctx_1024"][bass.ds(i, 1), :, :].rearrange("b t d -> (b t) d")).then_inc(s_x[par], 16)
            rounds(sp, n, 0, body, 8)

        @block.tensor
        def _(pe):
            pe.wait_ge(s_w, 16 * 7)
            pe.wait_ge(s_set, 2)

            def body(i, u, on):
                par = u % 2
                q = 1 - par
                if on(5):
                    t = i - 5
                    need(pe, s_oT, t + 1)
                    need(pe, s_y, t)
                    nc.tensor.matmul(pO[:, 0:D], oT[q][:], w[:, 3, :], start=True, stop=True).then_inc(s_op, 1)
                if on(4):
                    t = i - 4
                    need(pe, s_pT, t + 1)
                    need(pe, s_oT, t)
                    nc.tensor.matmul(pM[:, 0:S], v[u][:], pT[par][:], start=True, stop=True).then_inc(s_mp, 1)
                if on(2):
                    t = i - 2
                    need(pe, s_q, t + 1)
                    need(pe, s_k, t + 1)
                    need(pe, s_ex, t)
                    nc.tensor.matmul(pS[:, 0:128], qT[par][:], kT[par][:], start=True, stop=True).then_inc(s_s, 1)
                if on(3):
                    t = i - 3
                    need(pe, s_pn, t + 1)
                    need(pe, s_pT, t)
                    nc.tensor.transpose(pP[0:T2, 0:S], pn[q][:], ident[:]).then_inc(s_pp, 1)
                if on(1):
                    t = i - 1
                    need(pe, s_xT, t + 1)
                    need(pe, s_cT, t + 1)
                    need(pe, s_v, t)
                    nc.tensor.matmul(pQ[:, 0:128], w[:, 0, :], xT[q][:], start=True, stop=True)
                    nc.tensor.matmul(pQ[:, 128:256], w[:, 1, :], cT[q][:], start=True, stop=True)
                    nc.tensor.matmul(pQ[0:T2, 256:384], cT[q][:, 0:T2], w[:, 2, :], start=True, stop=True).then_inc(s_qp, 1)
                if on(0):
                    need(pe, s_x[par], landed(i, par) * 2)
                    need(pe, s_cT, i)
                    nc.tensor.transpose(pX[:, 0:S], xs[par][:], ident[:])
                    nc.tensor.transpose(pX[:, S:S + T2], cs[par][:], ident[0:T2, 0:T2]).then_inc(s_xp, 1)
            rounds(pe, n, 5, body, 8)

        @block.scalar
        def _(act):
            act.wait_ge(s_w, 16 * 7)
            act.wait_ge(s_set, 2)

            def body(i, u, on):
                par = u % 2
                q = 1 - par
                if on(4):
                    t = i - 4
                    need(act, s_mp, t + 1)
                    need(act, s_op, t - 1)
                    nc.scalar.activation(oT[par][:], pM[:, 0:S], ACT.Identity, bias=bv[:]).then_inc(s_oT, 1)
                if on(3):
                    t = i - 3
                    need(act, s_pp, t + 1)
                    need(act, s_mp, t - 1)
                    nc.scalar.copy(pT[q][:], pP[0:T2, 0:S]).then_inc(s_pT, 1)
                if on(2):
                    t = i - 2
                    need(act, s_nm, t + 1)
                    need(act, s_pn, t - 1)
                    need(act, s_rd, t - 1)
                    nc.scalar.activation(ex[par][:], pS[:, 0:T2], ACT.Exp, bias=nm[par][:], scale=SCALE,
                                         accum_out=den[par][:]).then_inc(s_ex, 1)
                if on(1):
                    t = i - 1
                    need(act, s_qp, t + 1)
                    need(act, s_s, t - 1)
                    nc.scalar.activation(qT[q][:], pQ[:, 0:128], ACT.Identity, bias=bq[:]).then_inc(s_q, 1)
                    nc.scalar.copy(kT[q][:], pQ[:, 128:256]).then_inc(s_k, 1)
                    need(act, s_mp, t - 3)
                    nc.scalar.copy(v[(u - 1) % 4][:], pQ[0:T2, 256:384]).then_inc(s_v, 1)
                if on(0):
                    need(act, s_xp, i + 1)
                    need(act, s_qp, i - 1)
                    nc.scalar.copy(xT[par][:], pX[:, 0:S]).then_inc(s_xT, 1)
                    nc.scalar.copy(cT[par][:, 0:T2], pX[:, S:S + T2]).then_inc(s_cT, 1)
            rounds(act, n, 5, body, 8)

        @block.vector
        def _(dve):
            dve.wait_ge(s_w, 16 * 7)

            def body(i, u, on):
                par = u % 2
                q = 1 - par
                if on(3):
                    t = i - 3
                    need(dve, s_ex, t + 1)
                    need(dve, s_pn, t - 1)
                    nc.vector.reciprocal(rden[q][:], den[q][:]).then_inc(s_rd, 1)
                    need(dve, s_rd, t + 1)
                    need(dve, s_pp, t - 1)
                    nc.vector.tensor_scalar(pn[q][:], ex[q][:], rden[q][:], None, ALU.mult).then_inc(s_pn, 1)
                if on(2):
                    t = i - 2
                    need(dve, s_s, t + 1)
                    nc.vector.tensor_reduce(mx[par][:], pS[:, 0:T2], AX, ALU.max).then_inc(s_mx, 1)
                    need(dve, s_mx, t + 1)
                    need(dve, s_ex, t - 1)
                    nc.vector.tensor_scalar(nm[par][:], mx[par][:], -SCALE, None, ALU.mult).then_inc(s_nm, 1)
                if on(6):
                    t = i - 6
                    norm_apply(nc, dve, norm, t, par, x_all[:, bass.ds(t, 1), :], y2[par][:])
                if on(5):
                    t = i - 5
                    need(dve, s_op, t + 1)
                    need(dve, s_y2, t - 1)
                    nc.vector.tensor_tensor(y[q][:, 0, :], pO[:, 0:D], x_all[:, bass.ds(t, 1), :].rearrange("s b d -> s (b d)"),
                                            ALU.add).then_inc(s_y, 1)
                    need(dve, s_y, t + 1)
                    need(dve, norm["normed"], t - 1)
                    nc.vector.tensor_tensor(y2[q][:, 0, :], y[q][:, 0, :], bo[:], ALU.add).then_inc(s_y2, 1)
                    need(dve, s_y2, t + 1)
                    norm_measure(nc, dve, norm, t, q, y2[q][:])
            rounds(dve, n, 6, body, 8)

        @block.gpsimd
        def _(pool):
            norm_start(nc, pool, norm)
            for k in range(2):
                nc.gpsimd.memset(cT[k][:], 0.0).then_inc(s_set, 1)

            def body(i, u, on):
                par = u % 2
                if on(5):
                    norm_root(nc, pool, norm, i - 5, 1 - par)
            rounds(pool, n, 6, body, 8)

def butterfly_weights(nc, sem, ident, A, w1, b1, w2, b2):
    with ExitStack() as ctx:
        def sb(name, shape, dt=F32):
            return ctx.enter_context(nc.sbuf_tensor(name, shape, dt))

        RING = 3
        wr = {k: [sb(f"b_w{k}{j}", [128, 2 * HID]) for j in range(RING)] for k in "ud"}
        row = {"u": [sb(f"b_u{j}", [128, 2, HID]) for j in range(2)], "d": [sb(f"b_d{j}", [128, 1, HID]) for j in range(2)]}
        tmp = {k: sb(f"b_t{k}", [128, 2, 2, HID]) for k in "ud"}
        bias = sb("b_bias", [128, 2, D])
        upb = sb("b_upb", [128, HID // 128])
        ones = sb("b_ones", [1, 1])
        p1 = ctx.enter_context(nc.psum_tensor("b_p1", [128, 512], F32))
        p2 = ctx.enter_context(nc.psum_tensor("b_p2", [128, 512], F32))
        s_in = sem("b_inputs")
        s_w = {k: [sem(f"b_w_{k}{j}") for j in range(RING)] for k in "ud"}
        s_mul = {k: sem(f"b_products_{k}") for k in "ud"}
        s_add = {k: sem(f"b_stage_{k}") for k in "ud"}
        s_cp, s_one, s_t, s_up, s_b2 = sem("b_w1_copied"), sem("b_one"), sem("b_turned"), sem("b_up_bias"), sem("b_out")
        nrow = {"u": 2, "d": 1}
        block = ctx.enter_context(nc.Block())

        def stage(k, n):
            return n if k == "u" else NSTAGE - 1 - n

        @block.sync
        def _(sp):
            sp.dma_start(row["u"][0][:, 0, :], A["L0_ffn_W_exp"]).then_inc(s_in, 16)
            sp.dma_start(row["u"][0][:, 1, :], A["L0_ffn_b_exp"].unsqueeze(0).broadcast_to([128, HID])).then_inc(s_in, 16)
            sp.dma_start(row["d"][0][:, 0, :], A["f_wconT"]).then_inc(s_in, 16)
            sp.dma_start(bias[:, 0, :], A["L0_ffn_b_con"].unsqueeze(0).broadcast_to([128, D])).then_inc(s_in, 16)
            sp.dma_start(bias[:, 1, :], A["L0_ffn_down_bias"].unsqueeze(0).broadcast_to([128, D])).then_inc(s_in, 16)
            sp.dma_start(upb[:], A["f_upb"]).then_inc(s_in, 16)
            for n in range(NSTAGE):
                for k, name in (("u", "L0_ffn_up_weights"), ("d", "L0_ffn_down_weights")):
                    if n >= RING:
                        sp.wait_ge(s_mul[k], 2 * nrow[k] * (n - RING + 1))
                    src = A[name][stage(k, n)].rearrange("p i j -> (p i j)").unsqueeze(0).broadcast_to([128, 2 * HID])
                    sp.dma_start(wr[k][n % RING][:], src).then_inc(s_w[k][n % RING], 16)

        def stages(eng, ops, k):
            R = nrow[k]
            eng.wait_ge(s_in, 16 * 6)
            for n in range(NSTAGE):
                st = 2 ** stage(k, n)
                nb = HID // (2 * st)
                w = wr[k][n % RING][:].rearrange("p (b s i j) -> p b s i j", b=nb, s=st, i=2)
                eng.wait_ge(s_w[k][n % RING], 16 * (n // RING + 1))
                if n >= 1:
                    eng.wait_ge(s_add[k], R * n)
                for r in range(R):
                    pairs = row[k][n % 2][:, r, :].rearrange("p (b w s) -> p b w s", b=nb, w=2)
                    for j in range(2):
                        wj = (w[:, :, :, :, j] if k == "u" else w[:, :, :, j, :]).rearrange("p b s i -> p b i s")
                        out = tmp[k][:, r, j, :].rearrange("p (b i s) -> p b i s", b=nb, i=2)
                        ops.tensor_tensor(out, pairs[:, :, j:j + 1, :].broadcast_to([128, nb, 2, st]), wj,
                                          ALU.mult).then_inc(s_mul[k], 1)
                eng.wait_ge(s_mul[k], 2 * R * (n + 1))
                for r in range(R):
                    ops.tensor_tensor(row[k][(n + 1) % 2][:, r, :], tmp[k][:, r, 0, :], tmp[k][:, r, 1, :],
                                      ALU.add).then_inc(s_add[k], 1)

        @block.vector
        def _(dve):
            nc.vector.memset(ones[:], 1.0).then_inc(s_one, 1)
            stages(dve, nc.vector, "u")
            dve.wait_ge(s_add["u"], 2 * NSTAGE)
            nc.vector.tensor_copy(w1[:], row["u"][NSTAGE % 2][:, 0, :]).then_inc(s_cp, 1)
            dve.wait_ge(s_t, 1)
            nc.vector.tensor_tensor(b1[:], p1[:, 0:4], upb[:], ALU.add).then_inc(s_up, 1)

        @block.gpsimd
        def _(pool):
            stages(pool, nc.gpsimd, "d")
            nc.gpsimd.tensor_tensor(b2[:], bias[:, 0, :], bias[:, 1, :], ALU.add).then_inc(s_b2, 1)

        @block.tensor
        def _(pe):
            pe.wait_ge(s_one, 1)
            pe.wait_ge(s_add["u"], 2 * NSTAGE)
            for c in range(4):
                last = nc.tensor.matmul(p1[:, c:c + 1], row["u"][NSTAGE % 2][0:1, 1, c * 128:(c + 1) * 128], ones[:],
                                        start=True, stop=True)
            last.then_inc(s_t, 1)
            pe.wait_ge(s_add["d"], NSTAGE)
            for c in range(4):
                last = nc.tensor.transpose(p2[:, c * 128:(c + 1) * 128], row["d"][NSTAGE % 2][:, 0, c * 128:(c + 1) * 128], ident[:])
            last.then_inc(s_t, 1)

        @block.scalar
        def _(act):
            act.wait_ge(s_t, 2)
            nc.scalar.copy(w2[:], p2[:].rearrange("p (c d) -> p c d", c=4)).then_inc(s_b2, 1)


def butterfly_ffn(nc, sem, n, x_all, ident, A):
    G = 4
    C = HID // 128
    with ExitStack() as ctx:
        def sb(name, shape, dt=F32):
            return ctx.enter_context(nc.sbuf_tensor(name, shape, dt))

        def bank(name):
            return ctx.enter_context(nc.psum_tensor(name, [128, 512], F32))

        w1, b1 = sb("f_w1", [D, HID]), sb("f_b1", [128, C])
        w2, b2 = sb("f_w2", [128, C, D]), sb("f_b2", [128, D])
        butterfly_weights(nc, sem, ident, A, w1, b1, w2, b2)

        xs = [sb(f"f_xs{k}", [S, G, D]) for k in range(2)]
        xT = [sb(f"f_xT{k}", [D, G * S]) for k in range(2)]
        g = [sb(f"f_g{k}", [128, C, G * S]) for k in range(2)]
        y, y2 = ([sb(f"f_{m}{k}", [S, G, D]) for k in range(2)] for m in ("y", "z"))
        norm = norm_parts(sb, sem, "f", G)
        pX, pY = bank("f_pX"), bank("f_pY")
        pH = [bank(f"f_pH{k}") for k in range(2)]
        s_x = [sem(f"f_loaded{k}") for k in range(2)]
        s_xp, s_xT, s_h, s_g, s_yp, s_y, s_y2 = (sem(f"f_{k}") for k in (
            "xT_in_psum", "xT_ready", "hidden", "gelu", "out_in_psum", "y_ready", "y2_ready"))
        block = ctx.enter_context(nc.Block())
        m = n // G

        @block.sync
        def _(sp):
            def body(i, u, on):
                par = u % 2
                need(sp, s_xp, i - 1)
                sp.dma_start(xs[par][:], x_all[:, bass.ds(i * G, G), :]).then_inc(s_x[par], 16)
            rounds(sp, m, 0, body)

        @block.tensor
        def _(pe):
            def body(i, u, on):
                par = u % 2
                q = 1 - par
                if on(0):
                    need(pe, s_x[par], landed(i, par))
                    need(pe, s_xT, i)
                    for k in range(G):
                        last = nc.tensor.transpose(pX[:, k * S:(k + 1) * S], xs[par][:, k, :], ident[:])
                    last.then_inc(s_xp, 1)
                if on(1):
                    t = i - 1
                    need(pe, s_xT, t + 1)
                    for c in range(C):
                        need(pe, s_g, C * t + c - 1)
                        nc.tensor.matmul(pH[c % 2][:], w1[:, c * 128:(c + 1) * 128], xT[q][:], start=True, stop=True).then_inc(s_h, 1)
                if on(2):
                    t = i - 2
                    need(pe, s_g, C * (t + 1))
                    need(pe, s_y, t)
                    for k in range(G):
                        for c in range(C):
                            last = nc.tensor.matmul(pY[:, k * D:(k + 1) * D], g[par][:, c, k * S:(k + 1) * S], w2[:, c, :],
                                                    start=(c == 0), stop=(c == C - 1))
                    last.then_inc(s_yp, 1)
            rounds(pe, m, 2, body)

        @block.scalar
        def _(act):
            def body(i, u, on):
                par = u % 2
                q = 1 - par
                if on(0):
                    need(act, s_xp, i + 1)
                    need(act, s_h, C * (i - 1))
                    nc.scalar.copy(xT[par][:], pX[:]).then_inc(s_xT, 1)
                if on(1):
                    t = i - 1
                    need(act, s_yp, t - 1)
                    for c in range(C):
                        need(act, s_h, C * t + c + 1)
                        nc.scalar.activation(g[q][:, c, :], pH[c % 2][:], ACT.Gelu, bias=b1[:, c:c + 1]).then_inc(s_g, 1)
            rounds(act, m, 1, body)

        @block.vector
        def _(dve):
            def body(i, u, on):
                par = u % 2
                q = 1 - par
                if on(3):
                    t = i - 3
                    norm_apply(nc, dve, norm, t, q, x_all[:, bass.ds(t * G, G), :], y2[q][:])
                if on(2):
                    t = i - 2
                    need(dve, s_yp, t + 1)
                    need(dve, s_y2, t - 1)
                    nc.vector.tensor_tensor(y[par][:], pY[:].rearrange("p (g d) -> p g d", g=G), x_all[:, bass.ds(t * G, G), :],
                                            ALU.add).then_inc(s_y, 1)
                    need(dve, s_y, t + 1)
                    need(dve, norm["normed"], G * (t - 1))
                    nc.vector.tensor_tensor(y2[par][:], y[par][:], spread(b2[:], G, 1), ALU.add).then_inc(s_y2, 1)
                    need(dve, s_y2, t + 1)
                    norm_measure(nc, dve, norm, t, par, y2[par][:])
            rounds(dve, m, 3, body)

        @block.gpsimd
        def _(pool):
            norm_start(nc, pool, norm)

            def body(i, u, on):
                if on(2):
                    norm_root(nc, pool, norm, i - 2, u % 2)
            rounds(pool, m, 2, body)


def attentions_1(nc, sem, n, x_all, ident, A):
    HQ = 4
    SCALE = float(DQ) ** -0.5
    BEHIND = 4
    TC = 16
    CH = [(t, min(TC, T2 - t)) for t in range(0, T2, TC)]
    NCH = len(CH)
    ON_POOL = (1, 2, 4)
    NB = T2P // 4
    R = NB // 4
    PEEL_1 = 12
    with ExitStack() as ctx:
        def sb(name, shape, dt=F32):
            return ctx.enter_context(nc.sbuf_tensor(name, shape, dt))

        def pair(name, shape, dt=F32):
            return [sb(f"{name}{k}", shape, dt) for k in range(2)]

        def bank(name):
            return ctx.enter_context(nc.psum_tensor(name, [128, 512], F32))

        wqk = sb("s_wqk", [DQ, 2, H, D])
        wa = sb("s_wa", [D, H, D])
        wv = sb("s_wv", [D, H * DQ])
        wo = sb("s_wo", [128, 8, D])
        hide = sb("s_hide", [S, S])
        hide_b, ident_b = sb("s_hide_b", [S, S], BF16), sb("s_ident_b", [128, 128], BF16)
        xs, xT, tT = pair("s_xs", [S, D]), pair("s_xT", [D, S]), pair("s_tT", [D, HQ * S])
        v = pair("s_v", [S, H * DQ])
        nm = pair("s_nm", [S, HQ])
        den, rden = ([sb(f"s_{m}{k}", [S, HQ]) for k in range(4)] for m in ("den", "rden"))
        p = [sb(f"s_p{k}", [S, HQ * S]) for k in range(4)]
        pn, pT = pair("s_pn", [S, HQ * S]), pair("s_pT", [S, HQ * S])
        yT, y = pair("s_yT", [128, 8, S]), pair("s_y", [S, 1, D])
        norm = norm_parts(sb, sem, "s")
        pM = bank("s_pM")
        pX, pO, pC = pM[:, 0:S], pM[:, 128:128 + D], pM[:, 256:256 + T2P]
        pT_, pY, pP = (bank(f"s_p{k}_") for k in "TYP")
        pS = [bank(f"s_pS{k}") for k in range(2)]

        s_w, s_b, s_ab, s_wa = sem("s_weights"), sem("s_casts"), sem("s_wa_in_psum"), sem("s_wa_ready")
        s_x = [sem(f"s_loaded{k}") for k in range(2)]
        s_xp, s_xT = sem("s_xT_in_psum"), sem("s_xT_ready")
        s_tq, s_tT = sem("s_t_in_psum"), sem("s_t_ready")
        s_vp, s_v = sem("s_v_in_psum"), sem("s_v_ready")
        s_s, s_nm, s_ex, s_rd, s_pn, s_tp, s_mix = (sem(f"s_{k}") for k in (
            "scores", "negmax", "exp", "rden", "probs", "probsT_in_psum", "mixed"))
        s_pT = [sem(f"s_probsT{k}") for k in range(2)]
        s_yT, s_op, s_y = sem("s_yT_ready"), sem("s_out_in_psum"), sem("s_y_ready")

        wt, wf = sb("t_ws", [D, D]), sb("t_w", [D, D])
        wc = sb("t_wc", [D, 2, D])
        wcol = sb("t_wcol", [D, 2, 1])
        wz = sb("t_wz", [D, 63])
        wcol_w = sb("t_wv", [D, 1])
        b = sb("t_b", [D, 1])
        bc = sb("t_bc", [S, 2])
        rows, cs, qm = pair("t_xs", [S, D]), pair("t_cs", [T2, D]), pair("t_qm", [S, T2P], I32)
        rowsT, cT = pair("t_xT", [D, S]), pair("t_cT", [D, 128])
        feat, txt = pair("t_feat", [D, S]), pair("t_txt", [D, T2P])
        cw, mk = ([sb(f"t_{m}{k}", [S, *w]) for k in range(4)] for m, w in (("cw", (2, 128)), ("mk", (T2P,))))
        args = [sb(f"t_args{k}", [D, TC, S]) for k in range(4)]
        th = [sb(f"t_th{k}", [D, TC, S]) for k in range(3)]
        rho_s = sb("t_rho_s", [128, 4, S])
        rho, m1 = pair("t_rho", [S, T2P]), pair("t_m1", [S, T2P])
        nmx, dens, rdens, acc, g = (pair(f"t_{k}", [S, w]) for k, w in (("nmx", 1), ("den", 1), ("rden", 1), ("acc", 2), ("g", 2)))
        ex, scr = pair("t_ex", [S, T2]), pair("t_scr", [S, 2, T2])
        z, z2 = pair("t_z", [S, 1, D]), pair("t_z2", [S, 1, D])
        norm_c = norm_parts(sb, sem, "t")
        pR = bank("t_pR")
        pN = bank("t_pN")

        c_w, c_set, c_zero = sem("t_weights"), sem("t_set"), sem("t_zeroed")
        c_x = [sem(f"t_loaded{k}") for k in range(2)]
        c_xp, c_xT, c_cT, c_fg = (sem(f"t_{k}") for k in ("xcT_in_psum", "xT", "cT", "proj_in_psum"))
        c_feat, c_txt, c_cw = (sem(f"t_{k}_ready") for k in ("feat", "txt", "cw"))
        c_sumd, c_sump = sem("t_sums_vector"), sem("t_sums_gpsimd")
        c_th, c_red = sem("t_tanh"), sem("t_reduced")
        c_rs, c_rt, c_m1, c_mk, c_rho, c_mx, c_ex = (sem(f"t_{k}") for k in (
            "rho_copied", "rho_turned", "unmasked", "mask_ready", "rho_ready", "negmax", "exp"))
        c_rd, c_acc, c_g, c_z, c_z2 = (sem(f"t_{k}") for k in ("rden", "averaged", "gates", "z_ready", "z2_ready"))

        TH = (0, 1, 0, 1, 2)
        picked = ident[:].rearrange("p (j r) -> p j r", j=4)[:, :, 0:R]

        def back(c, k):
            return (1, c - k) if c >= k else (2, c - k + 4)

        BUFFER = {0: (0, 5), 3: (1, 5), 1: (2, 2), 2: (3, 5), 4: (2, 3)}

        def sums_ready(eng, t, k):
            if k in ON_POOL:
                need(eng, c_sump, 3 * t + ON_POOL.index(k) + 1)
            else:
                need(eng, c_sumd, 2 * t + k // 3 + 1)

        def buffer_free(eng, t, k):
            need(eng, c_th, NCH * t + k - BUFFER[k][1] + 1)

        block = ctx.enter_context(nc.Block())

        @block.sync
        def _(sp):
            sp.dma_start(wqk[:, 0, :, :], A["L1_attn_w_q"].rearrange("h d c -> d h c")).then_inc(s_w, 16)
            sp.dma_start(wqk[:, 1, :, :], A["L1_attn_w_k"].rearrange("h d c -> d h c")).then_inc(s_w, 16)
            sp.dma_start(wv[:], A["s_wvT"]).then_inc(s_w, 16)
            sp.dma_start(wo[:], A["L1_attn_w_o"].rearrange("(m p) d -> p m d", p=128)).then_inc(s_w, 16)
            sp.dma_start(hide[:], A["hide"]).then_inc(s_w, 16)
            for dst, src in ((wt[:], A["L1_xattn_Ws"]), (wf[:], A["L1_xattn_W"]), (wcol_w[:], A["L1_xattn_w"]),
                             (b[:], A["L1_xattn_b"].rearrange("o d -> d o")),
                             (wcol[:, 0, :], A["L1_xattn_Wcw"].rearrange("o d -> d o")),
                             (wcol[:, 1, :], A["L1_xattn_Wcb"].rearrange("o d -> d o")),
                             (bc[:, 0:1], A["L1_xattn_bcw"].unsqueeze(0).broadcast_to([S, 1])),
                             (bc[:, 1:2], A["L1_xattn_bcb"].unsqueeze(0).broadcast_to([S, 1]))):
                sp.dma_start(dst, src).then_inc(c_w, 16)

            def body(i, u, on):
                par = u % 2
                if on(0):
                    need(sp, s_xp, i - 1)
                    sp.dma_start(xs[par][:], x_all[:, bass.ds(i, 1), :].rearrange("s b d -> s (b d)")).then_inc(s_x[par], 16)
                if on(BEHIND):
                    t = i - BEHIND
                    if not isinstance(t, int):
                        for value in (t - 1, t + 1):
                            sp.to_reg(value)
                    need(sp, norm["normed"], t + 1)
                    need(sp, c_xp, t - 1)
                    need(sp, c_m1, t - 1)
                    sp.dma_start(rows[par][:], x_all[:, bass.ds(t, 1), :].rearrange("s b d -> s (b d)")).then_inc(c_x[par], 16)
                    sp.dma_start(cs[par][:], A["ctx_1024"][bass.ds(t, 1), :, :].rearrange("b t d -> (b t) d")).then_inc(c_x[par], 16)
                    sp.dma_start(qm[par][:, 0:T2], A["mask_BxS2_ik0"][bass.ds(t, 1), :].broadcast_to([S, T2])).then_inc(c_x[par], 16)
            rounds(sp, n, BEHIND, body, PEEL_1)

        @block.tensor
        def _(pe):
            pe.wait_ge(s_w, 16 * 5)
            for h in range(H):
                if h % 4 == 0 and h >= 8:
                    pe.wait_ge(s_wa, h // 4 - 1)
                last = nc.tensor.matmul(pS[h // 4 % 2][:, h % 4 * D:(h % 4 + 1) * D], wqk[:, 0, h, :], wqk[:, 1, h, :],
                                        start=True, stop=True)
                if h % 4 == 3:
                    last.then_inc(s_ab, 1)
            pe.wait_ge(s_wa, 4)
            pe.wait_ge(s_b, 2)
            pe.wait_ge(c_w, 16 * 8)
            pe.wait_ge(c_set, 5)

            def turn_queries(a, q, c):
                if c == 0:
                    need(pe, s_xT, a + 1)
                if c in (0, 3):
                    need(pe, s_tT, 4 * a + c)
                else:
                    need(pe, s_v, 2 * a + c)
                for j in range(HQ):
                    last = nc.tensor.matmul(pP[:, j * S:(j + 1) * S], wa[:, HQ * c + j, :], xT[q][:], start=True, stop=True)
                last.then_inc(s_tq, 1)

            def values(a, q, k):
                need(pe, s_tT, 4 * a + k + 1)
                nc.tensor.matmul(pP[:], xT[q][:], wv[:, k * 512:(k + 1) * 512], start=True, stop=True).then_inc(s_vp, 1)

            def scores(x, par, c):
                need(pe, s_tT, 4 * x + c + 1)
                need(pe, s_ex, 4 * x + c - 1)
                nc.tensor.matmul(pS[c % 2][:], ident_b[:], spread(hide_b[:], HQ, 1), start=True, stop=True)
                for j in range(HQ):
                    last = nc.tensor.matmul(pS[c % 2][:, j * S:(j + 1) * S], tT[c % 2][:, j * S:(j + 1) * S], xT[par][:],
                                            start=False, stop=True, skip_group_check=True)
                last.then_inc(s_s, 1)

            def turn_probs(x, c):
                need(pe, s_pn, 4 * x + c + 1)
                need(pe, s_pT[1 - c % 2], 2 * x + (c + 1) // 2)
                for j in range(HQ):
                    last = nc.tensor.transpose(pT_[:, j * S:(j + 1) * S], pn[c % 2][:, j * S:(j + 1) * S], ident[:])
                last.then_inc(s_tp, 1)

            def mix(x, par, c):
                need(pe, s_pT[c % 2], 2 * x + c // 2 + 1)
                if c == 0:
                    need(pe, s_v, 2 * x + 2)
                if c % 2 == 0:
                    need(pe, s_yT, 2 * x + c // 2)
                for j in range(HQ):
                    r, m = 64 * (j % 2), (2 * c + j // 2) % 4
                    last = nc.tensor.matmul(pY[r:r + 64, m * S:(m + 1) * S], v[par][:, (HQ * c + j) * DQ:(HQ * c + j + 1) * DQ],
                                            pT[c % 2][:, j * S:(j + 1) * S], start=True, stop=True)
                last.then_inc(s_mix, 1)

            def reduce(t, q, k):
                need(pe, c_th, NCH * t + k + 1)
                if k == 0:
                    need(pe, c_rs, t)
                t0, nt = CH[k]
                for b0 in range(0, nt, 4):
                    blk = (t0 + b0) // 4
                    j, r = blk % 4, blk // 4
                    w = min(4, nt - b0)
                    last = nc.tensor.matmul(pR[32 * j:32 * j + 32, 0:w * S], wz[:, 31 - r:63 - r],
                                            th[TH[k]][:, b0:b0 + w, :].rearrange("p t f -> p (t f)"),
                                            start=(r == 0), stop=(r == R - 1), skip_group_check=True)
                last.then_inc(c_red, 1)

            def body(i, u, on):
                par = u % 2
                q = 1 - par
                for c in range(4):
                    if on(1):
                        turn_queries(i - 1, q, c)
                    lag, cc = back(c, 1)
                    if on(lag):
                        scores(i - lag, (par + lag) % 2, cc)
                    if c == 1 and on(BEHIND + 1):
                        t = i - BEHIND - 1
                        need(pe, c_cT, t + 1)
                        nc.tensor.matmul(pN[:, 0:128], wf[:], rowsT[q][:], start=True, stop=True)
                        nc.tensor.matmul(pN[:, 128:256], wt[:], cT[q][:], start=True, stop=True)
                        for k in range(2):
                            last = nc.tensor.matmul(pN[:, 128 * (k + 2):128 * (k + 3)], wc[:, k, :], cT[q][:], start=True, stop=True)
                        last.then_inc(c_fg, 1)
                    lag, cc = back(c, 3)
                    if on(lag):
                        turn_probs(i - lag, cc)
                    if on(1) and c < 2:
                        values(i - 1, q, c)
                    if c == 2 and on(BEHIND + 3):
                        t = i - BEHIND - 3
                        need(pe, c_rs, t + 1)
                        if on(4):
                            need(pe, s_y, t + 4)
                        need(pe, c_rho, t)
                        if on(0):
                            need(pe, s_xT, i + 1)
                        for k in range(4):
                            last = nc.tensor.matmul(pC[:, k * NB:(k + 1) * NB], rho_s[:, k, :], picked, start=True, stop=True)
                        last.then_inc(c_rt, 1)
                    if c == 2 and on(3):
                        t = i - 3
                        need(pe, s_yT, 2 * t + 2)
                        if on(0):
                            need(pe, s_xT, i + 1)
                        need(pe, s_y, t)
                        for m in range(8):
                            last = nc.tensor.matmul(pO, yT[q][:, m, :], wo[:, m, :], start=(m == 0), stop=(m == 7))
                        last.then_inc(s_op, 1)
                    if on(2):
                        mix(i - 2, par, c)
                    if c == 0 and on(0):
                        need(pe, s_x[par], landed(i, par))
                        need(pe, s_xT, i)
                        need(pe, s_y, i - 3)
                        need(pe, c_rho, i - 7)
                        nc.tensor.transpose(pX, xs[par][:], ident[:]).then_inc(s_xp, 1)
                    if c == 0 and on(BEHIND + 3):
                        reduce(i - BEHIND - 3, q, 3)
                        reduce(i - BEHIND - 3, q, 4)
                    if c >= 1 and on(BEHIND + 2):
                        reduce(i - BEHIND - 2, par, c - 1)
                    if c == 3 and on(BEHIND):
                        t = i - BEHIND
                        need(pe, c_x[par], landed(t, par) * 3)
                        need(pe, c_cw, t)
                        nc.tensor.transpose(pN[:, 0:S], rows[par][:], ident[:])
                        nc.tensor.transpose(pN[:, S:S + T2], cs[par][:], ident[0:T2, 0:T2]).then_inc(c_xp, 1)
            rounds(pe, n, BEHIND + 3, body, PEEL_1)

        @block.scalar
        def _(act):
            for k in range(4):
                act.wait_ge(s_ab, k + 1)
                nc.scalar.activation(wa[:, 4 * k:4 * k + 4, :], heads(pS[k % 2][:], 4), ACT.Copy, scale=SCALE).then_inc(s_wa, 1)
            act.wait_ge(c_w, 16 * 8)
            act.wait_ge(c_set, 5)

            def exps(x, c):
                need(act, s_nm, 4 * x + c + 1)
                need(act, s_pn, 4 * x + c - 3)
                need(act, s_rd, 4 * x + c - 3)
                for j in range(HQ):
                    last = nc.scalar.activation(p[c][:, j * S:(j + 1) * S], pS[c % 2][:, j * S:(j + 1) * S], ACT.Exp,
                                                bias=nm[c % 2][:, j:j + 1], accum_out=den[c][:, j:j + 1])
                last.then_inc(s_ex, 1)

            def tanh(t, par, k):
                sums_ready(act, t, k)
                need(act, c_red, NCH * t + k - (3, 3, 2, 2, 5)[k] + 1)
                nt = CH[k][1]
                nc.scalar.activation(th[TH[k]][:, 0:nt, :], args[BUFFER[k][0]][:, 0:nt, :], ACT.Tanh).then_inc(c_th, 1)

            def body(i, u, on):
                par = u % 2
                q = 1 - par
                for c in range(4):
                    if c == 3 and on(BEHIND + 2):
                        tanh(i - BEHIND - 2, par, 3)
                    if c in (0, 2):
                        lag, half = (3, 1) if c == 0 else (2, 0)
                        if on(lag):
                            t = i - lag
                            need(act, s_mix, 4 * t + 2 * half + 2)
                            need(act, s_op, t - 1)
                            nc.scalar.copy(yT[(u + lag) % 2][:, 4 * half:4 * half + 4, :], heads(pY[:], 4)).then_inc(s_yT, 1)
                    if on(1) and c < 2:
                        a = i - 1
                        need(act, s_vp, 2 * a + c + 1)
                        need(act, s_mix, 4 * (a - 1))
                        nc.scalar.copy(v[q][:, c * 512:(c + 1) * 512], pP[:]).then_inc(s_v, 1)
                    lag, cc = back(c, 1)
                    if on(lag):
                        exps(i - lag, cc)
                    lag, cc = back(c, 3)
                    if on(lag) and cc % 2 == 1:
                        x = i - lag
                        need(act, s_tp, 4 * x + cc + 1)
                        need(act, s_mix, 4 * x + cc - 1)
                        nc.scalar.copy(pT[1][:], pT_[:]).then_inc(s_pT[1], 1)
                    if c == 1 and on(0):
                        need(act, s_xp, i + 1)
                        need(act, s_s, 4 * (i - 1))
                        nc.scalar.copy(xT[par][:], pX).then_inc(s_xT, 1)
                    if c == 0 and on(BEHIND + 1):
                        t = i - BEHIND - 1
                        need(act, c_xp, t + 1)
                        need(act, c_fg, t - 1)
                        nc.scalar.copy(rowsT[q][:], pN[:, 0:S]).then_inc(c_xT, 1)
                        nc.scalar.copy(cT[q][:, 0:T2], pN[:, S:S + T2]).then_inc(c_cT, 1)
                    if c == 0 and on(BEHIND + 4):
                        t = i - BEHIND - 4
                        need(act, c_mx, t + 1)
                        need(act, c_acc, 2 * (t - 1))
                        need(act, c_rd, t - 1)
                        nc.scalar.activation(ex[par][:], rho[par][:, 0:T2], ACT.Exp, bias=nmx[par][:],
                                             accum_out=dens[par][:]).then_inc(c_ex, 1)
                    if c == 2 and on(BEHIND + 1):
                        t = i - BEHIND - 1
                        need(act, c_fg, t + 1)
                        need(act, c_sump, 3 * (t - 1))
                        need(act, c_sumd, 2 * (t - 1))
                        nc.scalar.copy(feat[q][:], pN[:, 0:128]).then_inc(c_feat, 1)
                        nc.scalar.activation(txt[q][:], pN[:, 128:128 + T2P], ACT.Identity, bias=b[:]).then_inc(c_txt, 1)
                        need(act, c_acc, 2 * (t - 3))
                        nc.scalar.copy(cw[(u + 3) % 4][:], pN[:, 256:512].rearrange("p (k t) -> p k t", k=2)).then_inc(c_cw, 1)
                    if c == 2 and on(BEHIND + 4):
                        t = i - BEHIND - 4
                        need(act, c_acc, 2 * t + 2)
                        need(act, c_rd, t + 1)
                        need(act, c_z, t - 1)
                        for k in range(2):
                            last = nc.scalar.activation(g[par][:, k:k + 1], acc[par][:, k:k + 1], ACT.Tanh, bias=bc[:, k:k + 1],
                                                        scale=rdens[par][:])
                        last.then_inc(c_g, 1)
                    if on(BEHIND + 2):
                        tanh(i - BEHIND - 2, par, c if c < 3 else 4)
            rounds(act, n, BEHIND + 4, body, PEEL_1)

        @block.vector
        def _(dve):
            dve.wait_ge(s_w, 16 * 5)
            nc.vector.tensor_copy(hide_b[:], hide[:]).then_inc(s_b, 1)
            nc.vector.tensor_copy(ident_b[:], ident[:]).then_inc(s_b, 1)
            dve.wait_ge(c_w, 16 * 8)
            for k in range(2):
                nc.vector.tensor_copy(wc[:, k, :], wcol[:, k, :].broadcast_to([D, D])).then_inc(c_set, 1)
            dve.wait_ge(c_set, 5)

            def sums(t, par, k):
                t0, nt = CH[k]
                need(dve, c_feat, t + 1)
                need(dve, c_txt, t + 1)
                buffer_free(dve, t, k)
                nc.vector.tensor_tensor(args[BUFFER[k][0]][:, 0:nt, :], spread(feat[par][:], nt, 1),
                                        spread(txt[par][:, t0:t0 + nt], S, 2), ALU.add).then_inc(c_sumd, 1)

            def body(i, u, on):
                par = u % 2
                q = 1 - par
                for c in range(4):
                    if on(1):
                        a = i - 1
                        need(dve, s_tq, 4 * a + c + 1)
                        need(dve, s_s, 4 * a + c - 1)
                        nc.vector.tensor_copy(tT[c % 2][:], pP[:]).then_inc(s_tT, 1)
                    if c == 1 and on(BEHIND + 3):
                        t = i - BEHIND - 3
                        need(dve, c_red, NCH * (t + 1))
                        need(dve, c_rt, t)
                        nc.vector.tensor_copy(rho_s[:], heads(pR[:], 4)).then_inc(c_rs, 1)
                    lag, cc = back(c, 1)
                    if on(lag):
                        x = i - lag
                        need(dve, s_s, 4 * x + cc + 1)
                        need(dve, s_ex, 4 * x + cc - 1)
                        nc.vector.tensor_reduce(nm[cc % 2][:], heads(pS[cc % 2][:], HQ), AX, ALU.max, negate=True).then_inc(s_nm, 1)
                    lag, cc = back(c, 2)
                    if on(lag):
                        x = i - lag
                        need(dve, s_ex, 4 * x + cc + 1)
                        need(dve, s_pn, 4 * x + cc - 3)
                        nc.vector.reciprocal(rden[cc][:], den[cc][:]).then_inc(s_rd, 1)
                    lag, cc = back(c, 3)
                    if on(lag) and cc % 2 == 0:
                        x = i - lag
                        need(dve, s_tp, 4 * x + cc + 1)
                        need(dve, s_mix, 4 * x + cc - 1)
                        nc.vector.tensor_copy(pT[0][:], pT_[:]).then_inc(s_pT[0], 1)
                    if c == 3 and on(3):
                        t = i - 3
                        need(dve, s_op, t + 1)
                        need(dve, norm["normed"], t - 1)
                        nc.vector.tensor_tensor(y[q][:, 0, :], pO, x_all[:, bass.ds(t, 1), :].rearrange("s b d -> s (b d)"),
                                                ALU.add).then_inc(s_y, 1)
                        need(dve, s_y, t + 1)
                        norm_measure(nc, dve, norm, t, q, y[q][:])
                    if c == 1 and on(4):
                        norm_apply(nc, dve, norm, i - 4, par, x_all[:, bass.ds(i - 4, 1), :], y[par][:])
                    if c == 0 and on(BEHIND + 5):
                        t = i - BEHIND - 5
                        x = x_all[:, bass.ds(t, 1), :]
                        need(dve, c_g, t + 1)
                        need(dve, c_z2, t - 1)
                        nc.vector.tensor_scalar(z[q][:], x, g[q][:, 0:1], g[q][:, 1:2], ALU.mult, ALU.add).then_inc(c_z, 1)
                        need(dve, c_z, t + 1)
                        need(dve, norm_c["normed"], t - 1)
                        nc.vector.tensor_tensor(z2[q][:], z[q][:], x, ALU.add).then_inc(c_z2, 1)
                        need(dve, c_z2, t + 1)
                        norm_measure(nc, dve, norm_c, t, q, z2[q][:])
                    if c == 0 and on(BEHIND + 2):
                        sums(i - BEHIND - 2, par, 0)
                    if c == 1 and on(BEHIND + 4):
                        t = i - BEHIND - 4
                        need(dve, c_ex, t + 1)
                        need(dve, c_g, t - 1)
                        nc.vector.reciprocal(rdens[par][:], dens[par][:]).then_inc(c_rd, 1)
                        for k in range(2):
                            nc.vector.tensor_tensor_reduce(scr[par][:, k, :], ex[par][:], cw[u][:, k, 0:T2], 1.0, 0.0, ALU.mult,
                                                           ALU.add, acc[par][:, k:k + 1]).then_inc(c_acc, 1)
                    if c == 2 and on(BEHIND + 1):
                        t = i - BEHIND - 1
                        need(dve, c_x[q], landed(t, q) * 3)
                        need(dve, c_mk, t - 1)
                        nc.vector.tensor_scalar(m1[q][:, 0:T2], qm[q][:, 0:T2], -1.0, 1.0, ALU.mult, ALU.add).then_inc(c_m1, 1)
                        need(dve, c_m1, t + 1)
                        need(dve, c_rho, t - 3)
                        nc.vector.tensor_scalar(mk[(u + 3) % 4][:, 0:T2], m1[q][:, 0:T2], HIDDEN, None, ALU.mult).then_inc(c_mk, 1)
                    if c == 2 and on(BEHIND + 2):
                        sums(i - BEHIND - 2, par, 3)
                    if c == 2 and on(BEHIND + 5):
                        t = i - BEHIND - 5
                        norm_apply(nc, dve, norm_c, t, q, x_all[:, bass.ds(t, 1), :], z2[q][:])
                    if c == 3 and on(BEHIND + 3):
                        t = i - BEHIND - 3
                        need(dve, c_rt, t + 1)
                        need(dve, c_mk, t + 1)
                        need(dve, c_ex, t - 1)
                        shape = "p (r j t) -> p r j t"
                        turned = pC.rearrange("p (t j r) -> p r j t", t=4, j=4)
                        nc.vector.tensor_tensor(rho[q][:].rearrange(shape, r=R, j=4), turned,
                                                mk[(u + 1) % 4][:].rearrange(shape, r=R, j=4), ALU.add).then_inc(c_rho, 1)
                        need(dve, c_rho, t + 1)
                        nc.vector.tensor_reduce(nmx[q][:], rho[q][:, 0:T2], AX, ALU.max, negate=True).then_inc(c_mx, 1)
            rounds(dve, n, BEHIND + 5, body, PEEL_1)

        @block.gpsimd
        def _(pool):
            norm_start(nc, pool, norm)
            norm_start(nc, pool, norm_c)
            nc.gpsimd.memset(wz[:], 0.0).then_inc(c_zero, 1)
            nc.gpsimd.memset(cT[0][:], 0.0).then_inc(c_set, 1)
            nc.gpsimd.memset(cT[1][:], 0.0).then_inc(c_set, 1)
            for k in range(4):
                nc.gpsimd.memset(mk[k][:], 0.0).then_inc(c_zero, 1)
            pool.wait_ge(c_zero, 5)
            pool.wait_ge(c_w, 16 * 8)
            nc.gpsimd.tensor_copy(wz[:, 31:32], wcol_w[:]).then_inc(c_set, 1)

            def sums(t, par, k):
                t0, nt = CH[k]
                need(pool, c_feat, t + 1)
                need(pool, c_txt, t + 1)
                buffer_free(pool, t, k)
                nc.gpsimd.tensor_tensor(args[BUFFER[k][0]][:, 0:nt, :], spread(feat[par][:], nt, 1),
                                        spread(txt[par][:, t0:t0 + nt], S, 2), ALU.add).then_inc(c_sump, 1)

            def body(i, u, on):
                par = u % 2
                q = 1 - par
                for c in range(4):
                    lag, cc = back(c, 2)
                    if on(lag):
                        x = i - lag
                        need(pool, s_rd, 4 * x + cc + 1)
                        need(pool, s_tp, 4 * x + cc - 1)
                        nc.gpsimd.tensor_tensor(heads(pn[cc % 2][:], HQ), heads(p[cc][:], HQ), spread(rden[cc][:], S, 2),
                                                ALU.mult).then_inc(s_pn, 1)
                    if c == 0 and on(4):
                        norm_root(nc, pool, norm, i - 4, par)
                    if c == 1 and on(BEHIND + 5):
                        norm_root(nc, pool, norm_c, i - BEHIND - 5, q)
                    if c < 3 and on(BEHIND + 2):
                        sums(i - BEHIND - 2, par, ON_POOL[c])
            rounds(pool, n, BEHIND + 5, body, PEEL_1)


def experts_ffn_1(nc, sem, n, x_all, ident, A, out):
    G = 4
    CH = [(c, min(128, FE - c)) for c in range(0, FE, 128)]
    NC = len(CH)
    with ExitStack() as ctx:
        def sb(name, shape, dt=F32):
            return ctx.enter_context(nc.sbuf_tensor(name, shape, dt))

        def pair(name, shape, dt=F32):
            return [sb(f"{name}{k}", shape, dt) for k in range(2)]

        def bank(name):
            return ctx.enter_context(nc.psum_tensor(name, [128, 512], F32))

        wg, wu = sb("e_wg", [D, E, FE]), sb("e_wu", [D, E, FE])
        wd = sb("e_wd", [128, E, NC, D])
        wr, br = sb("e_wr", [D, E]), sb("e_br", [S, E])
        number = sb("e_number", [S, E])
        xs, xT = pair("e_xs", [S, G, D]), pair("e_xT", [D, G * S])
        logit, top, topi, topf = (pair(f"e_{k}", [S, G, 8], dt) for k, dt in (("logit", F32), ("top", F32), ("topi", U32), ("topf", F32)))
        gap, tg = pair("e_gap", [S, G]), pair("e_tg", [S, G])
        pw = pair("e_pw", [S, 2, G])
        c1, c2, w1, w2, cb = (pair(f"e_{k}", [S, G, E]) for k in ("c1", "c2", "w1", "w2", "cb"))
        sg, h = [sb(f"e_sg{k}", [128, G * S]) for k in range(2)], [sb(f"e_h{k}", [128, G * S]) for k in range(6)]
        acc = pair("e_acc", [S, G, D])
        res = pair("e_res", [S, G, D])
        norm = norm_parts(sb, sem, "e", G)
        pX = bank("e_pX")
        pY = bank("e_pY")
        pG = [bank(f"e_pG{k}") for k in range(3)]
        pU = [bank(f"e_pU{k}") for k in range(3)]

        s_w = sem("e_weights")
        s_x = [sem(f"e_loaded{k}") for k in range(2)]
        s_xp, s_xT, s_lp, s_lg, s_top, s_topi, s_topf, s_gap, s_tg, s_pw, s_c1, s_c2, s_cb = (sem(f"e_{k}") for k in (
            "xT_in_psum", "xT_ready", "logits_in_psum", "logits", "top", "top_number", "top_number_f", "gap", "tanh_gap",
            "pair_weights", "first", "second", "combine"))
        s_eq = sem("e_chosen")
        s_gp, s_up, s_sg, s_h = (sem(f"e_{k}") for k in ("gate_in_psum", "up_in_psum", "silu", "hidden"))
        s_yp, s_acc = sem("e_expert_in_psum"), sem("e_added")
        s_st = [sem(f"e_stored{k}") for k in range(2)]
        block = ctx.enter_context(nc.Block())
        m = n // G
        NCE = NC * E

        @block.sync
        def _(sp):
            sp.dma_start(wr[:], A["L1_ffn_Ws"]).then_inc(s_w, 16)
            sp.dma_start(br[:], A["L1_ffn_bs"].unsqueeze(0).broadcast_to([S, E])).then_inc(s_w, 16)
            sp.dma_start(number[:], A["number"].unsqueeze(0).broadcast_to([S, E])).then_inc(s_w, 16)
            for e in range(0, E, 4):
                sp.dma_start(wg[:, e:e + 4, :], A["L1_ffn_Wg"][e:e + 4].rearrange("e d f -> d e f")).then_inc(s_w, 16)
                sp.dma_start(wu[:, e:e + 4, :], A["L1_ffn_Wu"][e:e + 4].rearrange("e d f -> d e f")).then_inc(s_w, 16)
            for c, (f0, nf) in enumerate(CH):
                sp.dma_start(wd[0:nf, :, c, :], A["L1_ffn_Wd"][:, f0:f0 + nf, :].rearrange("e f d -> f e d")).then_inc(s_w, 16)

            def body(i, u, on):
                par = u % 2
                if on(0):
                    need(sp, s_xp, i - 1)
                    sp.dma_start(xs[par][:], x_all[:, bass.ds(i * G, G), :]).then_inc(s_x[par], 16)
                if on(2):
                    t = i - 2
                    need(sp, norm["normed"], G * (t + 1))
                    sp.dma_start(out[bass.ds(t * G, G), :, :].rearrange("b s d -> s b d"), res[par][:]).then_inc(s_st[par], 16)
            rounds(sp, m, 2, body)
            for k in range(2):
                sp.wait_ge(s_st[k], 16 * (m // 2))

        @block.tensor
        def _(pe):
            pe.wait_ge(s_w, 16 * 10)

            def body(i, u, on):
                par = u % 2
                q = 1 - par

                def down(t, e):
                    need(pe, s_h, NCE * t + NC * (e + 1))
                    need(pe, s_acc, G * (E * t + e))
                    for k in range(G):
                        for c, (f0, nf) in enumerate(CH):
                            last = nc.tensor.matmul(pY[:, k * D:(k + 1) * D], h[(NC * e + c) % 6][0:nf, k * S:(k + 1) * S],
                                                    wd[0:nf, e, c, :], start=(c == 0), stop=(c == NC - 1))
                    last.then_inc(s_yp, 1)

                def front(k):
                    if k == 0:
                        need(pe, s_x[par], landed(i, par))
                        need(pe, s_lg, i)
                        for j in range(G):
                            last = nc.tensor.transpose(pX[:, j * S:(j + 1) * S], xs[par][:, j, :], ident[:])
                        last.then_inc(s_xp, 1)
                    else:
                        need(pe, s_xT, i + 1)
                        for j in range(G):
                            last = nc.tensor.matmul(pX[:, j * E:(j + 1) * E], xT[par][:, j * S:(j + 1) * S], wr[:], start=True, stop=True)
                        last.then_inc(s_lp, 1)

                for e in range(E):
                    if on(1):
                        t = i - 1
                        if e == 0:
                            need(pe, s_xT, t + 1)
                        for c, (f0, nf) in enumerate(CH):
                            k = NC * e + c
                            need(pe, s_sg, NCE * t + k - 2)
                            nc.tensor.matmul(pG[c][0:nf, :], wg[:, e, f0:f0 + nf], xT[q][:], start=True, stop=True).then_inc(s_gp, 1)
                            need(pe, s_h, NCE * t + k - 2)
                            nc.tensor.matmul(pU[c][0:nf, :], wu[:, e, f0:f0 + nf], xT[q][:], start=True, stop=True).then_inc(s_up, 1)
                        if e >= 1:
                            down(t, e - 1)
                    if on(0) and e in (2, 4):
                        front(e // 2 - 1)
                if on(1):
                    down(i - 1, E - 1)
            rounds(pe, m, 1, body)

        @block.scalar
        def _(act):
            def body(i, u, on):
                par = u % 2
                for e in range(E):
                    if on(1):
                        t = i - 1
                        for c, (f0, nf) in enumerate(CH):
                            k = NC * e + c
                            need(act, s_gp, NCE * t + k + 1)
                            need(act, s_h, NCE * t + k - 1)
                            nc.scalar.activation(sg[k % 2][0:nf, :], pG[c][0:nf, :], ACT.Silu).then_inc(s_sg, 1)
                    if on(0) and e == 2:
                        need(act, s_xp, i + 1)
                        need(act, s_up, NCE * (i - 1))
                        need(act, s_lp, i - 1)
                        nc.scalar.copy(xT[par][:], pX[:]).then_inc(s_xT, 1)
                    if on(0) and e == 6:
                        need(act, s_gap, i + 1)
                        need(act, s_pw, 2 * (i - 1))
                        nc.scalar.activation(tg[par][:], gap[par][:], ACT.Tanh, scale=0.5).then_inc(s_tg, 1)
            rounds(act, m, 1, body)

        @block.vector
        def _(dve):
            dve.wait_ge(s_w, 16 * 10)

            def combine(i, par, k):
                if k == 0:
                    need(dve, s_lp, i + 1)
                    need(dve, s_topi, G * (i - 1))
                    nc.vector.tensor_tensor(logit[par][:], pX[:, 0:G * E].rearrange("p (g e) -> p g e", g=G), spread(br[:], G, 1),
                                            ALU.add).then_inc(s_lg, 1)
                    apart(dve, s_w, 16 * 10, ((s_lg, i + 1), (s_gap, i - 1)))
                    for j in range(G):
                        nc.vector.max(top[par][:, j, :], logit[par][:, j, :]).then_inc(s_top, 1)
                    apart(dve, s_w, 16 * 10, ((s_top, G * (i + 1)), (s_topf, i - 1)))
                    for j in range(G):
                        nc.vector.max_index(topi[par][:, j, :], top[par][:, j, :], logit[par][:, j, :]).then_inc(s_topi, 1)
                    need(dve, s_tg, i - 1)
                    nc.vector.tensor_tensor(gap[par][:], top[par][:, :, 0], top[par][:, :, 1], ALU.subtract).then_inc(s_gap, 1)
                    need(dve, s_topi, G * (i + 1))
                    need(dve, s_c2, i - 1)
                    nc.vector.tensor_copy(topf[par][:], topi[par][:]).then_inc(s_topf, 1)
                else:
                    need(dve, s_tg, i + 1)
                    need(dve, s_c2, i - 1)
                    nc.vector.tensor_scalar(pw[par][:, 0, :], tg[par][:], 0.5, 0.5, ALU.mult, ALU.add).then_inc(s_pw, 1)
                    nc.vector.tensor_scalar(pw[par][:, 1, :], tg[par][:], -0.5, 0.5, ALU.mult, ALU.add).then_inc(s_pw, 1)
                    need(dve, s_topf, i + 1)
                    need(dve, s_cb, i - 1)
                    nc.vector.tensor_tensor(c1[par][:], spread(number[:], G, 1), topf[par][:, :, 0:1].broadcast_to([S, G, E]),
                                            ALU.is_equal).then_inc(s_eq, 1)
                    nc.vector.tensor_tensor(c2[par][:], spread(number[:], G, 1), topf[par][:, :, 1:2].broadcast_to([S, G, E]),
                                            ALU.is_equal).then_inc(s_eq, 1)
                    need(dve, s_eq, 2 * (i + 1))
                    need(dve, s_pw, 2 * (i + 1))
                    nc.vector.tensor_tensor(w1[par][:], c1[par][:], spread(pw[par][:, 0, :], E, 2), ALU.mult).then_inc(s_c1, 1)
                    nc.vector.tensor_tensor(w2[par][:], c2[par][:], spread(pw[par][:, 1, :], E, 2), ALU.mult).then_inc(s_c2, 1)
                    need(dve, s_c1, i + 1)
                    need(dve, s_c2, i + 1)
                    need(dve, s_acc, G * E * (i - 1))
                    nc.vector.tensor_tensor(cb[par][:], w1[par][:], w2[par][:], ALU.add).then_inc(s_cb, 1)

            def body(i, u, on):
                par = u % 2
                q = 1 - par

                def add(t, e):
                    need(dve, s_yp, E * t + e + 1)
                    if e == 0:
                        need(dve, s_cb, t + 1)
                        need(dve, norm["normed"], G * (t - 1))
                    else:
                        need(dve, s_acc, G * (E * t + e))
                    for k in range(G):
                        before = x_all[:, bass.ds(t * G + k, 1), :].rearrange("s b d -> s (b d)") if e == 0 else acc[q][:, k, :]
                        nc.vector.scalar_tensor_tensor(acc[q][:, k, :], pY[:, k * D:(k + 1) * D], cb[q][:, k, e:e + 1], before,
                                                       ALU.mult, ALU.add).then_inc(s_acc, 1)

                for e in range(E):
                    if on(1):
                        t = i - 1
                        for c, (f0, nf) in enumerate(CH):
                            k = NC * e + c
                            need(dve, s_sg, NCE * t + k + 1)
                            need(dve, s_up, NCE * t + k + 1)
                            need(dve, s_yp, E * t + e - 1)
                            nc.vector.tensor_tensor(h[k % 6][0:nf, :], sg[k % 2][0:nf, :], pU[c][0:nf, :], ALU.mult).then_inc(s_h, 1)
                        if e >= 1:
                            add(t, e - 1)
                    if on(2) and e == 0:
                        t = i - 2
                        need(dve, s_st[par], 8 * t - 8 * par)
                        norm_apply(nc, dve, norm, t, par, res[par][:], acc[par][:])
                    if on(0) and e == 5:
                        combine(i, par, 0)
                    if on(0) and e == 7:
                        combine(i, par, 1)
                if on(1):
                    add(i - 1, E - 1)
                    need(dve, s_acc, G * E * i)
                    norm_measure(nc, dve, norm, i - 1, q, acc[q][:])
            rounds(dve, m, 2, body)

        @block.gpsimd
        def _(pool):
            norm_start(nc, pool, norm)

            def body(i, u, on):
                if on(1):
                    norm_root(nc, pool, norm, i - 1, 1 - u % 2)
            rounds(pool, m, 1, body)


def decoder_kernel(nc, A, out):
    n = A["x"].shape[0]
    with ExitStack() as ctx:
        x_all = ctx.enter_context(nc.sbuf_tensor("x_all", [S, n, D], F32))
        ident = ctx.enter_context(nc.sbuf_tensor("ident", [128, 128], F32))
        for sublayer, more in ((self_attention_0, ()), (cross_attention_0, ()), (butterfly_ffn, ()), (attentions_1, ()),
                               (experts_ffn_1, (out,))):
            with nc.cleanup_on_exit():
                sublayer(nc, nc.alloc_semaphore, n, x_all, ident, A, *more)


def shape_tables():
    import numpy as np

    c = {"ident": np.eye(128, dtype=np.float32), "number": np.arange(E, dtype=np.float32)}
    q, r = np.arange(S), np.arange(128)
    c["above"] = (q[None, :] > q[:, None] + 1).astype(np.uint32)
    c["beside"] = (q[None, :] == q[:, None] + 1).astype(np.uint32)
    c["hide"] = np.where(q[None, :] > q[:, None], np.float32(HIDDEN), np.float32(0))
    c["a_hmask"] = (((r // DK) % 8)[:, None] == np.arange(8)[None]).astype(np.float32)
    c["a_hsum"] = ((r // DK)[:, None] == np.arange(H)[None]).astype(np.float32)
    freq = 1.0 / 10000.0 ** (np.arange(0, DK, 2) / DK)
    turn, rpos = np.zeros((128, 8, S)), np.zeros((128, H, S))
    for g in range(2):
        base, rel = (slice(0, 64), 64) if g == 0 else (slice(64, 128), 0)
        turn[base, 2 * g] = 1.0
        for h in range(8):
            for d in range(DK):
                row, w = rel + h * DK + d, freq[d % 4]
                for at, angle in ((0, q * w), (4, (S + 1 + q) * w)):
                    turn[row, at + 2 * g] = -np.cos(angle) if d < 4 else np.cos(angle)
                    turn[row, at + 2 * g + 1] = np.sin(angle)
                rpos[row, 8 * g + h] = np.sin(q * w) if d < 4 else np.cos(q * w)
    c["a_turn"] = (turn * DK ** -0.5).astype(np.float32)
    c["a_rpos"] = rpos.reshape(128, H * S).astype(np.float32)
    return c


def laid_out(inputs):
    import numpy as np

    A = {k: np.asarray(v) for k, v in inputs.items() if k != "mask_BxS_ff1"}
    swap = np.arange(D).reshape(H, 2, DK // 2)[:, ::-1].reshape(-1)
    lo, hi = slice(0, 64), slice(64, 128)
    Wq, Wk = A["L0_attn_Wq"], A["L0_attn_Wk"]
    Ws = Wq[:, swap]
    A["a_wq"] = np.stack([np.concatenate(p, 1) for p in (
        (Wq[:, lo], Wq[:, lo]), (Wq[:, lo], Ws[:, lo]), (Wq[:, hi], Wq[:, hi]), (Ws[:, hi], Wq[:, hi]))] + [Wk], 1)
    u, v = A["L0_attn_u"].reshape(-1), A["L0_attn_v"].reshape(-1)
    vs = v[swap]
    A["a_ub"] = np.stack([np.concatenate(p) for p in ((u[lo], v[lo]), (v[lo], vs[lo]), (v[hi], u[hi]), (vs[hi], v[hi]))], 1)
    for new, old in (("q", "q"), ("k", "k"), ("v", "v"), ("o", "o")):
        A[f"c_w{new}T"] = A[f"L0_xattn_W{old}"].T
    A["f_wconT"] = A["L0_ffn_W_con"].T
    A["f_upb"] = A["L0_ffn_up_bias"].reshape(HID // 128, 128).T
    A["s_wvT"] = A["L1_attn_w_v"].reshape(H * DQ, D).T
    for k in ("L0_attn_Wq", "L0_attn_Wk", "L0_attn_u", "L0_attn_v", "L0_xattn_Wq", "L0_xattn_Wk", "L0_xattn_Wv", "L0_xattn_Wo",
              "L0_ffn_W_con", "L0_ffn_up_bias", "L1_attn_w_v"):
        del A[k]
    return A


def kernel(**inputs):
    import numpy as np
    import concourse.bacc as bacc
    from concourse.bass_utils import run_bass_kernel_spmd

    nc = bacc.Bacc("TRN2", target_bir_lowering=False, num_devices=1)
    arrays = {f"in_{k}": np.ascontiguousarray(v) for k, v in {**laid_out(inputs), **shape_tables()}.items()}
    A = {k[3:]: nc.dram_tensor(k, a.shape, mybir.dt.from_np(a.dtype), kind="ExternalInput").ap() for k, a in arrays.items()}
    shape = inputs["x"].shape
    out = nc.dram_tensor("out_x", shape, F32, kind="ExternalOutput").ap()
    decoder_kernel(nc, A, out)
    r = run_bass_kernel_spmd(nc, [arrays], core_ids=[0])
    return r.results[0]["out_x"]
```

```python
from contextlib import ExitStack

import concourse.bass as bass
from concourse import mybir
from concourse.alu_op_type import AluOpType as ALU

F32 = mybir.dt.float32
BF16 = mybir.dt.bfloat16
I32 = mybir.dt.int32
U32 = mybir.dt.uint32
ACT = mybir.ActivationFunctionType
AX = mybir.AxisListType.X

S = 128
D = 128
T2 = 77
T2P = 80
H = 16
DK = D // H
DQ = 64
HID = 512
NSTAGE = 9
FE = 344
E = 8
EPS = 1e-5
HIDDEN = -1e30
PEEL = 8
UNROLL = 4


def awaited(value):
    return not isinstance(value, int) or value > 0


def in_registers(eng, *values):
    for value in values:
        if not isinstance(value, int):
            eng.to_reg(value)


def rounds(eng, n, lag, body, peel=PEEL):
    def peeled(i):
        body(i, i % UNROLL, lambda k: 0 <= i - k < n)
    for i in range(peel):
        peeled(i)
    with eng.Fori(peel // UNROLL, n // UNROLL) as r:
        for u in range(UNROLL):
            body(r * UNROLL + u, u, lambda k: True)
    for i in range(n, n + lag):
        peeled(i)


def load_ahead(sp, sem, ahead):
    for dst, src in ahead:
        sp.dma_start(dst, src).then_inc(sem, 16)
    sp.wait_ge(sem, 16 * len(ahead))


def landed(i, par):
    return i * 8 + (16 - 8 * par)


def heads(ap, n):
    return ap.rearrange("p (h k) -> p h k", h=n)


def spread(ap, n, where):
    ap = ap.unsqueeze(where)
    shape = list(ap.shape)
    shape[where] = n
    return ap.broadcast_to(shape)


def norm_parts(sb, sem, p, g=1):
    return {
        "g": g,
        "stats": [sb(f"{p}_stats{k}", [S, g, 6], F32) for k in range(2)],
        "mv": [sb(f"{p}_mv{k}", [S, g, 2], F32) for k in range(2)],
        "vare": [sb(f"{p}_vare{k}", [S, g], F32) for k in range(2)],
        "rstd": [sb(f"{p}_rstd{k}", [S, g], F32) for k in range(2)],
        "power": sb(f"{p}_power", [S, g], F32),
        "power_set": sem(f"{p}_power_set"),
        "stat_done": sem(f"{p}_stat_done"),
        "mv_done": sem(f"{p}_mv_done"),
        "vare_done": sem(f"{p}_vare_done"),
        "rstd_done": sem(f"{p}_rstd_done"),
        "normed": sem(f"{p}_normed"),
    }


def norm_measure(nc, dve, norm, i, par, y):
    g = norm["g"]
    if awaited(g * (i - 1)):
        dve.wait_ge(norm["mv_done"], g * (i - 1))
    for k in range(g):
        nc.vector.bn_stats(norm["stats"][par][:, k, :], y[:, k, :]).then_inc(norm["stat_done"], 1)
    in_registers(dve, g * (i + 1), g * (i - 1), i - 1)
    dve.wait_ge(norm["power_set"], 1)
    if awaited(g * (i + 1)):
        dve.wait_ge(norm["stat_done"], g * (i + 1))
    if awaited(g * (i - 1)):
        dve.wait_ge(norm["normed"], g * (i - 1))
    if awaited(i - 1):
        dve.wait_ge(norm["vare_done"], i - 1)
    for k in range(g):
        nc.vector.bn_aggr(norm["mv"][par][:, k, :], norm["stats"][par][:, k, :]).then_inc(norm["mv_done"], 1)


def norm_start(nc, pool, norm):
    nc.gpsimd.memset(norm["power"][:], -0.5).then_inc(norm["power_set"], 1)
    pool.wait_ge(norm["power_set"], 1)


def norm_root(nc, pool, norm, i, par, own_done=None, own=0):
    in_registers(pool, norm["g"] * (i + 1), i - 1, own)
    pool.wait_ge(norm["power_set"], 1)
    if awaited(norm["g"] * (i + 1)):
        pool.wait_ge(norm["mv_done"], norm["g"] * (i + 1))
    if awaited(i - 1):
        pool.wait_ge(norm["rstd_done"], i - 1)
    if own_done is not None:
        pool.wait_ge(own_done, own)
    nc.gpsimd.tensor_scalar(norm["vare"][par][:], norm["mv"][par][:, :, 1], EPS, None, ALU.add).then_inc(norm["vare_done"], 1)
    pool.wait_ge(norm["vare_done"], i + 1)
    if awaited(norm["g"] * (i - 1)):
        pool.wait_ge(norm["normed"], norm["g"] * (i - 1))
    nc.gpsimd.tensor_tensor(norm["rstd"][par][:], norm["vare"][par][:], norm["power"][:], ALU.pow).then_inc(norm["rstd_done"], 1)


def norm_apply(nc, dve, norm, i, par, out, y):
    dve.wait_ge(norm["rstd_done"], i + 1)
    for k in range(norm["g"]):
        nc.vector.tensor_scalar(out[:, k, :], y[:, k, :], norm["mv"][par][:, k, 0:1], norm["rstd"][par][:, k:k + 1],
                                ALU.subtract, ALU.mult).then_inc(norm["normed"], 1)


def self_attention_0(nc, sem, n, x_all, ident, A, ahead):
    NQ = 4
    HQ = H // NQ
    with ExitStack() as ctx:
        def sb(name, shape, dt):
            return ctx.enter_context(nc.sbuf_tensor(name, shape, dt))

        def psum(name, shape):
            return ctx.enter_context(nc.psum_tensor(name, shape, F32))

        wq = sb("a_wq", [D, 5, 128], F32)
        wv = sb("a_wv", [D, D], F32)
        wo = sb("a_wo", [D, D], F32)
        bo = sb("a_bo", [S, D], F32)
        ub = sb("a_ub", [128, 4], F32)
        turn = sb("a_turn", [128, 8, S], F32)
        hmask = sb("a_hmask", [128, 8], F32)
        hsum = sb("a_hsum", [128, H], F32)
        above = sb("a_above", [S, S], U32)
        beside = sb("a_beside", [S, S], U32)
        xs = [sb(f"a_xs{k}", [S, D], F32) for k in range(2)]
        xT = [sb(f"a_xT{k}", [D, S], F32) for k in range(2)]
        kT = [sb(f"a_kT{k}", [D, S], F32) for k in range(2)]
        kr = [sb(f"a_kr{k}", [128, H * S], F32) for k in range(2)]
        vp = [sb(f"a_vp{k}", [S, H, 32], F32) for k in range(4)]
        ql = [sb(f"a_ql{k}", [128, 2, S], F32) for k in range(2)]
        qu = [sb(f"a_qu{k}", [128, 2, S], F32) for k in range(2)]
        t1 = sb("a_t1", [128, 4, S], F32)
        qb = sb("a_qb", [128, 4, S], F32)
        t2 = sb("a_t2", [128, 4, S], F32)
        pr = [sb(f"a_pr{k}", [128, S], F32) for k in range(2)]
        nmx = [sb(f"a_nmx{k}", [S, HQ], F32) for k in range(NQ)]
        pe_ = [sb(f"a_pe{k}", [S, HQ * S], F32) for k in range(NQ)]
        bs = [sb(f"a_bs{k}", [S, H], F32) for k in range(2)]
        pT = [sb(f"a_pT{k}", [S, HQ * S], F32) for k in range(2)]
        avs = sb("a_avs", [128, 4, S], F32)
        rden = sb("a_rden", [S, H], F32)
        att = sb("a_att", [S, D], F32)
        attT = sb("a_attT", [D, S], F32)
        y = [sb(f"a_y{k}", [S, D], F32) for k in range(2)]
        y2 = [sb(f"a_y2{k}", [S, D], F32) for k in range(2)]
        norm = norm_parts(sb, sem, "a")

        pS = [psum(f"a_pS{k}", [128, 512]) for k in range(2)]
        pU = psum("a_pU", [128, 512])
        pT_ = psum("a_pT_", [128, 512])
        pA = psum("a_pA", [128, 512])
        pO = psum("a_pO", [128, 512])
        pQ = psum("a_pQ", [128, 512])
        pW = psum("a_pW", [128, 512])
        pxT, pkT, pv, pB = pW[:, 0:128], pW[:, 128:256], pW[:, 256:384], pW[:, 384:384 + H]

        s_w = sem("a_weights")
        s_set = sem("a_set")
        s_x = [sem(f"a_x_loaded{k}") for k in range(2)]
        s_xTp = sem("a_xT_in_psum")
        s_xT = sem("a_xT_ready")
        s_kvp = sem("a_kv_in_psum")
        s_kT = sem("a_kT_ready")
        s_v = sem("a_v_ready")
        s_qp = sem("a_q_in_psum")
        s_t = sem("a_turned_parts")
        s_ql = sem("a_ql_ready")
        s_ub = sem("a_biased_queries")
        s_tm = sem("a_turned_parts_above")
        s_qu = sem("a_qu_turned")
        s_kr = sem("a_kr_ready")
        s_pr = sem("a_products")
        s_B = sem("a_beside_scores")
        s_su = sem("a_scores")
        s_pu = sem("a_above_put")
        s_pe = sem("a_beside_put")
        s_mx = sem("a_max")
        s_Bc = sem("a_beside_copied")
        s_ex = sem("a_probs")
        s_tp = sem("a_probsT_in_psum")
        s_pT = sem("a_probsT")
        s_av = sem("a_values_mixed")
        s_avs = sem("a_mixed_copied")
        s_ot = sem("a_mixed_turned")
        s_rd = sem("a_den_inverse")
        s_at = sem("a_att_normed")
        s_atp = sem("a_attT_in_psum")
        s_atT = sem("a_attT")
        s_wo = sem("a_projected")
        s_y = sem("a_y")
        s_y2 = sem("a_y2")
        s_qb = sem("a_qu_base")
        s_ini = sem("a_rows_loaded")
        s_zero = sem("a_zeroed")
        s_rest = sem("a_later_rows_loaded")
        s_ahead = sem("a_ahead")
        NW = 12

        block = ctx.enter_context(nc.Block())

        @block.sync
        def _(sp):
            for dst, src in ((ident[:], A["ident"]), (wq[:], A["a_wq"]), (wv[:], A["L0_attn_Wv"]),
                             (wo[:], A["L0_attn_Wo"]), (ub[:], A["a_ub"]), (turn[:], A["a_turn"]),
                             (hmask[:], A["a_hmask"]), (hsum[:], A["a_hsum"]), (above[:], A["above"]),
                             (beside[:], A["beside"]), (bo[:], A["L0_attn_bo"].unsqueeze(0).broadcast_to([S, D]))):
                sp.dma_start(dst, src).then_inc(s_w, 16)
            for k in range(2):
                sp.dma_start(kr[k][:], A["a_rpos"]).then_inc(s_ini, 16)
            x = A["x"].rearrange("b s d -> s b d")
            sp.dma_start(x_all[:, 0:PEEL, :], x[:, 0:PEEL, :]).then_inc(s_w, 16)
            sp.wait_ge(s_w, 16 * NW)

            def body(i, u, on):
                par = u % 2
                if awaited(i - 1):
                    sp.wait_ge(s_xTp, i - 1)
                sp.dma_start(xs[par][:], x_all[:, bass.ds(i, 1), :].rearrange("s b d -> s (b d)")).then_inc(s_x[par], 16)
                if isinstance(i, int) and i == PEEL - 1:
                    sp.dma_start(x_all[:, PEEL:n, :], x[:, PEEL:n, :]).then_inc(s_rest, 16)
                    sp.wait_ge(s_rest, 16)
            rounds(sp, n, 0, body)
            load_ahead(sp, s_ahead, ahead)

        @block.tensor
        def _(pe):
            pe.wait_ge(s_w, 16 * NW)
            pe.wait_ge(s_set, 4)

            def scores(a, par, c):
                g, half = c // 2, c % 2
                if c == 0:
                    pe.wait_ge(s_ql, a + 1)
                    pe.wait_ge(s_qb, 2 * a + 2)
                if half == 0:
                    pe.wait_ge(s_qu, 2 * a + g + 1)
                    pe.wait_ge(s_kr, 2 * a + g + 1)
                if awaited(4 * a + c - 1):
                    pe.wait_ge(s_ex, 4 * a + c - 1)
                nc.tensor.matmul(pS[c % 2][:], ql[par][:, g, :], kr[par][:, c * 512:(c + 1) * 512],
                                 start=True, stop=True)
                if awaited(4 * a + c):
                    pe.wait_ge(s_pu, 4 * a + c)
                nc.tensor.matmul(pU[:], qu[par][:, g, :], kr[par][:, c * 512:(c + 1) * 512],
                                 start=True, stop=True).then_inc(s_su, 1)

            def turn_probs(a, c):
                pe.wait_ge(s_ex, 4 * a + c + 1)
                if awaited(4 * a + c):
                    pe.wait_ge(s_pT, 4 * a + c)
                for j in range(HQ):
                    last = nc.tensor.transpose(pT_[:, j * S:(j + 1) * S], pe_[c][:, j * S:(j + 1) * S], ident[:])
                last.then_inc(s_tp, 1)

            def mix(a, v, c):
                pe.wait_ge(s_pT, 4 * a + c + 1)
                if c == 0:
                    pe.wait_ge(s_v, a + 1)
                    if awaited(a):
                        pe.wait_ge(s_avs, a)
                for j in range(HQ):
                    last = nc.tensor.matmul(pA[32 * j:32 * j + 32, c * S:(c + 1) * S], v[:, 4 * c + j, :],
                                            pT[c % 2][:, j * S:(j + 1) * S], start=True, stop=True)
                last.then_inc(s_av, 1)

            def body(i, u, on):
                par = u % 2
                a, t, z, q = i - 1, i - 2, i - 3, 1 - par
                v1, v2 = vp[(u + 3) % 4], vp[(u + 2) % 4]
                if on(1):
                    scores(a, q, 0)
                if on(2):
                    mix(t, v2, 1)
                if on(0):
                    pe.wait_ge(s_x[par], landed(i, par))
                    if awaited(i):
                        pe.wait_ge(s_Bc, i)
                    nc.tensor.transpose(pxT, xs[par][:], ident[:]).then_inc(s_xTp, 1)
                if on(2):
                    turn_probs(t, 2)
                if on(1):
                    scores(a, q, 1)
                if on(0):
                    pe.wait_ge(s_xT, i + 1)
                    nc.tensor.matmul(pkT, wq[:, 4, :], xT[par][:], start=True, stop=True)
                    nc.tensor.matmul(pv, xT[par][:], wv[:], start=True, stop=True).then_inc(s_kvp, 1)
                if on(2):
                    turn_probs(t, 3)
                if on(2):
                    mix(t, v2, 2)
                if on(0):
                    if awaited(4 * i):
                        pe.wait_ge(s_t, 4 * i)
                    if awaited(i):
                        pe.wait_ge(s_ub, i)
                    for m in range(4):
                        last = nc.tensor.matmul(pQ[:, m * S:(m + 1) * S], wq[:, m, :], xT[par][:],
                                                start=True, stop=True)
                    last.then_inc(s_qp, 1)
                if on(1):
                    scores(a, q, 2)
                if on(3):
                    pe.wait_ge(s_at, z + 1)
                    nc.tensor.transpose(pO[:, 0:128], att[:], ident[:]).then_inc(s_atp, 1)
                if on(1):
                    turn_probs(a, 0)
                if on(2):
                    mix(t, v2, 3)
                if on(3):
                    pe.wait_ge(s_atT, z + 1)
                    nc.tensor.matmul(pO[:, 128:256], attT[:], wo[:], start=True, stop=True).then_inc(s_wo, 1)
                if on(1):
                    scores(a, q, 3)
                if on(1):
                    turn_probs(a, 1)
                if on(1):
                    mix(a, v1, 0)
                if on(0):
                    pe.wait_ge(s_pr, 2 * i + 2)
                    pe.wait_ge(s_kT, i + 1)
                    pe.wait_ge(s_v, i + 1)
                    nc.tensor.matmul(pB, pr[par][:], hsum[:], start=True, stop=True).then_inc(s_B, 1)
                if on(2):
                    pe.wait_ge(s_avs, t + 1)
                    if awaited(t):
                        pe.wait_ge(s_y, t)
                    for c in range(4):
                        last = nc.tensor.transpose(pO[:, c * S:(c + 1) * S], avs[:, c, :], ident[:])
                    last.then_inc(s_ot, 1)
            rounds(pe, n, 3, body)

        @block.vector
        def _(dve):
            dve.wait_ge(s_w, 16 * NW)
            dve.wait_ge(s_set, 4)

            def soften(a, par, c):
                s3 = heads(pS[c % 2][:], HQ)
                in_registers(dve, 4 * a + c + 1)
                dve.wait_ge(s_set, 4)
                dve.wait_ge(s_su, 4 * a + c + 1)
                nc.vector.copy_predicated(s3, spread(above[:], HQ, 1), heads(pU[:], HQ)).then_inc(s_pu, 1)
                in_registers(dve, 4 * a + c + 1, a + 1)
                dve.wait_ge(s_set, 4)
                dve.wait_ge(s_pu, 4 * a + c + 1)
                dve.wait_ge(s_Bc, a + 1)
                nc.vector.copy_predicated(s3, spread(beside[:], HQ, 1),
                                          spread(bs[par][:, 4 * c:4 * c + 4], S, 2)).then_inc(s_pe, 1)
                dve.wait_ge(s_pe, 4 * a + c + 1)
                if awaited(4 * a + c - 3):
                    dve.wait_ge(s_ex, 4 * a + c - 3)
                nc.vector.tensor_reduce(nmx[c][:], s3, AX, ALU.max, negate=True).then_inc(s_mx, 1)

            def body(i, u, on):
                par = u % 2
                a, z, w, q = i - 1, i - 3, i - 4, 1 - par
                if on(3):
                    dve.wait_ge(s_ot, z + 1)
                    o4 = pO[:].rearrange("p (h e) -> p h e", h=H)
                    nc.vector.reciprocal(rden[:], o4[:, :, DK]).then_inc(s_rd, 1)
                    dve.wait_ge(s_rd, z + 1)
                    if awaited(z):
                        dve.wait_ge(s_atp, z)
                    nc.vector.tensor_tensor(heads(att[:], H), o4[:, :, 0:DK], spread(rden[:], DK, 2),
                                            ALU.mult).then_inc(s_at, 1)
                if on(1):
                    soften(a, q, 0)
                if on(4):
                    norm_apply(nc, dve, norm, w, par, x_all[:, bass.ds(w, 1), :], y2[par][:].unsqueeze(1))
                if on(1):
                    soften(a, q, 1)
                if on(0):
                    dve.wait_ge(s_qp, i + 1)
                    if awaited(i):
                        dve.wait_ge(s_ql, i)
                    for k in range(4):
                        nc.vector.scalar_tensor_tensor(t1[:, k, :], pQ[:, k * S:(k + 1) * S], ub[:, k:k + 1], turn[:, k, :],
                                                       ALU.add, ALU.mult).then_inc(s_t, 1)
                    dve.wait_ge(s_t, 4 * i + 4)
                    if awaited(4 * (i - 1)):
                        dve.wait_ge(s_su, 4 * (i - 1))
                    if awaited(2 * (i - 1)):
                        dve.wait_ge(s_pr, 2 * (i - 1))
                    t4 = t1[:].rearrange("p (g m) q -> p g m q", g=2)
                    nc.vector.tensor_tensor(ql[par][:], t4[:, :, 0, :], t4[:, :, 1, :], ALU.add).then_inc(s_ql, 1)
                if on(1):
                    soften(a, q, 2)
                if on(3):
                    dve.wait_ge(s_wo, z + 1)
                    if awaited(z - 1):
                        dve.wait_ge(s_y2, z - 1)
                    nc.vector.tensor_tensor(y[q][:], pO[:, 128:256], x_all[:, bass.ds(z, 1), :].rearrange("s b d -> s (b d)"),
                                            ALU.add).then_inc(s_y, 1)
                    dve.wait_ge(s_y, z + 1)
                    if awaited(z - 1):
                        dve.wait_ge(norm["normed"], z - 1)
                    nc.vector.tensor_tensor(y2[q][:], y[q][:], bo[:], ALU.add).then_inc(s_y2, 1)
                    dve.wait_ge(s_y2, z + 1)
                    norm_measure(nc, dve, norm, z, q, y2[q][:].unsqueeze(1))
                if on(1):
                    soften(a, q, 3)
            rounds(dve, n, 4, body)

        @block.scalar
        def _(act):
            act.wait_ge(s_set, 4)

            def probs(a, c):
                act.wait_ge(s_mx, 4 * a + c + 1)
                if awaited(4 * a + c - 3):
                    act.wait_ge(s_tp, 4 * a + c - 3)
                for j in range(HQ):
                    last = nc.scalar.activation(pe_[c][:, j * S:(j + 1) * S], pS[c % 2][:, j * S:(j + 1) * S], ACT.Exp,
                                                bias=nmx[c][:, j:j + 1])
                last.then_inc(s_ex, 1)

            def probsT(a, c):
                act.wait_ge(s_tp, 4 * a + c + 1)
                if awaited(4 * a + c - 1):
                    act.wait_ge(s_av, 4 * a + c - 1)
                nc.scalar.copy(pT[c % 2][:], pT_[:]).then_inc(s_pT, 1)

            def body(i, u, on):
                par = u % 2
                a, t, z = i - 1, i - 2, i - 3
                if on(0):
                    act.wait_ge(s_xTp, i + 1)
                    if awaited(i - 1):
                        act.wait_ge(s_qp, i - 1)
                    nc.scalar.copy(xT[par][:], pxT).then_inc(s_xT, 1)
                if on(2):
                    probsT(t, 2)
                if on(1):
                    probs(a, 0)
                if on(0):
                    act.wait_ge(s_kvp, i + 1)
                    if awaited(2 * (i - 1)):
                        act.wait_ge(s_kr, 2 * (i - 1))
                    if awaited(2 * (i - 1)):
                        act.wait_ge(s_pr, 2 * (i - 1))
                    nc.scalar.copy(kT[par][:], pkT).then_inc(s_kT, 1)
                    if awaited(4 * (i - 3)):
                        act.wait_ge(s_av, 4 * (i - 3))
                    nc.scalar.copy(vp[u][:, :, 0:DK], heads(pv, H)).then_inc(s_v, 1)
                if on(2):
                    probsT(t, 3)
                if on(1):
                    probs(a, 1)
                if on(3):
                    act.wait_ge(s_atp, z + 1)
                    if awaited(z):
                        act.wait_ge(s_wo, z)
                    nc.scalar.copy(attT[:], pO[:, 0:128]).then_inc(s_atT, 1)
                if on(1):
                    probsT(a, 0)
                if on(2):
                    act.wait_ge(s_av, 4 * t + 4)
                    if awaited(t):
                        act.wait_ge(s_ot, t)
                    nc.scalar.copy(avs[:], heads(pA[:], 4)).then_inc(s_avs, 1)
                if on(0):
                    act.wait_ge(s_t, 4 * i + 4)
                    if awaited(2 * i):
                        act.wait_ge(s_tm, 2 * i)
                    for k in range(4):
                        rel = slice(64, 128) if k < 2 else slice(0, 64)
                        last = nc.scalar.activation(qb[rel, k, :], pQ[rel, k * S:(k + 1) * S], ACT.Identity, bias=ub[rel, k:k + 1])
                    last.then_inc(s_ub, 1)
                if on(1):
                    probs(a, 2)
                if on(1):
                    probsT(a, 1)
                if on(0):
                    act.wait_ge(s_B, i + 1)
                    if awaited(4 * (i - 1)):
                        act.wait_ge(s_pe, 4 * (i - 1))
                    nc.scalar.copy(bs[par][:], pB).then_inc(s_Bc, 1)
                if on(1):
                    probs(a, 3)
            rounds(act, n, 3, body)

        @block.gpsimd
        def _(pool):
            norm_start(nc, pool, norm)
            for k in range(2):
                nc.gpsimd.memset(pr[k][:], 0.0).then_inc(s_zero, 1)
                nc.gpsimd.memset(qu[k][:], 0.0).then_inc(s_zero, 1)
            for k in range(4):
                nc.gpsimd.memset(vp[k][:], 0.0).then_inc(s_zero, 1)
            pool.wait_ge(s_zero, 8)
            pool.wait_ge(s_ini, 32)
            pool.wait_ge(s_w, 16 * NW)
            for k in range(4):
                nc.gpsimd.memset(vp[k][:, :, DK:DK + 1], 1.0).then_inc(s_set, 1)

            def keys(i, par, g):
                r = slice(64 * g, 64 * g + 64)
                nc.gpsimd.tensor_tensor(heads(kr[par][r, g * 1024:(g + 1) * 1024], 8), spread(kT[par][r, :], 8, 1),
                                        spread(hmask[r, :], S, 2), ALU.mult).then_inc(s_kr, 1)

            def above_rows(i, par, g):
                rel = slice(64, 128) if g == 0 else slice(0, 64)
                nc.gpsimd.tensor_tensor(t2[rel, 2 * g:2 * g + 2, 0:S - 1], qb[rel, 2 * g:2 * g + 2, 1:S],
                                        turn[rel, 4 + 2 * g:6 + 2 * g, 0:S - 1], ALU.mult).then_inc(s_tm, 1)
                pool.wait_ge(s_tm, 2 * i + g + 1)
                nc.gpsimd.tensor_tensor(qu[par][rel, g, 0:S - 1], t2[rel, 2 * g, 0:S - 1], t2[rel, 2 * g + 1, 0:S - 1],
                                        ALU.add).then_inc(s_qu, 1)

            def body(i, u, on):
                par = u % 2
                z, q = i - 3, 1 - par
                if on(0):
                    pool.wait_ge(s_kT, i + 1)
                    if awaited(4 * (i - 1)):
                        pool.wait_ge(s_su, 4 * (i - 1))
                    if awaited(i - 3):
                        pool.wait_ge(norm["rstd_done"], i - 3)
                    if awaited(2 * i):
                        pool.wait_ge(s_kr, 2 * i)
                    keys(i, par, 0)
                    pool.wait_ge(s_ql, i + 1)
                    if awaited(i - 1):
                        pool.wait_ge(s_B, i - 1)
                    pool.wait_ge(s_kr, 2 * i + 1)
                    for g in range(2):
                        r = slice(64 * g, 64 * g + 64)
                        if awaited(2 * i + g):
                            pool.wait_ge(s_qb, 2 * i + g)
                        nc.gpsimd.tensor_tensor(pr[par][r, 0:S - 1], ql[par][r, g, 0:S - 1], kT[par][r, 1:S],
                                                ALU.mult).then_inc(s_pr, 1)
                        in_registers(pool, 2 * i + g + 1)
                        pool.wait_ge(s_zero, 8)
                        pool.wait_ge(s_pr, 2 * i + g + 1)
                        nc.gpsimd.tensor_copy(qu[par][r, g, :], ql[par][r, g, :]).then_inc(s_qb, 1)
                    pool.wait_ge(s_qb, 2 * i + 2)
                    pool.wait_ge(s_ub, i + 1)
                    if awaited(2 * i):
                        pool.wait_ge(s_qu, 2 * i)
                    above_rows(i, par, 0)
                    pool.wait_ge(s_qu, 2 * i + 1)
                    keys(i, par, 1)
                    pool.wait_ge(s_kr, 2 * i + 2)
                    above_rows(i, par, 1)
                if on(3):
                    norm_root(nc, pool, norm, z, q, s_qu if on(0) else None, 2 * i + 2 if on(0) else 0)
            rounds(pool, n, 3, body)


def cross_0_weights(sb, A):
    w = sb("c_w", [D, 4, D])
    bq, bv, bo = sb("c_bq", [D, 1]), sb("c_bv", [D, 1]), sb("c_bo", [S, D])
    return (w, bq, bv, bo), (
        *((w[:, k, :], A[name]) for k, name in enumerate(("c_wqT", "c_wkT", "c_wvT", "c_woT"))),
        (bq[:], A["L0_xattn_bq"].unsqueeze(1)), (bv[:], A["L0_xattn_bv"].unsqueeze(1)),
        (bo[:], A["L0_xattn_bo"].unsqueeze(0).broadcast_to([S, D])))


def cross_attention_0(nc, sem, n, x_all, ident, A, weights):
    SCALE = float(D) ** -0.5
    with ExitStack() as ctx:
        def sb(name, shape, dt=F32):
            return ctx.enter_context(nc.sbuf_tensor(name, shape, dt))

        def pair(name, shape):
            return [sb(f"{name}{k}", shape) for k in range(2)]

        def bank(name):
            return ctx.enter_context(nc.psum_tensor(name, [128, 512], F32))

        w, bq, bv, bo = weights
        xs, cs = pair("c_xs", [S, D]), pair("c_cs", [T2, D])
        xT, cT = pair("c_xT", [D, S]), pair("c_cT", [D, 128])
        qT, kT = pair("c_qT", [D, S]), pair("c_kT", [D, 128])
        v = [sb(f"c_v{k}", [T2, D]) for k in range(4)]
        mx, nm, den, rden = pair("c_mx", [S, 1]), pair("c_nm", [S, 1]), pair("c_den", [S, 1]), pair("c_rden", [S, 1])
        ex, pn = pair("c_ex", [S, T2]), pair("c_pn", [S, T2])
        pT, oT = pair("c_pT", [T2, S]), pair("c_oT", [D, S])
        y, y2 = pair("c_y", [S, 1, D]), pair("c_y2", [S, 1, D])
        norm = norm_parts(sb, sem, "c")
        pX, pQ, pS, pP, pM, pO = (bank(f"c_p{k}") for k in "XQSPMO")

        s_set = sem("c_set")
        s_x = [sem(f"c_loaded{k}") for k in range(2)]
        s_xp, s_xT, s_cT = sem("c_xcT_in_psum"), sem("c_xT"), sem("c_cT")
        s_qp, s_q, s_k, s_v = sem("c_qkv_in_psum"), sem("c_q"), sem("c_k"), sem("c_v_ready")
        s_s, s_mx, s_nm, s_ex, s_rd, s_pn = (sem(f"c_{k}") for k in ("scores", "max", "negmax", "exp", "rden", "probs"))
        s_pp, s_pT, s_mp, s_oT, s_op, s_y, s_y2 = (sem(f"c_{k}") for k in (
            "pT_in_psum", "pT_ready", "mixed_in_psum", "mixed", "out_in_psum", "y_ready", "y2_ready"))

        block = ctx.enter_context(nc.Block())

        @block.sync
        def _(sp):
            def body(i, u, on):
                par = u % 2
                if awaited(i - 1):
                    sp.wait_ge(s_xp, i - 1)
                sp.dma_start(xs[par][:], x_all[:, bass.ds(i, 1), :].rearrange("s b d -> s (b d)")).then_inc(s_x[par], 16)
                sp.dma_start(cs[par][:], A["ctx_1024"][bass.ds(i, 1), :, :].rearrange("b t d -> (b t) d")).then_inc(s_x[par], 16)
            rounds(sp, n, 0, body, 8)

        @block.tensor
        def _(pe):
            pe.wait_ge(s_set, 2)

            def body(i, u, on):
                par = u % 2
                q = 1 - par
                if on(5):
                    t = i - 5
                    pe.wait_ge(s_oT, t + 1)
                    if awaited(t):
                        pe.wait_ge(s_y, t)
                    nc.tensor.matmul(pO[:, 0:D], oT[q][:], w[:, 3, :], start=True, stop=True).then_inc(s_op, 1)
                if on(4):
                    t = i - 4
                    pe.wait_ge(s_pT, t + 1)
                    if awaited(t):
                        pe.wait_ge(s_oT, t)
                    nc.tensor.matmul(pM[:, 0:S], v[u][:], pT[par][:], start=True, stop=True).then_inc(s_mp, 1)
                if on(2):
                    t = i - 2
                    pe.wait_ge(s_q, t + 1)
                    pe.wait_ge(s_k, t + 1)
                    if awaited(t):
                        pe.wait_ge(s_ex, t)
                    nc.tensor.matmul(pS[:, 0:128], qT[par][:], kT[par][:], start=True, stop=True).then_inc(s_s, 1)
                if on(3):
                    t = i - 3
                    pe.wait_ge(s_pn, t + 1)
                    if awaited(t):
                        pe.wait_ge(s_pT, t)
                    nc.tensor.transpose(pP[0:T2, 0:S], pn[q][:], ident[:]).then_inc(s_pp, 1)
                if on(1):
                    t = i - 1
                    pe.wait_ge(s_xT, t + 1)
                    pe.wait_ge(s_cT, t + 1)
                    if awaited(t):
                        pe.wait_ge(s_v, t)
                    nc.tensor.matmul(pQ[:, 0:128], w[:, 0, :], xT[q][:], start=True, stop=True)
                    nc.tensor.matmul(pQ[:, 128:256], w[:, 1, :], cT[q][:], start=True, stop=True)
                    nc.tensor.matmul(pQ[0:T2, 256:384], cT[q][:, 0:T2], w[:, 2, :], start=True, stop=True).then_inc(s_qp, 1)
                if on(0):
                    pe.wait_ge(s_x[par], landed(i, par) * 2)
                    if awaited(i):
                        pe.wait_ge(s_cT, i)
                    nc.tensor.transpose(pX[:, 0:S], xs[par][:], ident[:])
                    nc.tensor.transpose(pX[:, S:S + T2], cs[par][:], ident[0:T2, 0:T2]).then_inc(s_xp, 1)
            rounds(pe, n, 5, body, 8)

        @block.scalar
        def _(act):
            act.wait_ge(s_set, 2)

            def body(i, u, on):
                par = u % 2
                q = 1 - par
                if on(4):
                    t = i - 4
                    act.wait_ge(s_mp, t + 1)
                    if awaited(t - 1):
                        act.wait_ge(s_op, t - 1)
                    nc.scalar.activation(oT[par][:], pM[:, 0:S], ACT.Identity, bias=bv[:]).then_inc(s_oT, 1)
                if on(3):
                    t = i - 3
                    act.wait_ge(s_pp, t + 1)
                    if awaited(t - 1):
                        act.wait_ge(s_mp, t - 1)
                    nc.scalar.copy(pT[q][:], pP[0:T2, 0:S]).then_inc(s_pT, 1)
                if on(2):
                    t = i - 2
                    act.wait_ge(s_nm, t + 1)
                    if awaited(t - 1):
                        act.wait_ge(s_pn, t - 1)
                    if awaited(t - 1):
                        act.wait_ge(s_rd, t - 1)
                    nc.scalar.activation(ex[par][:], pS[:, 0:T2], ACT.Exp, bias=nm[par][:], scale=SCALE,
                                         accum_out=den[par][:]).then_inc(s_ex, 1)
                if on(1):
                    t = i - 1
                    act.wait_ge(s_qp, t + 1)
                    if awaited(t - 1):
                        act.wait_ge(s_s, t - 1)
                    nc.scalar.activation(qT[q][:], pQ[:, 0:128], ACT.Identity, bias=bq[:]).then_inc(s_q, 1)
                    nc.scalar.copy(kT[q][:], pQ[:, 128:256]).then_inc(s_k, 1)
                    if awaited(t - 3):
                        act.wait_ge(s_mp, t - 3)
                    nc.scalar.copy(v[(u - 1) % 4][:], pQ[0:T2, 256:384]).then_inc(s_v, 1)
                if on(0):
                    act.wait_ge(s_xp, i + 1)
                    if awaited(i - 1):
                        act.wait_ge(s_qp, i - 1)
                    nc.scalar.copy(xT[par][:], pX[:, 0:S]).then_inc(s_xT, 1)
                    nc.scalar.copy(cT[par][:, 0:T2], pX[:, S:S + T2]).then_inc(s_cT, 1)
            rounds(act, n, 5, body, 8)

        @block.vector
        def _(dve):

            def body(i, u, on):
                par = u % 2
                q = 1 - par
                if on(3):
                    t = i - 3
                    dve.wait_ge(s_ex, t + 1)
                    if awaited(t - 1):
                        dve.wait_ge(s_pn, t - 1)
                    nc.vector.reciprocal(rden[q][:], den[q][:]).then_inc(s_rd, 1)
                    dve.wait_ge(s_rd, t + 1)
                    if awaited(t - 1):
                        dve.wait_ge(s_pp, t - 1)
                    nc.vector.tensor_scalar(pn[q][:], ex[q][:], rden[q][:], None, ALU.mult).then_inc(s_pn, 1)
                if on(2):
                    t = i - 2
                    dve.wait_ge(s_s, t + 1)
                    nc.vector.tensor_reduce(mx[par][:], pS[:, 0:T2], AX, ALU.max).then_inc(s_mx, 1)
                    dve.wait_ge(s_mx, t + 1)
                    if awaited(t - 1):
                        dve.wait_ge(s_ex, t - 1)
                    nc.vector.tensor_scalar(nm[par][:], mx[par][:], -SCALE, None, ALU.mult).then_inc(s_nm, 1)
                if on(6):
                    t = i - 6
                    norm_apply(nc, dve, norm, t, par, x_all[:, bass.ds(t, 1), :], y2[par][:])
                if on(5):
                    t = i - 5
                    dve.wait_ge(s_op, t + 1)
                    if awaited(t - 1):
                        dve.wait_ge(s_y2, t - 1)
                    nc.vector.tensor_tensor(y[q][:, 0, :], pO[:, 0:D], x_all[:, bass.ds(t, 1), :].rearrange("s b d -> s (b d)"),
                                            ALU.add).then_inc(s_y, 1)
                    dve.wait_ge(s_y, t + 1)
                    if awaited(t - 1):
                        dve.wait_ge(norm["normed"], t - 1)
                    nc.vector.tensor_tensor(y2[q][:, 0, :], y[q][:, 0, :], bo[:], ALU.add).then_inc(s_y2, 1)
                    dve.wait_ge(s_y2, t + 1)
                    norm_measure(nc, dve, norm, t, q, y2[q][:])
            rounds(dve, n, 6, body, 8)

        @block.gpsimd
        def _(pool):
            norm_start(nc, pool, norm)
            for k in range(2):
                nc.gpsimd.memset(cT[k][:], 0.0).then_inc(s_set, 1)

            def body(i, u, on):
                par = u % 2
                if on(5):
                    norm_root(nc, pool, norm, i - 5, 1 - par)
            rounds(pool, n, 6, body, 8)

def butterfly_weights(nc, sem, ident, A, w1, b1, w2, b2):
    with ExitStack() as ctx:
        def sb(name, shape, dt=F32):
            return ctx.enter_context(nc.sbuf_tensor(name, shape, dt))

        RING = 3
        wr = {k: [sb(f"b_w{k}{j}", [128, 2 * HID]) for j in range(RING)] for k in "ud"}
        row = {"u": [sb(f"b_u{j}", [128, 2, HID]) for j in range(2)], "d": [sb(f"b_d{j}", [128, 1, HID]) for j in range(2)]}
        tmp = {k: sb(f"b_t{k}", [128, 2, 2, HID]) for k in "ud"}
        bias = sb("b_bias", [128, 2, D])
        upb = sb("b_upb", [128, HID // 128])
        ones = sb("b_ones", [1, 1])
        p1 = ctx.enter_context(nc.psum_tensor("b_p1", [128, 512], F32))
        p2 = ctx.enter_context(nc.psum_tensor("b_p2", [128, 512], F32))
        s_in = sem("b_inputs")
        s_w = {k: [sem(f"b_w_{k}{j}") for j in range(RING)] for k in "ud"}
        s_mul = {k: sem(f"b_products_{k}") for k in "ud"}
        s_add = {k: sem(f"b_stage_{k}") for k in "ud"}
        s_cp, s_one, s_t, s_up, s_b2 = sem("b_w1_copied"), sem("b_one"), sem("b_turned"), sem("b_up_bias"), sem("b_out")
        nrow = {"u": 2, "d": 1}
        block = ctx.enter_context(nc.Block())

        def stage(k, n):
            return n if k == "u" else NSTAGE - 1 - n

        @block.sync
        def _(sp):
            sp.dma_start(row["u"][0][:, 0, :], A["L0_ffn_W_exp"]).then_inc(s_in, 16)
            sp.dma_start(row["u"][0][:, 1, :], A["L0_ffn_b_exp"].unsqueeze(0).broadcast_to([128, HID])).then_inc(s_in, 16)
            sp.dma_start(row["d"][0][:, 0, :], A["f_wconT"]).then_inc(s_in, 16)
            sp.dma_start(bias[:, 0, :], A["L0_ffn_b_con"].unsqueeze(0).broadcast_to([128, D])).then_inc(s_in, 16)
            sp.dma_start(bias[:, 1, :], A["L0_ffn_down_bias"].unsqueeze(0).broadcast_to([128, D])).then_inc(s_in, 16)
            sp.dma_start(upb[:], A["f_upb"]).then_inc(s_in, 16)
            for n in range(NSTAGE):
                for k, name in (("u", "L0_ffn_up_weights"), ("d", "L0_ffn_down_weights")):
                    if n >= RING:
                        sp.wait_ge(s_mul[k], 2 * nrow[k] * (n - RING + 1))
                    src = A[name][stage(k, n)].rearrange("p i j -> (p i j)").unsqueeze(0).broadcast_to([128, 2 * HID])
                    sp.dma_start(wr[k][n % RING][:], src).then_inc(s_w[k][n % RING], 16)

        def stages(eng, ops, k):
            R = nrow[k]
            eng.wait_ge(s_in, 16 * 6)
            for n in range(NSTAGE):
                st = 2 ** stage(k, n)
                nb = HID // (2 * st)
                w = wr[k][n % RING][:].rearrange("p (b s i j) -> p b s i j", b=nb, s=st, i=2)
                eng.wait_ge(s_w[k][n % RING], 16 * (n // RING + 1))
                if n >= 1:
                    eng.wait_ge(s_add[k], R * n)
                for r in range(R):
                    pairs = row[k][n % 2][:, r, :].rearrange("p (b w s) -> p b w s", b=nb, w=2)
                    for j in range(2):
                        wj = (w[:, :, :, :, j] if k == "u" else w[:, :, :, j, :]).rearrange("p b s i -> p b i s")
                        out = tmp[k][:, r, j, :].rearrange("p (b i s) -> p b i s", b=nb, i=2)
                        ops.tensor_tensor(out, pairs[:, :, j:j + 1, :].broadcast_to([128, nb, 2, st]), wj,
                                          ALU.mult).then_inc(s_mul[k], 1)
                eng.wait_ge(s_mul[k], 2 * R * (n + 1))
                for r in range(R):
                    ops.tensor_tensor(row[k][(n + 1) % 2][:, r, :], tmp[k][:, r, 0, :], tmp[k][:, r, 1, :],
                                      ALU.add).then_inc(s_add[k], 1)

        @block.vector
        def _(dve):
            nc.vector.memset(ones[:], 1.0).then_inc(s_one, 1)
            stages(dve, nc.vector, "u")
            dve.wait_ge(s_add["u"], 2 * NSTAGE)
            nc.vector.tensor_copy(w1[:], row["u"][NSTAGE % 2][:, 0, :]).then_inc(s_cp, 1)
            dve.wait_ge(s_t, 1)
            nc.vector.tensor_tensor(b1[:], p1[:, 0:4], upb[:], ALU.add).then_inc(s_up, 1)

        @block.gpsimd
        def _(pool):
            stages(pool, nc.gpsimd, "d")
            nc.gpsimd.tensor_tensor(b2[:], bias[:, 0, :], bias[:, 1, :], ALU.add).then_inc(s_b2, 1)

        @block.tensor
        def _(pe):
            pe.wait_ge(s_one, 1)
            pe.wait_ge(s_add["u"], 2 * NSTAGE)
            for c in range(4):
                last = nc.tensor.matmul(p1[:, c:c + 1], row["u"][NSTAGE % 2][0:1, 1, c * 128:(c + 1) * 128], ones[:],
                                        start=True, stop=True)
            last.then_inc(s_t, 1)
            pe.wait_ge(s_add["d"], NSTAGE)
            for c in range(4):
                last = nc.tensor.transpose(p2[:, c * 128:(c + 1) * 128], row["d"][NSTAGE % 2][:, 0, c * 128:(c + 1) * 128], ident[:])
            last.then_inc(s_t, 1)

        @block.scalar
        def _(act):
            act.wait_ge(s_t, 2)
            nc.scalar.copy(w2[:], p2[:].rearrange("p (c d) -> p c d", c=4)).then_inc(s_b2, 1)


def butterfly_ffn(nc, sem, n, x_all, ident, A, ahead):
    G = 4
    C = HID // 128
    with ExitStack() as ctx:
        def sb(name, shape, dt=F32):
            return ctx.enter_context(nc.sbuf_tensor(name, shape, dt))

        def bank(name):
            return ctx.enter_context(nc.psum_tensor(name, [128, 512], F32))

        w1, b1 = sb("f_w1", [D, HID]), sb("f_b1", [128, C])
        w2, b2 = sb("f_w2", [128, C, D]), sb("f_b2", [128, D])
        butterfly_weights(nc, sem, ident, A, w1, b1, w2, b2)

        xs = [sb(f"f_xs{k}", [S, G, D]) for k in range(2)]
        xT = [sb(f"f_xT{k}", [D, G * S]) for k in range(2)]
        g = [sb(f"f_g{k}", [128, C, G * S]) for k in range(2)]
        y, y2 = ([sb(f"f_{m}{k}", [S, G, D]) for k in range(2)] for m in ("y", "z"))
        norm = norm_parts(sb, sem, "f", G)
        pX, pY = bank("f_pX"), bank("f_pY")
        pH = [bank(f"f_pH{k}") for k in range(2)]
        s_x = [sem(f"f_loaded{k}") for k in range(2)]
        s_xp, s_xT, s_h, s_g, s_yp, s_y, s_y2 = (sem(f"f_{k}") for k in (
            "xT_in_psum", "xT_ready", "hidden", "gelu", "out_in_psum", "y_ready", "y2_ready"))
        s_ahead = sem("f_ahead")
        block = ctx.enter_context(nc.Block())
        m = n // G

        @block.sync
        def _(sp):
            def body(i, u, on):
                par = u % 2
                if awaited(i - 1):
                    sp.wait_ge(s_xp, i - 1)
                sp.dma_start(xs[par][:], x_all[:, bass.ds(i * G, G), :]).then_inc(s_x[par], 16)
            rounds(sp, m, 0, body)
            load_ahead(sp, s_ahead, ahead)

        @block.tensor
        def _(pe):
            def body(i, u, on):
                par = u % 2
                q = 1 - par
                if on(0):
                    pe.wait_ge(s_x[par], landed(i, par))
                    if awaited(i):
                        pe.wait_ge(s_xT, i)
                    for k in range(G):
                        last = nc.tensor.transpose(pX[:, k * S:(k + 1) * S], xs[par][:, k, :], ident[:])
                    last.then_inc(s_xp, 1)
                if on(1):
                    t = i - 1
                    pe.wait_ge(s_xT, t + 1)
                    for c in range(C):
                        if awaited(C * t + c - 1):
                            pe.wait_ge(s_g, C * t + c - 1)
                        nc.tensor.matmul(pH[c % 2][:], w1[:, c * 128:(c + 1) * 128], xT[q][:], start=True, stop=True).then_inc(s_h, 1)
                if on(2):
                    t = i - 2
                    if awaited(C * (t + 1)):
                        pe.wait_ge(s_g, C * (t + 1))
                    if awaited(t):
                        pe.wait_ge(s_y, t)
                    for k in range(G):
                        for c in range(C):
                            last = nc.tensor.matmul(pY[:, k * D:(k + 1) * D], g[par][:, c, k * S:(k + 1) * S], w2[:, c, :],
                                                    start=(c == 0), stop=(c == C - 1))
                    last.then_inc(s_yp, 1)
            rounds(pe, m, 2, body)

        @block.scalar
        def _(act):
            def body(i, u, on):
                par = u % 2
                q = 1 - par
                if on(0):
                    act.wait_ge(s_xp, i + 1)
                    if awaited(C * (i - 1)):
                        act.wait_ge(s_h, C * (i - 1))
                    nc.scalar.copy(xT[par][:], pX[:]).then_inc(s_xT, 1)
                if on(1):
                    t = i - 1
                    if awaited(t - 1):
                        act.wait_ge(s_yp, t - 1)
                    for c in range(C):
                        act.wait_ge(s_h, C * t + c + 1)
                        nc.scalar.activation(g[q][:, c, :], pH[c % 2][:], ACT.Gelu, bias=b1[:, c:c + 1]).then_inc(s_g, 1)
            rounds(act, m, 1, body)

        @block.vector
        def _(dve):
            def body(i, u, on):
                par = u % 2
                q = 1 - par
                if on(3):
                    t = i - 3
                    norm_apply(nc, dve, norm, t, q, x_all[:, bass.ds(t * G, G), :], y2[q][:])
                if on(2):
                    t = i - 2
                    dve.wait_ge(s_yp, t + 1)
                    if awaited(t - 1):
                        dve.wait_ge(s_y2, t - 1)
                    nc.vector.tensor_tensor(y[par][:], pY[:].rearrange("p (g d) -> p g d", g=G), x_all[:, bass.ds(t * G, G), :],
                                            ALU.add).then_inc(s_y, 1)
                    dve.wait_ge(s_y, t + 1)
                    if awaited(G * (t - 1)):
                        dve.wait_ge(norm["normed"], G * (t - 1))
                    nc.vector.tensor_tensor(y2[par][:], y[par][:], spread(b2[:], G, 1), ALU.add).then_inc(s_y2, 1)
                    dve.wait_ge(s_y2, t + 1)
                    norm_measure(nc, dve, norm, t, par, y2[par][:])
            rounds(dve, m, 3, body)

        @block.gpsimd
        def _(pool):
            norm_start(nc, pool, norm)

            def body(i, u, on):
                if on(2):
                    norm_root(nc, pool, norm, i - 2, u % 2)
            rounds(pool, m, 2, body)


def attentions_1_weights(sb, A):
    wqk = sb("s_wqk", [DQ, 2, H, D])
    wv = sb("s_wv", [D, H * DQ])
    wo = sb("s_wo", [128, 8, D])
    hide = sb("s_hide", [S, S])
    wt, wf = sb("t_ws", [D, D]), sb("t_w", [D, D])
    wcol = sb("t_wcol", [D, 2, 1])
    wcol_w = sb("t_wv", [D, 1])
    b = sb("t_b", [D, 1])
    bc = sb("t_bc", [S, 2])
    return (wqk, wv, wo, hide, wt, wf, wcol, wcol_w, b, bc), (
        (wqk[:, 0, :, :], A["L1_attn_w_q"].rearrange("h d c -> d h c")),
        (wqk[:, 1, :, :], A["L1_attn_w_k"].rearrange("h d c -> d h c")),
        (wv[:], A["s_wvT"]), (wo[:], A["L1_attn_w_o"].rearrange("(m p) d -> p m d", p=128)), (hide[:], A["hide"]),
        (wt[:], A["L1_xattn_Ws"]), (wf[:], A["L1_xattn_W"]), (wcol_w[:], A["L1_xattn_w"]),
        (b[:], A["L1_xattn_b"].rearrange("o d -> d o")),
        (wcol[:, 0, :], A["L1_xattn_Wcw"].rearrange("o d -> d o")),
        (wcol[:, 1, :], A["L1_xattn_Wcb"].rearrange("o d -> d o")),
        (bc[:, 0:1], A["L1_xattn_bcw"].unsqueeze(0).broadcast_to([S, 1])),
        (bc[:, 1:2], A["L1_xattn_bcb"].unsqueeze(0).broadcast_to([S, 1])))


def attentions_1(nc, sem, n, x_all, ident, A, weights, ahead):
    HQ = 4
    SCALE = float(DQ) ** -0.5
    BEHIND = 4
    TC = 16
    CH = [(t, min(TC, T2 - t)) for t in range(0, T2, TC)]
    NCH = len(CH)
    ON_POOL = (1, 2, 4)
    NB = T2P // 4
    R = NB // 4
    PEEL_1 = 12
    with ExitStack() as ctx:
        def sb(name, shape, dt=F32):
            return ctx.enter_context(nc.sbuf_tensor(name, shape, dt))

        def pair(name, shape, dt=F32):
            return [sb(f"{name}{k}", shape, dt) for k in range(2)]

        def bank(name):
            return ctx.enter_context(nc.psum_tensor(name, [128, 512], F32))

        wqk, wv, wo, hide, wt, wf, wcol, wcol_w, b, bc = weights
        wa = sb("s_wa", [D, H, D])
        hide_b, ident_b = sb("s_hide_b", [S, S], BF16), sb("s_ident_b", [128, 128], BF16)
        xs, xT, tT = pair("s_xs", [S, D]), pair("s_xT", [D, S]), pair("s_tT", [D, HQ * S])
        v = pair("s_v", [S, H * DQ])
        nm = pair("s_nm", [S, HQ])
        den, rden = ([sb(f"s_{m}{k}", [S, HQ]) for k in range(4)] for m in ("den", "rden"))
        p = [sb(f"s_p{k}", [S, HQ * S]) for k in range(4)]
        pn, pT = pair("s_pn", [S, HQ * S]), pair("s_pT", [S, HQ * S])
        yT, y = pair("s_yT", [128, 8, S]), pair("s_y", [S, 1, D])
        norm = norm_parts(sb, sem, "s")
        pM = bank("s_pM")
        pX, pO, pC = pM[:, 0:S], pM[:, 128:128 + D], pM[:, 256:256 + T2P]
        pT_, pY, pP = (bank(f"s_p{k}_") for k in "TYP")
        pS = [bank(f"s_pS{k}") for k in range(2)]

        s_ahead = sem("s_ahead")
        s_b, s_ab, s_wa = sem("s_casts"), sem("s_wa_in_psum"), sem("s_wa_ready")
        s_x = [sem(f"s_loaded{k}") for k in range(2)]
        s_xp, s_xT = sem("s_xT_in_psum"), sem("s_xT_ready")
        s_tq, s_tT = sem("s_t_in_psum"), sem("s_t_ready")
        s_vp, s_v = sem("s_v_in_psum"), sem("s_v_ready")
        s_s, s_nm, s_ex, s_rd, s_pn, s_tp, s_mix = (sem(f"s_{k}") for k in (
            "scores", "negmax", "exp", "rden", "probs", "probsT_in_psum", "mixed"))
        s_pT = [sem(f"s_probsT{k}") for k in range(2)]
        s_yT, s_op, s_y = sem("s_yT_ready"), sem("s_out_in_psum"), sem("s_y_ready")

        wc = sb("t_wc", [D, 2, D])
        wz = sb("t_wz", [D, 63])
        rows, cs, qm = pair("t_xs", [S, D]), pair("t_cs", [T2, D]), pair("t_qm", [S, T2P], I32)
        rowsT, cT = pair("t_xT", [D, S]), pair("t_cT", [D, 128])
        feat, txt = pair("t_feat", [D, S]), pair("t_txt", [D, T2P])
        cw, mk = ([sb(f"t_{m}{k}", [S, *w]) for k in range(4)] for m, w in (("cw", (2, 128)), ("mk", (T2P,))))
        args = [sb(f"t_args{k}", [D, TC, S]) for k in range(4)]
        th = [sb(f"t_th{k}", [D, TC, S]) for k in range(3)]
        rho_s = sb("t_rho_s", [128, 4, S])
        rho, m1 = pair("t_rho", [S, T2P]), pair("t_m1", [S, T2P])
        nmx, dens, rdens, acc, g = (pair(f"t_{k}", [S, w]) for k, w in (("nmx", 1), ("den", 1), ("rden", 1), ("acc", 2), ("g", 2)))
        ex, scr = pair("t_ex", [S, T2]), pair("t_scr", [S, 2, T2])
        z, z2 = pair("t_z", [S, 1, D]), pair("t_z2", [S, 1, D])
        norm_c = norm_parts(sb, sem, "t")
        pR = bank("t_pR")
        pN = bank("t_pN")

        c_set, c_zero = sem("t_set"), sem("t_zeroed")
        c_x = [sem(f"t_loaded{k}") for k in range(2)]
        c_xp, c_xT, c_cT, c_fg = (sem(f"t_{k}") for k in ("xcT_in_psum", "xT", "cT", "proj_in_psum"))
        c_feat, c_txt, c_cw = (sem(f"t_{k}_ready") for k in ("feat", "txt", "cw"))
        c_sumd, c_sump = sem("t_sums_vector"), sem("t_sums_gpsimd")
        c_th, c_red = sem("t_tanh"), sem("t_reduced")
        c_rs, c_rt, c_m1, c_mk, c_rho, c_mx, c_ex = (sem(f"t_{k}") for k in (
            "rho_copied", "rho_turned", "unmasked", "mask_ready", "rho_ready", "negmax", "exp"))
        c_rd, c_acc, c_g, c_z, c_z2 = (sem(f"t_{k}") for k in ("rden", "averaged", "gates", "z_ready", "z2_ready"))

        TH = (0, 1, 0, 1, 2)
        picked = ident[:].rearrange("p (j r) -> p j r", j=4)[:, :, 0:R]

        def back(c, k):
            return (1, c - k) if c >= k else (2, c - k + 4)

        BUFFER = {0: (0, 5), 3: (1, 5), 1: (2, 2), 2: (3, 5), 4: (2, 3)}

        def sums_ready(eng, t, k):
            if k in ON_POOL:
                eng.wait_ge(c_sump, 3 * t + ON_POOL.index(k) + 1)
            else:
                eng.wait_ge(c_sumd, 2 * t + k // 3 + 1)

        def buffer_free(eng, t, k):
            if awaited(NCH * t + k - BUFFER[k][1] + 1):
                eng.wait_ge(c_th, NCH * t + k - BUFFER[k][1] + 1)

        block = ctx.enter_context(nc.Block())

        @block.sync
        def _(sp):
            def body(i, u, on):
                par = u % 2
                if on(0):
                    if awaited(i - 1):
                        sp.wait_ge(s_xp, i - 1)
                    sp.dma_start(xs[par][:], x_all[:, bass.ds(i, 1), :].rearrange("s b d -> s (b d)")).then_inc(s_x[par], 16)
                if on(BEHIND):
                    t = i - BEHIND
                    if not isinstance(t, int):
                        for value in (t - 1, t + 1):
                            sp.to_reg(value)
                    sp.wait_ge(norm["normed"], t + 1)
                    if awaited(t - 1):
                        sp.wait_ge(c_xp, t - 1)
                    if awaited(t - 1):
                        sp.wait_ge(c_m1, t - 1)
                    sp.dma_start(rows[par][:], x_all[:, bass.ds(t, 1), :].rearrange("s b d -> s (b d)")).then_inc(c_x[par], 16)
                    sp.dma_start(cs[par][:], A["ctx_1024"][bass.ds(t, 1), :, :].rearrange("b t d -> (b t) d")).then_inc(c_x[par], 16)
                    sp.dma_start(qm[par][:, 0:T2], A["mask_BxS2_ik0"][bass.ds(t, 1), :].broadcast_to([S, T2])).then_inc(c_x[par], 16)
            rounds(sp, n, BEHIND, body, PEEL_1)
            load_ahead(sp, s_ahead, ahead)

        @block.tensor
        def _(pe):
            for h in range(H):
                if h % 4 == 0 and h >= 8:
                    pe.wait_ge(s_wa, h // 4 - 1)
                last = nc.tensor.matmul(pS[h // 4 % 2][:, h % 4 * D:(h % 4 + 1) * D], wqk[:, 0, h, :], wqk[:, 1, h, :],
                                        start=True, stop=True)
                if h % 4 == 3:
                    last.then_inc(s_ab, 1)
            pe.wait_ge(s_wa, 4)
            pe.wait_ge(s_b, 2)
            pe.wait_ge(c_set, 5)

            def turn_queries(a, q, c):
                if c == 0:
                    pe.wait_ge(s_xT, a + 1)
                if c in (0, 3):
                    if awaited(4 * a + c):
                        pe.wait_ge(s_tT, 4 * a + c)
                else:
                    if awaited(2 * a + c):
                        pe.wait_ge(s_v, 2 * a + c)
                for j in range(HQ):
                    last = nc.tensor.matmul(pP[:, j * S:(j + 1) * S], wa[:, HQ * c + j, :], xT[q][:], start=True, stop=True)
                last.then_inc(s_tq, 1)

            def values(a, q, k):
                pe.wait_ge(s_tT, 4 * a + k + 1)
                nc.tensor.matmul(pP[:], xT[q][:], wv[:, k * 512:(k + 1) * 512], start=True, stop=True).then_inc(s_vp, 1)

            def scores(x, par, c):
                pe.wait_ge(s_tT, 4 * x + c + 1)
                if awaited(4 * x + c - 1):
                    pe.wait_ge(s_ex, 4 * x + c - 1)
                nc.tensor.matmul(pS[c % 2][:], ident_b[:], spread(hide_b[:], HQ, 1), start=True, stop=True)
                for j in range(HQ):
                    last = nc.tensor.matmul(pS[c % 2][:, j * S:(j + 1) * S], tT[c % 2][:, j * S:(j + 1) * S], xT[par][:],
                                            start=False, stop=True, skip_group_check=True)
                last.then_inc(s_s, 1)

            def turn_probs(x, c):
                pe.wait_ge(s_pn, 4 * x + c + 1)
                if awaited(2 * x + (c + 1) // 2):
                    pe.wait_ge(s_pT[1 - c % 2], 2 * x + (c + 1) // 2)
                for j in range(HQ):
                    last = nc.tensor.transpose(pT_[:, j * S:(j + 1) * S], pn[c % 2][:, j * S:(j + 1) * S], ident[:])
                last.then_inc(s_tp, 1)

            def mix(x, par, c):
                pe.wait_ge(s_pT[c % 2], 2 * x + c // 2 + 1)
                if c == 0:
                    pe.wait_ge(s_v, 2 * x + 2)
                if c % 2 == 0:
                    if awaited(2 * x + c // 2):
                        pe.wait_ge(s_yT, 2 * x + c // 2)
                for j in range(HQ):
                    r, m = 64 * (j % 2), (2 * c + j // 2) % 4
                    last = nc.tensor.matmul(pY[r:r + 64, m * S:(m + 1) * S], v[par][:, (HQ * c + j) * DQ:(HQ * c + j + 1) * DQ],
                                            pT[c % 2][:, j * S:(j + 1) * S], start=True, stop=True)
                last.then_inc(s_mix, 1)

            def reduce(t, q, k):
                pe.wait_ge(c_th, NCH * t + k + 1)
                if k == 0:
                    if awaited(t):
                        pe.wait_ge(c_rs, t)
                t0, nt = CH[k]
                for b0 in range(0, nt, 4):
                    blk = (t0 + b0) // 4
                    j, r = blk % 4, blk // 4
                    w = min(4, nt - b0)
                    last = nc.tensor.matmul(pR[32 * j:32 * j + 32, 0:w * S], wz[:, 31 - r:63 - r],
                                            th[TH[k]][:, b0:b0 + w, :].rearrange("p t f -> p (t f)"),
                                            start=(r == 0), stop=(r == R - 1), skip_group_check=True)
                last.then_inc(c_red, 1)

            def body(i, u, on):
                par = u % 2
                q = 1 - par
                for c in range(4):
                    if on(1):
                        turn_queries(i - 1, q, c)
                    lag, cc = back(c, 1)
                    if on(lag):
                        scores(i - lag, (par + lag) % 2, cc)
                    if c == 2 and on(BEHIND + 3):
                        t = i - BEHIND - 3
                        pe.wait_ge(c_rs, t + 1)
                        if on(4):
                            pe.wait_ge(s_y, t + 4)
                        if awaited(t):
                            pe.wait_ge(c_rho, t)
                        if on(0):
                            pe.wait_ge(s_xT, i + 1)
                        for k in range(4):
                            last = nc.tensor.matmul(pC[:, k * NB:(k + 1) * NB], rho_s[:, k, :], picked, start=True, stop=True)
                        last.then_inc(c_rt, 1)
                    if on(1) and c < 2:
                        values(i - 1, q, c)
                    if c == 1 and on(BEHIND + 1):
                        t = i - BEHIND - 1
                        pe.wait_ge(c_cT, t + 1)
                        nc.tensor.matmul(pN[:, 0:128], wf[:], rowsT[q][:], start=True, stop=True)
                        nc.tensor.matmul(pN[:, 128:256], wt[:], cT[q][:], start=True, stop=True)
                        for k in range(2):
                            last = nc.tensor.matmul(pN[:, 128 * (k + 2):128 * (k + 3)], wc[:, k, :], cT[q][:], start=True, stop=True)
                        last.then_inc(c_fg, 1)
                    lag, cc = back(c, 3)
                    if on(lag):
                        turn_probs(i - lag, cc)
                    if c == 2 and on(3):
                        t = i - 3
                        pe.wait_ge(s_yT, 2 * t + 2)
                        if on(0):
                            pe.wait_ge(s_xT, i + 1)
                        if awaited(t):
                            pe.wait_ge(s_y, t)
                        for m in range(8):
                            last = nc.tensor.matmul(pO, yT[q][:, m, :], wo[:, m, :], start=(m == 0), stop=(m == 7))
                        last.then_inc(s_op, 1)
                    if on(2):
                        mix(i - 2, par, c)
                    if c == 0 and on(BEHIND + 3):
                        reduce(i - BEHIND - 3, q, 3)
                        reduce(i - BEHIND - 3, q, 4)
                    if c >= 1 and on(BEHIND + 2):
                        reduce(i - BEHIND - 2, par, c - 1)
                    if c == 3 and on(BEHIND):
                        t = i - BEHIND
                        pe.wait_ge(c_x[par], landed(t, par) * 3)
                        if awaited(t):
                            pe.wait_ge(c_cw, t)
                        nc.tensor.transpose(pN[:, 0:S], rows[par][:], ident[:])
                        nc.tensor.transpose(pN[:, S:S + T2], cs[par][:], ident[0:T2, 0:T2]).then_inc(c_xp, 1)
                    if c == 0 and on(0):
                        pe.wait_ge(s_x[par], landed(i, par))
                        if awaited(i):
                            pe.wait_ge(s_xT, i)
                        if awaited(i - 3):
                            pe.wait_ge(s_y, i - 3)
                        if awaited(i - 7):
                            pe.wait_ge(c_rho, i - 7)
                        nc.tensor.transpose(pX, xs[par][:], ident[:]).then_inc(s_xp, 1)
            rounds(pe, n, BEHIND + 3, body, PEEL_1)

        @block.scalar
        def _(act):
            for k in range(4):
                act.wait_ge(s_ab, k + 1)
                nc.scalar.activation(wa[:, 4 * k:4 * k + 4, :], heads(pS[k % 2][:], 4), ACT.Copy, scale=SCALE).then_inc(s_wa, 1)
            act.wait_ge(c_set, 5)

            def exps(x, c):
                act.wait_ge(s_nm, 4 * x + c + 1)
                if awaited(4 * x + c - 3):
                    act.wait_ge(s_pn, 4 * x + c - 3)
                if awaited(4 * x + c - 3):
                    act.wait_ge(s_rd, 4 * x + c - 3)
                for j in range(HQ):
                    last = nc.scalar.activation(p[c][:, j * S:(j + 1) * S], pS[c % 2][:, j * S:(j + 1) * S], ACT.Exp,
                                                bias=nm[c % 2][:, j:j + 1], accum_out=den[c][:, j:j + 1])
                last.then_inc(s_ex, 1)

            def tanh(t, par, k):
                sums_ready(act, t, k)
                if awaited(NCH * t + k - (3, 3, 2, 2, 5)[k] + 1):
                    act.wait_ge(c_red, NCH * t + k - (3, 3, 2, 2, 5)[k] + 1)
                nt = CH[k][1]
                nc.scalar.activation(th[TH[k]][:, 0:nt, :], args[BUFFER[k][0]][:, 0:nt, :], ACT.Tanh).then_inc(c_th, 1)

            def body(i, u, on):
                par = u % 2
                q = 1 - par
                for c in range(4):
                    if c == 3 and on(BEHIND + 2):
                        tanh(i - BEHIND - 2, par, 3)
                    if c in (0, 2):
                        lag, half = (3, 1) if c == 0 else (2, 0)
                        if on(lag):
                            t = i - lag
                            act.wait_ge(s_mix, 4 * t + 2 * half + 2)
                            if awaited(t - 1):
                                act.wait_ge(s_op, t - 1)
                            nc.scalar.copy(yT[(u + lag) % 2][:, 4 * half:4 * half + 4, :], heads(pY[:], 4)).then_inc(s_yT, 1)
                    if on(1) and c < 2:
                        a = i - 1
                        act.wait_ge(s_vp, 2 * a + c + 1)
                        if awaited(4 * (a - 1)):
                            act.wait_ge(s_mix, 4 * (a - 1))
                        nc.scalar.copy(v[q][:, c * 512:(c + 1) * 512], pP[:]).then_inc(s_v, 1)
                    lag, cc = back(c, 3)
                    if on(lag) and cc % 2 == 1:
                        x = i - lag
                        act.wait_ge(s_tp, 4 * x + cc + 1)
                        if awaited(4 * x + cc - 1):
                            act.wait_ge(s_mix, 4 * x + cc - 1)
                        nc.scalar.copy(pT[1][:], pT_[:]).then_inc(s_pT[1], 1)
                    if c == 1 and on(0):
                        act.wait_ge(s_xp, i + 1)
                        if awaited(4 * (i - 1)):
                            act.wait_ge(s_s, 4 * (i - 1))
                        nc.scalar.copy(xT[par][:], pX).then_inc(s_xT, 1)
                    if c == 0 and on(BEHIND + 1):
                        t = i - BEHIND - 1
                        act.wait_ge(c_xp, t + 1)
                        if awaited(t - 1):
                            act.wait_ge(c_fg, t - 1)
                        nc.scalar.copy(rowsT[q][:], pN[:, 0:S]).then_inc(c_xT, 1)
                        nc.scalar.copy(cT[q][:, 0:T2], pN[:, S:S + T2]).then_inc(c_cT, 1)
                    lag, cc = back(c, 1)
                    if on(lag):
                        exps(i - lag, cc)
                    if c == 0 and on(BEHIND + 4):
                        t = i - BEHIND - 4
                        act.wait_ge(c_mx, t + 1)
                        if awaited(2 * (t - 1)):
                            act.wait_ge(c_acc, 2 * (t - 1))
                        if awaited(t - 1):
                            act.wait_ge(c_rd, t - 1)
                        nc.scalar.activation(ex[par][:], rho[par][:, 0:T2], ACT.Exp, bias=nmx[par][:],
                                             accum_out=dens[par][:]).then_inc(c_ex, 1)
                    if c == 2 and on(BEHIND + 1):
                        t = i - BEHIND - 1
                        act.wait_ge(c_fg, t + 1)
                        if awaited(3 * (t - 1)):
                            act.wait_ge(c_sump, 3 * (t - 1))
                        if awaited(2 * (t - 1)):
                            act.wait_ge(c_sumd, 2 * (t - 1))
                        nc.scalar.copy(feat[q][:], pN[:, 0:128]).then_inc(c_feat, 1)
                        nc.scalar.activation(txt[q][:], pN[:, 128:128 + T2P], ACT.Identity, bias=b[:]).then_inc(c_txt, 1)
                        if awaited(2 * (t - 3)):
                            act.wait_ge(c_acc, 2 * (t - 3))
                        nc.scalar.copy(cw[(u + 3) % 4][:], pN[:, 256:512].rearrange("p (k t) -> p k t", k=2)).then_inc(c_cw, 1)
                    if c == 2 and on(BEHIND + 4):
                        t = i - BEHIND - 4
                        act.wait_ge(c_acc, 2 * t + 2)
                        act.wait_ge(c_rd, t + 1)
                        if awaited(t - 1):
                            act.wait_ge(c_z, t - 1)
                        for k in range(2):
                            last = nc.scalar.activation(g[par][:, k:k + 1], acc[par][:, k:k + 1], ACT.Tanh, bias=bc[:, k:k + 1],
                                                        scale=rdens[par][:])
                        last.then_inc(c_g, 1)
                    if on(BEHIND + 2):
                        tanh(i - BEHIND - 2, par, c if c < 3 else 4)
            rounds(act, n, BEHIND + 4, body, PEEL_1)

        @block.vector
        def _(dve):
            nc.vector.tensor_copy(hide_b[:], hide[:]).then_inc(s_b, 1)
            nc.vector.tensor_copy(ident_b[:], ident[:]).then_inc(s_b, 1)
            for k in range(2):
                nc.vector.tensor_copy(wc[:, k, :], wcol[:, k, :].broadcast_to([D, D])).then_inc(c_set, 1)
            dve.wait_ge(c_set, 5)

            def sums(t, par, k):
                t0, nt = CH[k]
                dve.wait_ge(c_feat, t + 1)
                dve.wait_ge(c_txt, t + 1)
                buffer_free(dve, t, k)
                nc.vector.tensor_tensor(args[BUFFER[k][0]][:, 0:nt, :], spread(feat[par][:], nt, 1),
                                        spread(txt[par][:, t0:t0 + nt], S, 2), ALU.add).then_inc(c_sumd, 1)

            def body(i, u, on):
                par = u % 2
                q = 1 - par
                for c in range(4):
                    if on(1):
                        a = i - 1
                        dve.wait_ge(s_tq, 4 * a + c + 1)
                        if awaited(4 * a + c - 1):
                            dve.wait_ge(s_s, 4 * a + c - 1)
                        nc.vector.tensor_copy(tT[c % 2][:], pP[:]).then_inc(s_tT, 1)
                    if c == 1 and on(BEHIND + 3):
                        t = i - BEHIND - 3
                        if awaited(NCH * (t + 1)):
                            dve.wait_ge(c_red, NCH * (t + 1))
                        if awaited(t):
                            dve.wait_ge(c_rt, t)
                        nc.vector.tensor_copy(rho_s[:], heads(pR[:], 4)).then_inc(c_rs, 1)
                    lag, cc = back(c, 2)
                    if on(lag):
                        x = i - lag
                        dve.wait_ge(s_ex, 4 * x + cc + 1)
                        if awaited(4 * x + cc - 3):
                            dve.wait_ge(s_pn, 4 * x + cc - 3)
                        nc.vector.reciprocal(rden[cc][:], den[cc][:]).then_inc(s_rd, 1)
                    lag, cc = back(c, 1)
                    if on(lag):
                        x = i - lag
                        dve.wait_ge(s_s, 4 * x + cc + 1)
                        if awaited(4 * x + cc - 1):
                            dve.wait_ge(s_ex, 4 * x + cc - 1)
                        nc.vector.tensor_reduce(nm[cc % 2][:], heads(pS[cc % 2][:], HQ), AX, ALU.max, negate=True).then_inc(s_nm, 1)
                    lag, cc = back(c, 3)
                    if on(lag) and cc % 2 == 0:
                        x = i - lag
                        dve.wait_ge(s_tp, 4 * x + cc + 1)
                        if awaited(4 * x + cc - 1):
                            dve.wait_ge(s_mix, 4 * x + cc - 1)
                        nc.vector.tensor_copy(pT[0][:], pT_[:]).then_inc(s_pT[0], 1)
                    if c == 3 and on(3):
                        t = i - 3
                        dve.wait_ge(s_op, t + 1)
                        if awaited(t - 1):
                            dve.wait_ge(norm["normed"], t - 1)
                        nc.vector.tensor_tensor(y[q][:, 0, :], pO, x_all[:, bass.ds(t, 1), :].rearrange("s b d -> s (b d)"),
                                                ALU.add).then_inc(s_y, 1)
                        dve.wait_ge(s_y, t + 1)
                        norm_measure(nc, dve, norm, t, q, y[q][:])
                    if c == 1 and on(4):
                        norm_apply(nc, dve, norm, i - 4, par, x_all[:, bass.ds(i - 4, 1), :], y[par][:])
                    if c == 0 and on(BEHIND + 5):
                        t = i - BEHIND - 5
                        x = x_all[:, bass.ds(t, 1), :]
                        dve.wait_ge(c_g, t + 1)
                        if awaited(t - 1):
                            dve.wait_ge(c_z2, t - 1)
                        nc.vector.tensor_scalar(z[q][:], x, g[q][:, 0:1], g[q][:, 1:2], ALU.mult, ALU.add).then_inc(c_z, 1)
                        dve.wait_ge(c_z, t + 1)
                        if awaited(t - 1):
                            dve.wait_ge(norm_c["normed"], t - 1)
                        nc.vector.tensor_tensor(z2[q][:], z[q][:], x, ALU.add).then_inc(c_z2, 1)
                        dve.wait_ge(c_z2, t + 1)
                        norm_measure(nc, dve, norm_c, t, q, z2[q][:])
                    if c == 0 and on(BEHIND + 2):
                        sums(i - BEHIND - 2, par, 0)
                    if c == 1 and on(BEHIND + 4):
                        t = i - BEHIND - 4
                        dve.wait_ge(c_ex, t + 1)
                        if awaited(t - 1):
                            dve.wait_ge(c_g, t - 1)
                        nc.vector.reciprocal(rdens[par][:], dens[par][:]).then_inc(c_rd, 1)
                        for k in range(2):
                            nc.vector.tensor_tensor_reduce(scr[par][:, k, :], ex[par][:], cw[u][:, k, 0:T2], 1.0, 0.0, ALU.mult,
                                                           ALU.add, acc[par][:, k:k + 1]).then_inc(c_acc, 1)
                    if c == 2 and on(BEHIND + 1):
                        t = i - BEHIND - 1
                        dve.wait_ge(c_x[q], landed(t, q) * 3)
                        if awaited(t - 1):
                            dve.wait_ge(c_mk, t - 1)
                        nc.vector.tensor_scalar(m1[q][:, 0:T2], qm[q][:, 0:T2], -1.0, 1.0, ALU.mult, ALU.add).then_inc(c_m1, 1)
                        dve.wait_ge(c_m1, t + 1)
                        if awaited(t - 3):
                            dve.wait_ge(c_rho, t - 3)
                        nc.vector.tensor_scalar(mk[(u + 3) % 4][:, 0:T2], m1[q][:, 0:T2], HIDDEN, None, ALU.mult).then_inc(c_mk, 1)
                    if c == 2 and on(BEHIND + 5):
                        t = i - BEHIND - 5
                        norm_apply(nc, dve, norm_c, t, q, x_all[:, bass.ds(t, 1), :], z2[q][:])
                    if c == 3 and on(BEHIND + 3):
                        t = i - BEHIND - 3
                        dve.wait_ge(c_rt, t + 1)
                        dve.wait_ge(c_mk, t + 1)
                        if awaited(t - 1):
                            dve.wait_ge(c_ex, t - 1)
                        shape = "p (r j t) -> p r j t"
                        turned = pC.rearrange("p (t j r) -> p r j t", t=4, j=4)
                        nc.vector.tensor_tensor(rho[q][:].rearrange(shape, r=R, j=4), turned,
                                                mk[(u + 1) % 4][:].rearrange(shape, r=R, j=4), ALU.add).then_inc(c_rho, 1)
                        dve.wait_ge(c_rho, t + 1)
                        nc.vector.tensor_reduce(nmx[q][:], rho[q][:, 0:T2], AX, ALU.max, negate=True).then_inc(c_mx, 1)
                    if c == 2 and on(BEHIND + 2):
                        sums(i - BEHIND - 2, par, 3)
            rounds(dve, n, BEHIND + 5, body, PEEL_1)

        @block.gpsimd
        def _(pool):
            norm_start(nc, pool, norm)
            norm_start(nc, pool, norm_c)
            nc.gpsimd.memset(wz[:], 0.0).then_inc(c_zero, 1)
            nc.gpsimd.memset(cT[0][:], 0.0).then_inc(c_set, 1)
            nc.gpsimd.memset(cT[1][:], 0.0).then_inc(c_set, 1)
            for k in range(4):
                nc.gpsimd.memset(mk[k][:], 0.0).then_inc(c_zero, 1)
            pool.wait_ge(c_zero, 5)
            nc.gpsimd.tensor_copy(wz[:, 31:32], wcol_w[:]).then_inc(c_set, 1)

            def sums(t, par, k):
                t0, nt = CH[k]
                pool.wait_ge(c_feat, t + 1)
                pool.wait_ge(c_txt, t + 1)
                buffer_free(pool, t, k)
                nc.gpsimd.tensor_tensor(args[BUFFER[k][0]][:, 0:nt, :], spread(feat[par][:], nt, 1),
                                        spread(txt[par][:, t0:t0 + nt], S, 2), ALU.add).then_inc(c_sump, 1)

            def body(i, u, on):
                par = u % 2
                q = 1 - par
                for c in range(4):
                    lag, cc = back(c, 2)
                    if on(lag):
                        x = i - lag
                        pool.wait_ge(s_rd, 4 * x + cc + 1)
                        if awaited(4 * x + cc - 1):
                            pool.wait_ge(s_tp, 4 * x + cc - 1)
                        nc.gpsimd.tensor_tensor(heads(pn[cc % 2][:], HQ), heads(p[cc][:], HQ), spread(rden[cc][:], S, 2),
                                                ALU.mult).then_inc(s_pn, 1)
                    if c == 0 and on(4):
                        norm_root(nc, pool, norm, i - 4, par)
                    if c == 1 and on(BEHIND + 5):
                        norm_root(nc, pool, norm_c, i - BEHIND - 5, q)
                    if c < 3 and on(BEHIND + 2):
                        sums(i - BEHIND - 2, par, ON_POOL[c])
            rounds(pool, n, BEHIND + 5, body, PEEL_1)


def experts_1_weights(sb, A):
    wg, wu = sb("e_wg", [D, E, FE]), sb("e_wu", [D, E, FE])
    wr, br = sb("e_wr", [D, E]), sb("e_br", [S, E])
    number = sb("e_number", [S, E])
    return (wg, wu, wr, br, number), (
        (wr[:], A["L1_ffn_Ws"]), (br[:], A["L1_ffn_bs"].unsqueeze(0).broadcast_to([S, E])),
        (number[:], A["number"].unsqueeze(0).broadcast_to([S, E])),
        (wg[:], A["L1_ffn_Wg"].rearrange("e d f -> d e f")), (wu[:], A["L1_ffn_Wu"].rearrange("e d f -> d e f")))


def experts_ffn_1(nc, sem, n, x_all, ident, A, out, weights):
    G = 4
    CH = [(c, min(128, FE - c)) for c in range(0, FE, 128)]
    NC = len(CH)
    with ExitStack() as ctx:
        def sb(name, shape, dt=F32):
            return ctx.enter_context(nc.sbuf_tensor(name, shape, dt))

        def pair(name, shape, dt=F32):
            return [sb(f"{name}{k}", shape, dt) for k in range(2)]

        def bank(name):
            return ctx.enter_context(nc.psum_tensor(name, [128, 512], F32))

        wg, wu, wr, br, number = weights
        wd = sb("e_wd", [128, E, NC, D])
        xs, xT = pair("e_xs", [S, G, D]), pair("e_xT", [D, G * S])
        logit, top, topi, topf = (pair(f"e_{k}", [S, G, 8], dt) for k, dt in (("logit", F32), ("top", F32), ("topi", U32), ("topf", F32)))
        gap, tg = pair("e_gap", [S, G]), pair("e_tg", [S, G])
        pw = pair("e_pw", [S, 2, G])
        c1, c2, w1, w2, cb = (pair(f"e_{k}", [S, G, E]) for k in ("c1", "c2", "w1", "w2", "cb"))
        sg, h = [sb(f"e_sg{k}", [128, G * S]) for k in range(2)], [sb(f"e_h{k}", [128, G * S]) for k in range(6)]
        acc = pair("e_acc", [S, G, D])
        res = pair("e_res", [S, G, D])
        norm = norm_parts(sb, sem, "e", G)
        pX = bank("e_pX")
        pY = bank("e_pY")
        pG = [bank(f"e_pG{k}") for k in range(3)]
        pU = [bank(f"e_pU{k}") for k in range(3)]

        s_w = sem("e_weights")
        s_x = [sem(f"e_loaded{k}") for k in range(2)]
        s_xp, s_xT, s_lp, s_lg, s_top, s_topi, s_topf, s_gap, s_tg, s_pw, s_c1, s_c2, s_cb = (sem(f"e_{k}") for k in (
            "xT_in_psum", "xT_ready", "logits_in_psum", "logits", "top", "top_number", "top_number_f", "gap", "tanh_gap",
            "pair_weights", "first", "second", "combine"))
        s_eq = sem("e_chosen")
        s_gp, s_up, s_sg, s_h = (sem(f"e_{k}") for k in ("gate_in_psum", "up_in_psum", "silu", "hidden"))
        s_yp, s_acc = sem("e_expert_in_psum"), sem("e_added")
        s_st = [sem(f"e_stored{k}") for k in range(2)]
        block = ctx.enter_context(nc.Block())
        m = n // G
        NCE = NC * E

        @block.sync
        def _(sp):
            def body(i, u, on):
                par = u % 2
                if on(0):
                    if awaited(i - 1):
                        sp.wait_ge(s_xp, i - 1)
                    sp.dma_start(xs[par][:], x_all[:, bass.ds(i * G, G), :]).then_inc(s_x[par], 16)
                if on(2):
                    t = i - 2
                    if awaited(G * (t + 1)):
                        sp.wait_ge(norm["normed"], G * (t + 1))
                    sp.dma_start(out[bass.ds(t * G, G), :, :].rearrange("b s d -> s b d"), res[par][:]).then_inc(s_st[par], 16)
            rounds(sp, m, 2, body)
            for k in range(2):
                sp.wait_ge(s_st[k], 16 * (m // 2))

        @block.tensor
        def _(pe):
            def body(i, u, on):
                par = u % 2
                q = 1 - par

                def down(t, e):
                    if e == 0 and isinstance(t, int):
                        pe.wait_ge(s_w, 16 * NC)
                    if awaited(NCE * t + NC * (e + 1)):
                        pe.wait_ge(s_h, NCE * t + NC * (e + 1))
                    if awaited(G * (E * t + e)):
                        pe.wait_ge(s_acc, G * (E * t + e))
                    for k in range(G):
                        for c, (f0, nf) in enumerate(CH):
                            last = nc.tensor.matmul(pY[:, k * D:(k + 1) * D], h[(NC * e + c) % 6][0:nf, k * S:(k + 1) * S],
                                                    wd[0:nf, e, c, :], start=(c == 0), stop=(c == NC - 1))
                    last.then_inc(s_yp, 1)

                def front(k):
                    if k == 0:
                        pe.wait_ge(s_x[par], landed(i, par))
                        if awaited(i):
                            pe.wait_ge(s_lg, i)
                        for j in range(G):
                            last = nc.tensor.transpose(pX[:, j * S:(j + 1) * S], xs[par][:, j, :], ident[:])
                        last.then_inc(s_xp, 1)
                    else:
                        pe.wait_ge(s_xT, i + 1)
                        for j in range(G):
                            last = nc.tensor.matmul(pX[:, j * E:(j + 1) * E], xT[par][:, j * S:(j + 1) * S], wr[:], start=True, stop=True)
                        last.then_inc(s_lp, 1)

                for e in range(E):
                    if on(1):
                        t = i - 1
                        if e == 0:
                            pe.wait_ge(s_xT, t + 1)
                        for c, (f0, nf) in enumerate(CH):
                            k = NC * e + c
                            if awaited(NCE * t + k - 2):
                                pe.wait_ge(s_sg, NCE * t + k - 2)
                            nc.tensor.matmul(pG[c][0:nf, :], wg[:, e, f0:f0 + nf], xT[q][:], start=True, stop=True).then_inc(s_gp, 1)
                            if awaited(NCE * t + k - 2):
                                pe.wait_ge(s_h, NCE * t + k - 2)
                            nc.tensor.matmul(pU[c][0:nf, :], wu[:, e, f0:f0 + nf], xT[q][:], start=True, stop=True).then_inc(s_up, 1)
                        if e >= 1:
                            down(t, e - 1)
                    if on(0) and e in (2, 4):
                        front(e // 2 - 1)
                if on(1):
                    down(i - 1, E - 1)
            rounds(pe, m, 1, body)

        @block.scalar
        def _(act):
            for c, (f0, nf) in enumerate(CH):
                act.dma_start(wd[0:nf, :, c, :], A["L1_ffn_Wd"][:, f0:f0 + nf, :].rearrange("e f d -> f e d")).then_inc(s_w, 16)

            def body(i, u, on):
                par = u % 2
                for e in range(E):
                    if on(1):
                        t = i - 1
                        for c, (f0, nf) in enumerate(CH):
                            k = NC * e + c
                            act.wait_ge(s_gp, NCE * t + k + 1)
                            if awaited(NCE * t + k - 1):
                                act.wait_ge(s_h, NCE * t + k - 1)
                            nc.scalar.activation(sg[k % 2][0:nf, :], pG[c][0:nf, :], ACT.Silu).then_inc(s_sg, 1)
                    if on(0) and e == 2:
                        act.wait_ge(s_xp, i + 1)
                        if awaited(NCE * (i - 1)):
                            act.wait_ge(s_up, NCE * (i - 1))
                        if awaited(i - 1):
                            act.wait_ge(s_lp, i - 1)
                        nc.scalar.copy(xT[par][:], pX[:]).then_inc(s_xT, 1)
                    if on(0) and e == 6:
                        act.wait_ge(s_gap, i + 1)
                        if awaited(2 * (i - 1)):
                            act.wait_ge(s_pw, 2 * (i - 1))
                        nc.scalar.activation(tg[par][:], gap[par][:], ACT.Tanh, scale=0.5).then_inc(s_tg, 1)
            rounds(act, m, 1, body)

        @block.vector
        def _(dve):

            def combine(i, par, k):
                if k == 0:
                    dve.wait_ge(s_lp, i + 1)
                    if awaited(G * (i - 1)):
                        dve.wait_ge(s_topi, G * (i - 1))
                    nc.vector.tensor_tensor(logit[par][:], pX[:, 0:G * E].rearrange("p (g e) -> p g e", g=G), spread(br[:], G, 1),
                                            ALU.add).then_inc(s_lg, 1)
                    in_registers(dve, i + 1, i - 1)
                    dve.wait_ge(s_w, 16 * NC)
                    dve.wait_ge(s_lg, i + 1)
                    if awaited(i - 1):
                        dve.wait_ge(s_gap, i - 1)
                    for j in range(G):
                        nc.vector.max(top[par][:, j, :], logit[par][:, j, :]).then_inc(s_top, 1)
                    in_registers(dve, G * (i + 1), i - 1)
                    dve.wait_ge(s_w, 16 * NC)
                    if awaited(G * (i + 1)):
                        dve.wait_ge(s_top, G * (i + 1))
                    if awaited(i - 1):
                        dve.wait_ge(s_topf, i - 1)
                    for j in range(G):
                        nc.vector.max_index(topi[par][:, j, :], top[par][:, j, :], logit[par][:, j, :]).then_inc(s_topi, 1)
                    if awaited(i - 1):
                        dve.wait_ge(s_tg, i - 1)
                    nc.vector.tensor_tensor(gap[par][:], top[par][:, :, 0], top[par][:, :, 1], ALU.subtract).then_inc(s_gap, 1)
                    if awaited(G * (i + 1)):
                        dve.wait_ge(s_topi, G * (i + 1))
                    if awaited(i - 1):
                        dve.wait_ge(s_c2, i - 1)
                    nc.vector.tensor_copy(topf[par][:], topi[par][:]).then_inc(s_topf, 1)
                else:
                    dve.wait_ge(s_tg, i + 1)
                    if awaited(i - 1):
                        dve.wait_ge(s_c2, i - 1)
                    nc.vector.tensor_scalar(pw[par][:, 0, :], tg[par][:], 0.5, 0.5, ALU.mult, ALU.add).then_inc(s_pw, 1)
                    nc.vector.tensor_scalar(pw[par][:, 1, :], tg[par][:], -0.5, 0.5, ALU.mult, ALU.add).then_inc(s_pw, 1)
                    dve.wait_ge(s_topf, i + 1)
                    if awaited(i - 1):
                        dve.wait_ge(s_cb, i - 1)
                    nc.vector.tensor_tensor(c1[par][:], spread(number[:], G, 1), topf[par][:, :, 0:1].broadcast_to([S, G, E]),
                                            ALU.is_equal).then_inc(s_eq, 1)
                    nc.vector.tensor_tensor(c2[par][:], spread(number[:], G, 1), topf[par][:, :, 1:2].broadcast_to([S, G, E]),
                                            ALU.is_equal).then_inc(s_eq, 1)
                    if awaited(2 * (i + 1)):
                        dve.wait_ge(s_eq, 2 * (i + 1))
                    if awaited(2 * (i + 1)):
                        dve.wait_ge(s_pw, 2 * (i + 1))
                    nc.vector.tensor_tensor(w1[par][:], c1[par][:], spread(pw[par][:, 0, :], E, 2), ALU.mult).then_inc(s_c1, 1)
                    nc.vector.tensor_tensor(w2[par][:], c2[par][:], spread(pw[par][:, 1, :], E, 2), ALU.mult).then_inc(s_c2, 1)
                    dve.wait_ge(s_c1, i + 1)
                    dve.wait_ge(s_c2, i + 1)
                    if awaited(G * E * (i - 1)):
                        dve.wait_ge(s_acc, G * E * (i - 1))
                    nc.vector.tensor_tensor(cb[par][:], w1[par][:], w2[par][:], ALU.add).then_inc(s_cb, 1)

            def body(i, u, on):
                par = u % 2
                q = 1 - par

                def add(t, e):
                    dve.wait_ge(s_yp, E * t + e + 1)
                    if e == 0:
                        dve.wait_ge(s_cb, t + 1)
                        if awaited(G * (t - 1)):
                            dve.wait_ge(norm["normed"], G * (t - 1))
                    else:
                        if awaited(G * (E * t + e)):
                            dve.wait_ge(s_acc, G * (E * t + e))
                    for k in range(G):
                        before = x_all[:, bass.ds(t * G + k, 1), :].rearrange("s b d -> s (b d)") if e == 0 else acc[q][:, k, :]
                        nc.vector.scalar_tensor_tensor(acc[q][:, k, :], pY[:, k * D:(k + 1) * D], cb[q][:, k, e:e + 1], before,
                                                       ALU.mult, ALU.add).then_inc(s_acc, 1)

                for e in range(E):
                    if on(1):
                        t = i - 1
                        for c, (f0, nf) in enumerate(CH):
                            k = NC * e + c
                            dve.wait_ge(s_sg, NCE * t + k + 1)
                            dve.wait_ge(s_up, NCE * t + k + 1)
                            if awaited(E * t + e - 1):
                                dve.wait_ge(s_yp, E * t + e - 1)
                            nc.vector.tensor_tensor(h[k % 6][0:nf, :], sg[k % 2][0:nf, :], pU[c][0:nf, :], ALU.mult).then_inc(s_h, 1)
                        if e >= 1:
                            add(t, e - 1)
                    if on(2) and e == 0:
                        t = i - 2
                        if awaited(8 * t - 8 * par):
                            dve.wait_ge(s_st[par], 8 * t - 8 * par)
                        norm_apply(nc, dve, norm, t, par, res[par][:], acc[par][:])
                    if on(0) and e == 5:
                        combine(i, par, 0)
                    if on(0) and e == 7:
                        combine(i, par, 1)
                if on(1):
                    add(i - 1, E - 1)
                    if awaited(G * E * i):
                        dve.wait_ge(s_acc, G * E * i)
                    norm_measure(nc, dve, norm, i - 1, q, acc[q][:])
            rounds(dve, m, 2, body)

        @block.gpsimd
        def _(pool):
            norm_start(nc, pool, norm)

            def body(i, u, on):
                if on(1):
                    norm_root(nc, pool, norm, i - 1, 1 - u % 2)
            rounds(pool, m, 1, body)


def decoder_kernel(nc, A, out):
    n = A["x"].shape[0]
    with ExitStack() as ctx:
        x_all = ctx.enter_context(nc.sbuf_tensor("x_all", [S, n, D], F32))
        ident = ctx.enter_context(nc.sbuf_tensor("ident", [128, 128], F32))

        def sb(name, shape):
            return ctx.enter_context(nc.sbuf_tensor(name, shape, F32))

        cross_0, cross_0_loads = cross_0_weights(sb, A)
        attentions, attentions_loads = attentions_1_weights(sb, A)
        experts, experts_loads = experts_1_weights(sb, A)
        for sublayer, more in ((self_attention_0, (cross_0_loads,)), (cross_attention_0, (cross_0,)),
                               (butterfly_ffn, (attentions_loads,)), (attentions_1, (attentions, experts_loads)),
                               (experts_ffn_1, (out, experts))):
            with nc.cleanup_on_exit():
                sublayer(nc, nc.alloc_semaphore, n, x_all, ident, A, *more)


def shape_tables():
    import numpy as np

    c = {"ident": np.eye(128, dtype=np.float32), "number": np.arange(E, dtype=np.float32)}
    q, r = np.arange(S), np.arange(128)
    c["above"] = (q[None, :] > q[:, None] + 1).astype(np.uint32)
    c["beside"] = (q[None, :] == q[:, None] + 1).astype(np.uint32)
    c["hide"] = np.where(q[None, :] > q[:, None], np.float32(HIDDEN), np.float32(0))
    c["a_hmask"] = (((r // DK) % 8)[:, None] == np.arange(8)[None]).astype(np.float32)
    c["a_hsum"] = ((r // DK)[:, None] == np.arange(H)[None]).astype(np.float32)
    freq = 1.0 / 10000.0 ** (np.arange(0, DK, 2) / DK)
    turn, rpos = np.zeros((128, 8, S)), np.zeros((128, H, S))
    for g in range(2):
        base, rel = (slice(0, 64), 64) if g == 0 else (slice(64, 128), 0)
        turn[base, 2 * g] = 1.0
        for h in range(8):
            for d in range(DK):
                row, w = rel + h * DK + d, freq[d % 4]
                for at, angle in ((0, q * w), (4, (S + 1 + q) * w)):
                    turn[row, at + 2 * g] = -np.cos(angle) if d < 4 else np.cos(angle)
                    turn[row, at + 2 * g + 1] = np.sin(angle)
                rpos[row, 8 * g + h] = np.sin(q * w) if d < 4 else np.cos(q * w)
    c["a_turn"] = (turn * DK ** -0.5).astype(np.float32)
    c["a_rpos"] = rpos.reshape(128, H * S).astype(np.float32)
    return c


def laid_out(inputs):
    import numpy as np

    A = {k: np.asarray(v) for k, v in inputs.items() if k != "mask_BxS_ff1"}
    swap = np.arange(D).reshape(H, 2, DK // 2)[:, ::-1].reshape(-1)
    lo, hi = slice(0, 64), slice(64, 128)
    Wq, Wk = A["L0_attn_Wq"], A["L0_attn_Wk"]
    Ws = Wq[:, swap]
    A["a_wq"] = np.stack([np.concatenate(p, 1) for p in (
        (Wq[:, lo], Wq[:, lo]), (Wq[:, lo], Ws[:, lo]), (Wq[:, hi], Wq[:, hi]), (Ws[:, hi], Wq[:, hi]))] + [Wk], 1)
    u, v = A["L0_attn_u"].reshape(-1), A["L0_attn_v"].reshape(-1)
    vs = v[swap]
    A["a_ub"] = np.stack([np.concatenate(p) for p in ((u[lo], v[lo]), (v[lo], vs[lo]), (v[hi], u[hi]), (vs[hi], v[hi]))], 1)
    for new, old in (("q", "q"), ("k", "k"), ("v", "v"), ("o", "o")):
        A[f"c_w{new}T"] = A[f"L0_xattn_W{old}"].T
    A["f_wconT"] = A["L0_ffn_W_con"].T
    A["f_upb"] = A["L0_ffn_up_bias"].reshape(HID // 128, 128).T
    A["s_wvT"] = A["L1_attn_w_v"].reshape(H * DQ, D).T
    for k in ("L0_attn_Wq", "L0_attn_Wk", "L0_attn_u", "L0_attn_v", "L0_xattn_Wq", "L0_xattn_Wk", "L0_xattn_Wv", "L0_xattn_Wo",
              "L0_ffn_W_con", "L0_ffn_up_bias", "L1_attn_w_v"):
        del A[k]
    return A


def kernel(**inputs):
    import numpy as np
    import concourse.bacc as bacc
    from concourse.bass_utils import run_bass_kernel_spmd

    nc = bacc.Bacc("TRN2", target_bir_lowering=False, num_devices=1)
    arrays = {f"in_{k}": np.ascontiguousarray(v) for k, v in {**laid_out(inputs), **shape_tables()}.items()}
    A = {k[3:]: nc.dram_tensor(k, a.shape, mybir.dt.from_np(a.dtype), kind="ExternalInput").ap() for k, a in arrays.items()}
    shape = inputs["x"].shape
    out = nc.dram_tensor("out_x", shape, F32, kind="ExternalOutput").ap()
    decoder_kernel(nc, A, out)
    r = run_bass_kernel_spmd(nc, [arrays], core_ids=[0])
    return r.results[0]["out_x"]
```
